# Optimizing a Trainium2 kernel written in Bass

```python
import numpy as np
import jax
import jax.numpy as jnp

def _softmax(x, axis=-1):
    return jax.nn.softmax(x, axis=axis)

def _gelu(x):
    return jax.nn.gelu(x, approximate=True)

def _silu(x):
    return jax.nn.silu(x)

def _sigmoid(x):
    return jax.nn.sigmoid(x)

def _layernorm(x, axis=-1, eps=1e-05):
    m = jnp.mean(x, axis=axis, keepdims=True)
    v = jnp.var(x, axis=axis, keepdims=True)
    return (x - m) / jnp.sqrt(v + eps)

def _scatter_add(tgt, idx, src, axis=0):
    return tgt.at[idx].add(src)

def _segment_sum(src, seg, n):
    return jax.ops.segment_sum(src, seg, n)
kernel_name = 'mk_decoder_preln_d2_seqx_r4_a94183'

def setup_inputs(seed: int=0):
    np.random.seed(seed)
    _w = jnp.asarray

    def _rec_inputs():
        import jax
        import jax.numpy as jnp
        _rk = jax.random.key(seed)
        x = -0.0002928 + 1 * jax.random.normal(jax.random.fold_in(_rk, 1), (2, 1024, 256), jnp.float32)
        _lenS = 1024 - jax.random.randint(jax.random.fold_in(_rk, 7), (2,), 0, max(1, 1024 // 4) + 1, jnp.int32)
        _lenS2 = 77 - jax.random.randint(jax.random.fold_in(_rk, 8), (2,), 0, max(1, 77 // 4) + 1, jnp.int32)
        _ctx_1024P = jax.random.normal(jax.random.fold_in(_rk, 11), (2, 16, 256), jnp.float32)
        _ctx_1024c = jax.random.dirichlet(jax.random.fold_in(_rk, 511), 0.3 * jnp.ones((16,), jnp.float32), (2, 77))
        _ctx_1024t = jnp.einsum('bsk,bkd->bsd', _ctx_1024c, _ctx_1024P)
        _ctx_1024t = _ctx_1024t * jax.lax.rsqrt(jnp.mean(jnp.square(_ctx_1024t)) + 1e-12) * 0.953939
        ctx_1024 = -1.39393e-06 + 0.999914 * (_ctx_1024t + 0.3 * jax.random.normal(jax.random.fold_in(_rk, 611), (2, 77, 256), jnp.float32))
        return (x, ctx_1024)
    x, ctx_1024 = _rec_inputs()

    def _L0_attn_setup():
        import jax, jax.numpy as jnp
        import numpy as np
        B, S, H, NH = (2, 512, 256, 16)
        HD = H // NH
        EPS = 1e-06

        def _layernorm(x, scale, bias):
            x32 = x.astype(jnp.float32)
            mean = jnp.mean(x32, axis=-1, keepdims=True)
            var = jnp.mean(jnp.square(x32 - mean), axis=-1, keepdims=True)
            return (x32 - mean) * jax.lax.rsqrt(var + EPS) * scale + bias
        key = jax.random.key(seed)
        ks = jax.random.split(key, 16)
        init = lambda k, shape, fan_in: jax.random.normal(k, shape, jnp.float32) / np.sqrt(fan_in)
        return {'x': jax.random.normal(ks[0], (B, S, H), jnp.float32), 'Wq': init(ks[1], (H, H), H), 'bq': jnp.zeros((H,), jnp.float32), 'Wk': init(ks[2], (H, H), H), 'bk': jnp.zeros((H,), jnp.float32), 'Wv': init(ks[3], (H, H), H), 'bv': jnp.zeros((H,), jnp.float32), 'q_scale': jnp.ones((HD,), jnp.float32), 'q_bias': jnp.zeros((HD,), jnp.float32), 'k_scale': jnp.ones((HD,), jnp.float32), 'k_bias': jnp.zeros((HD,), jnp.float32), 'v_scale': jnp.ones((HD,), jnp.float32), 'v_bias': jnp.zeros((HD,), jnp.float32), 'Wo': init(ks[4], (H, H), H), 'bo': jnp.zeros((H,), jnp.float32)}
    _L0_attn_all = _L0_attn_setup()
    _L0_attn_in = {k: v for k, v in _L0_attn_all.items() if k in ('Wq', 'bq', 'Wk', 'bk', 'Wv', 'bv', 'q_scale', 'q_bias', 'k_scale', 'k_bias', 'v_scale', 'v_bias', 'Wo', 'bo')}
    del _L0_attn_all

    def _L0_xattn_setup():
        import jax, jax.numpy as jnp
        import numpy as np
        import math
        D_MODEL = 256
        N_HEADS = 16
        HEAD_DIM = D_MODEL // N_HEADS
        TOP_K = 32
        SCALE = math.sqrt(HEAD_DIM)

        def _split_heads(t, n):
            B, L, _ = t.shape
            return t.reshape(B, L, N_HEADS, HEAD_DIM).transpose(0, 2, 1, 3)
        key = jax.random.key(seed)
        ks = jax.random.split(key, 12)
        B, S, N = (2, 512, 512)
        std = 1.0 / math.sqrt(D_MODEL)
        inp = {'x': jax.random.normal(ks[0], (B, S, D_MODEL), dtype=jnp.float32), 'knowledge_embeddings': jax.random.normal(ks[1], (B, N, D_MODEL), dtype=jnp.float32), 'Wq': jax.random.normal(ks[2], (D_MODEL, D_MODEL), dtype=jnp.float32) * std, 'bq': jnp.zeros((D_MODEL,), dtype=jnp.float32), 'Wk': jax.random.normal(ks[3], (D_MODEL, D_MODEL), dtype=jnp.float32) * std, 'bk': jnp.zeros((D_MODEL,), dtype=jnp.float32), 'Wv': jax.random.normal(ks[4], (D_MODEL, D_MODEL), dtype=jnp.float32) * std, 'bv': jnp.zeros((D_MODEL,), dtype=jnp.float32), 'Wo': jax.random.normal(ks[5], (D_MODEL, D_MODEL), dtype=jnp.float32) * std, 'bo': jnp.zeros((D_MODEL,), dtype=jnp.float32)}
        return inp
    _L0_xattn_all = _L0_xattn_setup()
    _L0_xattn_in = {k: v for k, v in _L0_xattn_all.items() if k in ('Wq', 'bq', 'Wk', 'bk', 'Wv', 'bv', 'Wo', 'bo')}
    del _L0_xattn_all

    def _L0_ffn_setup():
        import jax, jax.numpy as jnp
        import numpy as np
        B, S, D, E = (2, 512, 256, 8)
        key = jax.random.key(seed)
        ks = jax.random.split(key, 5)
        x = jax.random.normal(ks[0], (B, S, D), dtype=jnp.float32)
        router_w = jax.random.normal(ks[1], (E, D), dtype=jnp.float32) * 0.02
        router_b = jnp.zeros((E,), dtype=jnp.float32)
        expert_w = jax.random.normal(ks[2], (E, D, D), dtype=jnp.float32) * 0.02
        expert_b = jnp.zeros((E, D), dtype=jnp.float32)
        return {'x': x, 'router_w': router_w, 'router_b': router_b, 'expert_w': expert_w, 'expert_b': expert_b}
    _L0_ffn_all = _L0_ffn_setup()
    _L0_ffn_in = {k: v for k, v in _L0_ffn_all.items() if k in ('router_w', 'router_b', 'expert_w', 'expert_b')}
    del _L0_ffn_all

    def _L1_attn_setup():
        import jax, jax.numpy as jnp
        import numpy as np
        B, S, D, H = (2, 512, 256, 16)
        HD = D // H
        key = jax.random.key(seed)
        k0, k1, k2 = jax.random.split(key, 3)
        return {'x': jax.random.normal(k0, (B, S, D), jnp.float32), 'qkv_w': jax.random.normal(k1, (D, 3 * D), jnp.float32) / np.sqrt(D).astype(np.float32), 'qkv_b': jnp.zeros((3 * D,), jnp.float32), 'out_w': jax.random.normal(k2, (D, D), jnp.float32) / np.sqrt(D).astype(np.float32), 'out_b': jnp.zeros((D,), jnp.float32)}
    _L1_attn_all = _L1_attn_setup()
    _L1_attn_in = {k: v for k, v in _L1_attn_all.items() if k in ('qkv_w', 'qkv_b', 'out_w', 'out_b')}
    del _L1_attn_all

    def _L1_xattn_setup():
        import jax, jax.numpy as jnp
        import numpy as np
        NUM_HEADS = 16
        D_MODEL = 256
        LN_EPS = 1e-05
        key = jax.random.key(seed)
        ks = jax.random.split(key, 10)
        B, S, D = (2, 512, D_MODEL)
        s = 1.0 / np.sqrt(D)
        return {'encoded': jax.random.normal(ks[0], (B, S, D), jnp.float32), 'decoded': jax.random.normal(ks[1], (B, S, D), jnp.float32), 'Wq': jax.random.normal(ks[2], (D, D), jnp.float32) * s, 'bq': jax.random.normal(ks[3], (D,), jnp.float32) * s, 'Wk': jax.random.normal(ks[4], (D, D), jnp.float32) * s, 'bk': jax.random.normal(ks[5], (D,), jnp.float32) * s, 'Wv': jax.random.normal(ks[6], (D, D), jnp.float32) * s, 'bv': jax.random.normal(ks[7], (D,), jnp.float32) * s, 'gamma': jnp.ones((D,), jnp.float32), 'beta': jnp.zeros((D,), jnp.float32)}
    _L1_xattn_all = _L1_xattn_setup()
    _L1_xattn_in = {k: v for k, v in _L1_xattn_all.items() if k in ('Wq', 'bq', 'Wk', 'bk', 'Wv', 'bv', 'gamma', 'beta')}
    del _L1_xattn_all

    def _L1_ffn_setup():
        import jax, jax.numpy as jnp
        import numpy as np
        H, E, DFF = (256, 8, 1024)
        key = jax.random.key(seed)
        ks = jax.random.split(key, 7)
        s = lambda *shape: 1.0 / np.sqrt(shape[-2] if len(shape) > 1 else shape[-1])
        x = jax.random.normal(ks[0], (2, 512, H), dtype=jnp.float32)
        Wr = jax.random.normal(ks[1], (H, E), dtype=jnp.float32) * (1.0 / np.sqrt(H))
        br = jnp.zeros((E,), dtype=jnp.float32)
        W1 = jax.random.normal(ks[2], (E, H, DFF), dtype=jnp.float32) * (1.0 / np.sqrt(H))
        b1 = jnp.zeros((E, DFF), dtype=jnp.float32)
        W2 = jax.random.normal(ks[3], (E, DFF, H), dtype=jnp.float32) * (1.0 / np.sqrt(DFF))
        b2 = jnp.zeros((E, H), dtype=jnp.float32)
        return {'x': x, 'Wr': Wr, 'br': br, 'W1': W1, 'b1': b1, 'W2': W2, 'b2': b2}
    _L1_ffn_all = _L1_ffn_setup()
    _L1_ffn_in = {k: v for k, v in _L1_ffn_all.items() if k in ('Wr', 'br', 'W1', 'b1', 'W2', 'b2')}
    del _L1_ffn_all
    return {'x': x, 'ctx_1024': ctx_1024, 'L0_attn_Wq': _L0_attn_in['Wq'], 'L0_attn_bq': _L0_attn_in['bq'], 'L0_attn_Wk': _L0_attn_in['Wk'], 'L0_attn_bk': _L0_attn_in['bk'], 'L0_attn_Wv': _L0_attn_in['Wv'], 'L0_attn_bv': _L0_attn_in['bv'], 'L0_attn_q_scale': _L0_attn_in['q_scale'], 'L0_attn_q_bias': _L0_attn_in['q_bias'], 'L0_attn_k_scale': _L0_attn_in['k_scale'], 'L0_attn_k_bias': _L0_attn_in['k_bias'], 'L0_attn_v_scale': _L0_attn_in['v_scale'], 'L0_attn_v_bias': _L0_attn_in['v_bias'], 'L0_attn_Wo': _L0_attn_in['Wo'], 'L0_attn_bo': _L0_attn_in['bo'], 'L0_xattn_Wq': _L0_xattn_in['Wq'], 'L0_xattn_bq': _L0_xattn_in['bq'], 'L0_xattn_Wk': _L0_xattn_in['Wk'], 'L0_xattn_bk': _L0_xattn_in['bk'], 'L0_xattn_Wv': _L0_xattn_in['Wv'], 'L0_xattn_bv': _L0_xattn_in['bv'], 'L0_xattn_Wo': _L0_xattn_in['Wo'], 'L0_xattn_bo': _L0_xattn_in['bo'], 'L0_ffn_router_w': _L0_ffn_in['router_w'], 'L0_ffn_router_b': _L0_ffn_in['router_b'], 'L0_ffn_expert_w': _L0_ffn_in['expert_w'], 'L0_ffn_expert_b': _L0_ffn_in['expert_b'], 'L1_attn_qkv_w': _L1_attn_in['qkv_w'], 'L1_attn_qkv_b': _L1_attn_in['qkv_b'], 'L1_attn_out_w': _L1_attn_in['out_w'], 'L1_attn_out_b': _L1_attn_in['out_b'], 'L1_xattn_Wq': _L1_xattn_in['Wq'], 'L1_xattn_bq': _L1_xattn_in['bq'], 'L1_xattn_Wk': _L1_xattn_in['Wk'], 'L1_xattn_bk': _L1_xattn_in['bk'], 'L1_xattn_Wv': _L1_xattn_in['Wv'], 'L1_xattn_bv': _L1_xattn_in['bv'], 'L1_xattn_gamma': _L1_xattn_in['gamma'], 'L1_xattn_beta': _L1_xattn_in['beta'], 'L1_ffn_Wr': _L1_ffn_in['Wr'], 'L1_ffn_br': _L1_ffn_in['br'], 'L1_ffn_W1': _L1_ffn_in['W1'], 'L1_ffn_b1': _L1_ffn_in['b1'], 'L1_ffn_W2': _L1_ffn_in['W2'], 'L1_ffn_b2': _L1_ffn_in['b2']}

def reference(x, ctx_1024, L0_attn_Wq, L0_attn_bq, L0_attn_Wk, L0_attn_bk, L0_attn_Wv, L0_attn_bv, L0_attn_q_scale, L0_attn_q_bias, L0_attn_k_scale, L0_attn_k_bias, L0_attn_v_scale, L0_attn_v_bias, L0_attn_Wo, L0_attn_bo, L0_xattn_Wq, L0_xattn_bq, L0_xattn_Wk, L0_xattn_bk, L0_xattn_Wv, L0_xattn_bv, L0_xattn_Wo, L0_xattn_bo, L0_ffn_router_w, L0_ffn_router_b, L0_ffn_expert_w, L0_ffn_expert_b, L1_attn_qkv_w, L1_attn_qkv_b, L1_attn_out_w, L1_attn_out_b, L1_xattn_Wq, L1_xattn_bq, L1_xattn_Wk, L1_xattn_bk, L1_xattn_Wv, L1_xattn_bv, L1_xattn_gamma, L1_xattn_beta, L1_ffn_Wr, L1_ffn_br, L1_ffn_W1, L1_ffn_b1, L1_ffn_W2, L1_ffn_b2):
    import jax
    import jax.numpy as jnp

    def _L0_attn_ref(x, Wq, bq, Wk, bk, Wv, bv, q_scale, q_bias, k_scale, k_bias, v_scale, v_bias, Wo, bo):
        import jax, jax.numpy as jnp
        import numpy as np
        B, S, H, NH = (2, 512, 256, 16)
        HD = H // NH
        EPS = 1e-06

        def _layernorm(x, scale, bias):
            x32 = x.astype(jnp.float32)
            mean = jnp.mean(x32, axis=-1, keepdims=True)
            var = jnp.mean(jnp.square(x32 - mean), axis=-1, keepdims=True)
            return (x32 - mean) * jax.lax.rsqrt(var + EPS) * scale + bias
        b, s, _ = x.shape
        q = (x @ Wq + bq).reshape(b, s, NH, HD)
        k = (x @ Wk + bk).reshape(b, s, NH, HD)
        v = (x @ Wv + bv).reshape(b, s, NH, HD)
        q = _layernorm(q, q_scale, q_bias)
        k = _layernorm(k, k_scale, k_bias)
        v = _layernorm(v, v_scale, v_bias)
        scale = HD ** (-0.5)
        scores = jnp.einsum('bqhd,bkhd->bhqk', q, k) * scale
        probs = jax.nn.softmax(scores, axis=-1)
        out = jnp.einsum('bhqk,bkhd->bqhd', probs, v).reshape(b, s, NH * HD)
        return out @ Wo + bo

    def _L0_xattn_ref(x, knowledge_embeddings, Wq, bq, Wk, bk, Wv, bv, Wo, bo):
        import jax, jax.numpy as jnp
        import numpy as np
        import math
        D_MODEL = 256
        N_HEADS = 16
        HEAD_DIM = D_MODEL // N_HEADS
        TOP_K = 32
        SCALE = math.sqrt(HEAD_DIM)

        def _split_heads(t, n):
            B, L, _ = t.shape
            return t.reshape(B, L, N_HEADS, HEAD_DIM).transpose(0, 2, 1, 3)
        B, S, _ = x.shape
        N = knowledge_embeddings.shape[1]
        Q = _split_heads(x @ Wq.T + bq, N_HEADS)
        K = _split_heads(knowledge_embeddings @ Wk.T + bk, N_HEADS)
        V = _split_heads(knowledge_embeddings @ Wv.T + bv, N_HEADS)
        scores = jnp.einsum('bhsd,bhnd->bhsn', Q, K) / SCALE
        k = min(TOP_K, N)
        topk_scores, topk_indices = jax.lax.top_k(scores, k)
        sparse_weights = jax.nn.softmax(topk_scores, axis=-1)
        sel_V = jnp.take_along_axis(V[:, :, None, :, :], topk_indices[..., None], axis=3)
        context = jnp.einsum('bhsk,bhskd->bhsd', sparse_weights, sel_V)
        context = context.transpose(0, 2, 1, 3).reshape(B, S, D_MODEL)
        return context @ Wo.T + bo

    def _L0_ffn_ref(x, router_w, router_b, expert_w, expert_b):
        import jax, jax.numpy as jnp
        import numpy as np
        B, S, D, E = (2, 512, 256, 8)
        logits = jnp.einsum('bsd,ed->bse', x, router_w) + router_b
        probs = jax.nn.softmax(logits, axis=-1)
        weights = jnp.max(probs, axis=-1)
        top1 = jnp.argmax(probs, axis=-1)
        y_all = jnp.einsum('bsd,eod->bseo', x, expert_w) + expert_b
        y = jnp.take_along_axis(y_all, top1[:, :, None, None], axis=2)[:, :, 0, :]
        out = y * weights[:, :, None]
        return out

    def _L1_attn_ref(x, qkv_w, qkv_b, out_w, out_b):
        import jax, jax.numpy as jnp
        import numpy as np
        B, S, D, H = (2, 512, 256, 16)
        HD = D // H
        b, s, d = x.shape
        h, hd = (H, d // H)
        scale = 1.0 / np.sqrt(hd).astype(np.float32)
        qkv = (x @ qkv_w + qkv_b).reshape(b, s, 3, h, hd)
        q, k, v = (qkv[:, :, 0], qkv[:, :, 1], qkv[:, :, 2])
        logits = jnp.einsum('bqhd,bkhd->bhqk', q, k)
        causal_mask = jnp.triu(jnp.ones((s, s), bool), 1)
        logits = jnp.where(causal_mask, -jnp.inf, logits) * scale
        att = jax.nn.softmax(logits, axis=-1)
        out = jnp.einsum('bhqk,bkhd->bqhd', att, v).reshape(b, s, d)
        return out @ out_w + out_b

    def _L1_xattn_ref(encoded, decoded, Wq, bq, Wk, bk, Wv, bv, gamma, beta):
        import jax, jax.numpy as jnp
        import numpy as np
        NUM_HEADS = 16
        D_MODEL = 256
        LN_EPS = 1e-05
        B, Sq, D = decoded.shape
        H = NUM_HEADS
        dh = D // H
        q = decoded @ Wq.T + bq
        k = encoded @ Wk.T + bk
        v = encoded @ Wv.T + bv
        q = q.reshape(B, Sq, H, dh).transpose(0, 2, 1, 3)
        k = k.reshape(B, -1, H, dh).transpose(0, 2, 1, 3)
        v = v.reshape(B, -1, H, dh).transpose(0, 2, 1, 3)
        qk = jnp.einsum('bhqd,bhkd->bhqk', q, k)
        qk = jnp.where(jnp.isnan(qk), -jnp.inf, qk)
        attn = jax.nn.softmax(qk, axis=-1)
        attn = jnp.where(jnp.isnan(attn), 0.0, attn)
        v = jnp.where(jnp.isnan(v), 0.0, v)
        z = jnp.einsum('bhqk,bhkd->bhqd', attn, v)
        z = z.reshape(B, Sq, D)
        x = z + decoded
        mu = jnp.mean(x, axis=-1, keepdims=True)
        var = jnp.var(x, axis=-1, keepdims=True)
        return (x - mu) * jax.lax.rsqrt(var + LN_EPS) * gamma + beta

    def _L1_ffn_ref(x, Wr, br, W1, b1, W2, b2):
        import jax, jax.numpy as jnp
        import numpy as np
        H, E, DFF = (256, 8, 1024)
        B, S, Hd = x.shape
        n_exp = W1.shape[0]
        xt = x.reshape(-1, Hd)
        logits = xt @ Wr + br
        probs = jax.nn.softmax(logits, axis=-1)
        gate = jnp.max(probs, axis=-1)
        idx = jnp.argmax(probs, axis=-1)
        h1 = jnp.maximum(jnp.einsum('th,ehf->etf', xt, W1) + b1[:, None, :], 0.0)
        ye = jnp.einsum('etf,efh->eth', h1, W2) + b2[:, None, :]
        onehot = jax.nn.one_hot(idx, n_exp, dtype=xt.dtype)
        y = jnp.einsum('te,eth->th', onehot, ye) * gate[:, None]
        return y.reshape(B, S, Hd)
    x = x + _L0_attn_ref(_layernorm(x, axis=-1), L0_attn_Wq, L0_attn_bq, L0_attn_Wk, L0_attn_bk, L0_attn_Wv, L0_attn_bv, L0_attn_q_scale, L0_attn_q_bias, L0_attn_k_scale, L0_attn_k_bias, L0_attn_v_scale, L0_attn_v_bias, L0_attn_Wo, L0_attn_bo)
    x = x + _L0_xattn_ref(_layernorm(x, axis=-1), ctx_1024, L0_xattn_Wq, L0_xattn_bq, L0_xattn_Wk, L0_xattn_bk, L0_xattn_Wv, L0_xattn_bv, L0_xattn_Wo, L0_xattn_bo)
    x = x + _L0_ffn_ref(_layernorm(x, axis=-1), L0_ffn_router_w, L0_ffn_router_b, L0_ffn_expert_w, L0_ffn_expert_b)
    x = x + _L1_attn_ref(_layernorm(x, axis=-1), L1_attn_qkv_w, L1_attn_qkv_b, L1_attn_out_w, L1_attn_out_b)
    x = x + _L1_xattn_ref(ctx_1024, _layernorm(x, axis=-1), L1_xattn_Wq, L1_xattn_bq, L1_xattn_Wk, L1_xattn_bk, L1_xattn_Wv, L1_xattn_bv, L1_xattn_gamma, L1_xattn_beta)
    x = x + _L1_ffn_ref(_layernorm(x, axis=-1), L1_ffn_Wr, L1_ffn_br, L1_ffn_W1, L1_ffn_b1, L1_ffn_W2, L1_ffn_b2)
    return x

_drawn_inputs = setup_inputs


def setup_inputs(seed=0):
    import zlib

    import numpy as np

    out = dict(_drawn_inputs(seed))
    spreads = {'L0_attn_bq': (0.0, 0.517),
     'L0_attn_bk': (0.0, 0.8),
     'L0_attn_bv': (0.0, 0.1),
     'L0_attn_q_scale': (1.0, 0.6),
     'L0_attn_q_bias': (0.0, 0.532),
     'L0_attn_k_scale': (1.0, 0.6),
     'L0_attn_k_bias': (0.0, 0.8),
     'L0_attn_v_scale': (1.0, 0.2),
     'L0_attn_v_bias': (0.0, 0.1),
     'L0_attn_bo': (0.0, 0.1),
     'L0_xattn_bq': (0.0, 0.1),
     'L0_xattn_bk': (0.0, 0.8),
     'L0_xattn_bv': (0.0, 0.1),
     'L0_xattn_bo': (0.0, 0.1),
     'L0_ffn_router_b': (0.0, 0.1),
     'L0_ffn_expert_b': (0.0, 0.351),
     'L1_attn_qkv_b': (0.0, 0.1),
     'L1_attn_out_b': (0.0, 0.1),
     'L1_xattn_gamma': (1.0, 0.2),
     'L1_xattn_beta': (0.0, 0.1),
     'L1_ffn_br': (0.0, 0.1),
     'L1_ffn_b1': (0.0, 0.639),
     'L1_ffn_b2': (0.0, 0.443)}
    factors = {'L1_xattn_bk': 8.0}
    for name, (base, spread) in spreads.items():
        noise = np.random.default_rng([zlib.crc32(name.encode()), seed]).standard_normal(out[name].shape)
        drawn = base * np.exp(spread * noise) if base else spread * noise
        out[name] = jnp.asarray(drawn.astype(out[name].dtype))
    for name, factor in factors.items():
        out[name] = (out[name] * factor).astype(out[name].dtype)
    return out
```

```python
from contextlib import ExitStack

import concourse.bass as bass
from concourse import mybir

F32 = mybir.dt.float32
BF16 = mybir.dt.bfloat16
I32 = mybir.dt.int32
U32 = mybir.dt.uint32
ALU = mybir.AluOpType
ACT = mybir.ActivationFunctionType
AX = mybir.AxisListType

P = 128
B, S, D = 2, 1024, 256
KD = D // P
NH, HD = 16, 16
T = B * S // P
TB = T // B
C = 77
E, F = 8, 1024
KF = F // P
BANK = 512
G = 4
NG = NH // G
NU = B * NG
SLOT = 32
QUERY_PARTS = (0, 0, 0, 1, 1, 2)
KEY_PARTS = (0, 1, 2, 0, 1, 0)
NPART = 3
NSLOT = len(QUERY_PARTS)
KS = NSLOT * HD
KM = KS + 2
NST = 3
PR = 8
SCALE = HD ** -0.5
TOPK = 32
LOWEST = -3.0e38
MASKED = -1.0e30
NS = T + E - 1
LN_EPS = 1e-5
L0_EPS = 1e-6


class Region:

    def __init__(self, arena, size):
        self.arena, self.size, self.at = arena, size, 0

    def f32(self, n):
        a = self.at
        self.at += n
        assert self.at <= self.size, (self.at, self.size)
        return self.arena[:, a:a + n]

    def bf16(self, n):
        return self.f32((n + 1) // 2).bitcast(BF16)


def fills(causal):
    out = []
    for i in range(TB):
        keys = (i + 1) * P if causal else S
        for k in range(0, keys, BANK):
            out.append((i, k // BANK, min(BANK, keys - k)))
    return out


def build(nc, a, out):
    ctx = ExitStack()
    with ctx:
        sems = {}
        KEPT = ("const", "w_in", "xw_in", "kblk", "xv", "xwo", "xs_clear", "x_in", "out", "e0_x")

        def sem(name):
            if name not in sems:
                sems[name] = nc.alloc_semaphore(name)
            return sems[name]

        SIZE = 53200
        arena = ctx.enter_context(nc.sbuf_tensor("arena", [P, SIZE], F32))
        PS = ctx.enter_context(nc.psum_tensor("banks", [P, 8, BANK], F32))
        R = Region(arena, SIZE)

        def scratch(name, shape, dt=F32):
            return nc.dram_tensor(name, shape, dt, kind="Internal").ap()

        parts_dram = [scratch(f"parts{l}", [2, NPART, B * D, S], BF16) for l in range(2)]
        v_dram = [scratch(f"v{l}", [NU, P, TB, G * SLOT]) for l in range(2)]
        o_dram = [scratch(f"o{l}", [B * D, S]) for l in range(2)]
        sum_dram = [scratch(f"sum{l}", [B * P, P]) for l in range(2)]
        rec_dram = [scratch(f"rec{l}", [B * NH, S]) for l in range(2)]
        xs_dram = [scratch(f"sorted{l}", [NS * P, D]) for l in range(2)]
        ys_dram = [scratch(f"expert_out{l}", [NS * P, D]) for l in range(2)]

        x = R.f32(T * D).rearrange("p (t d) -> p t d", t=T)
        h = R.f32(T * D).rearrange("p (t d) -> p t d", t=T)
        hT = R.f32(KD * B * S).rearrange("p (k n) -> p k n", k=KD)
        ident = R.f32(P)
        identb = R.bf16(P)
        upper = R.bf16(P)
        onesb = R.bf16(P)
        onesf = R.f32(P)
        future = R.bf16(P)
        futureT = R.bf16(P)
        stats = R.f32(T * 6).rearrange("p (t s) -> p t s", t=T)
        mv = R.f32(T * 2).rearrange("p (t s) -> p t s", t=T)
        std = R.f32(T)
        rstd = R.f32(T)
        count = R.f32(32)
        order = R.f32(E)
        hmask = R.f32(8)
        pick = R.f32(NG * D).rearrange("p (g n) -> p g n", g=NG)
        base_mark = R.at

        w_qkv = [R.f32(3 * 3 * D).rearrange("p (k n) -> p k n", k=3) for _ in range(2)]
        w_out = [R.f32(KD * D).rearrange("p (k n) -> p k n", k=KD) for _ in range(2)]
        b_out = [R.f32(D) for _ in range(2)]
        b_qk1 = R.f32(4)
        ln_scale = R.f32(3 * HD).rearrange("p (s d) -> p s d", s=3)
        ln_bias = R.f32(3 * HD).rearrange("p (s d) -> p s d", s=3)
        cmean = R.f32(9 * NH)
        xb_out = R.f32(D)
        gamma, beta = R.f32(D), R.f32(D)
        xq_b = [R.f32(KD) for _ in range(2)]
        xk_b = [R.f32(KD) for _ in range(2)]
        xv_b = [R.f32(D) for _ in range(2)]
        xwqT = [R.f32(KD * D).rearrange("p (k n) -> p k n", k=KD) for _ in range(2)]
        xwo = R.f32(NG * D).rearrange("p (g n) -> p g n", g=NG)
        ctxT = R.f32(KD * B * C).rearrange("p (k n) -> p k n", k=KD)
        kblk = [R.f32(B * KD * 8 * C).rearrange("p (b k j c) -> p b k j c", b=B, k=KD, j=8) for _ in range(2)]
        xv = [R.f32(B * NH * SLOT).rearrange("p (b h s) -> p b h s", b=B, h=NH) for _ in range(2)]
        work_mark = R.at


        W0_IN, XW_IN, W_IN = 16 * 12, 16 * (8 + 2 * 5), 16 * 13
        CONST = 33

        def prepare(block):
            R.at = work_mark
            xw_names = [("L0_xattn_Wk", 0), ("L0_xattn_Wv", 0), ("L1_xattn_Wk", 1), ("L1_xattn_Wv", 1),
                        ("L0_xattn_Wq", 0), ("L1_xattn_Wq", 1), ("L0_xattn_Wo", 0)]
            xw_raw = [R.f32(KD * D).rearrange("p (k n) -> p k n", k=KD) for _ in xw_names]
            xw_t = [R.f32(KD * D).rearrange("p (k n) -> p k n", k=KD) for _ in range(4)]
            ctx_raw = R.f32(B * D).rearrange("p (b d) -> p b d", b=B)
            ctx_wo = R.f32(KD * D).rearrange("p (k n) -> p k n", k=KD)
            kt_raw = R.f32(KD * B * C).rearrange("p (k n) -> p k n", k=KD)
            vx_raw = R.f32(D)
            vx_mask = R.f32(D).bitcast(I32)
            ZW = 2048
            zero_tile = R.f32(ZW)
            tmp = R.f32(P)

            @block.sync
            def _(sp):
                def load(dst, src, name):
                    sp.dma_start(dst, src).then_inc(sem(name), 16)

                for b in range(B):
                    for t in range(0, TB, 4):
                        load(x[:, b * TB + t:b * TB + t + 4, :],
                             a["x"][b].rearrange("(t p) d -> p t d", p=P)[:, t:t + 4, :], "x_in")
                for i, n in enumerate(("Wq", "Wk", "Wv")):
                    load(w_qkv[0][:, 0:KD, i * D:(i + 1) * D], a[f"L0_attn_{n}"].rearrange("(k p) n -> p k n", p=P), "w0_in")
                for i, n in enumerate(("bq", "bk", "bv")):
                    load(w_qkv[0][:, 2, i * D:(i + 1) * D], a[f"L0_attn_{n}"].partition_broadcast(P), "w0_in")
                for i, n in enumerate("qkv"):
                    load(ln_scale[:, i, :], a[f"L0_attn_{n}_scale"].partition_broadcast(P), "w0_in")
                    load(ln_bias[:, i, :], a[f"L0_attn_{n}_bias"].partition_broadcast(P), "w0_in")
                for (n, _), dst in zip(xw_names, xw_raw):
                    load(dst, a[n].rearrange("(k p) n -> p k n", p=P), "xw_in")
                load(ctx_raw[0:C], a["ctx_1024"].rearrange("b c d -> c b d"), "xw_in")
                for l in range(2):
                    for dst, n in ((xq_b[l], "bq"), (xk_b[l], "bk")):
                        for k in range(KD):
                            load(dst[:, k:k + 1], a[f"L{l}_xattn_{n}"][k * P:(k + 1) * P].unsqueeze(1), "xw_in")
                    load(xv_b[l][0:C], a[f"L{l}_xattn_bv"].partition_broadcast(C), "xw_in")
                load(w_out[0], a["L0_attn_Wo"].rearrange("(k p) n -> p k n", p=P), "w_in")
                load(b_out[0], a["L0_attn_bo"].partition_broadcast(P), "w_in")
                load(xb_out, a["L0_xattn_bo"].partition_broadcast(P), "w_in")
                load(w_qkv[1][:, 0:KD, :], a["L1_attn_qkv_w"].rearrange("(k p) n -> p k n", p=P), "w_in")
                load(w_qkv[1][:, 2, :], a["L1_attn_qkv_b"].partition_broadcast(P), "w_in")
                for k in range(4):
                    load(b_qk1[:, k:k + 1], a["L1_attn_qkv_b"][k * P:(k + 1) * P].unsqueeze(1), "w_in")
                load(w_out[1], a["L1_attn_out_w"].rearrange("(k p) n -> p k n", p=P), "w_in")
                load(b_out[1], a["L1_attn_out_b"].partition_broadcast(P), "w_in")
                load(gamma, a["L1_xattn_gamma"].partition_broadcast(P), "w_in")
                load(beta, a["L1_xattn_beta"].partition_broadcast(P), "w_in")
                sp.wait_ge(sem("zeroed"), 1)
                for l in range(2):
                    rows = xs_dram[l].rearrange("(p r) d -> p (r d)", p=P)
                    for n0 in range(0, NS * D, ZW):
                        w = min(ZW, NS * D - n0)
                        sp.dma_start(rows[:, n0:n0 + w], zero_tile[:, 0:w]).then_inc(sem("xs_clear"), 16)


            @block.gpsimd
            def _(pool):
                pool.memset(zero_tile, 0.0).then_inc(sem("zeroed"), 1)
                pool.memset(tmp, 0.0).then_inc(sem("const"), 1)
                pool.memset(onesf, 1.0).then_inc(sem("const"), 1)
                pool.memset(onesb, 1.0).then_inc(sem("const"), 1)
                pool.memset(hmask, 1.0).then_inc(sem("const"), 1)
                pool.memset(pick.rearrange("p g n -> p (g n)"), 0.0).then_inc(sem("const"), 1)
                pool.memset(xwo.rearrange("p g n -> p (g n)"), 0.0).then_inc(sem("const"), 1)
                for l in range(2):
                    pool.memset(xv[l].rearrange("p b h s -> p (b h s)"), 0.0).then_inc(sem("const"), 1)
                pool.iota(count, pattern=[[1, 32]], base=0, channel_multiplier=0,
                          allow_small_or_imprecise_dtypes=True).then_inc(sem("const"), 1)
                pool.iota(order, pattern=[[-1, E]], base=E, channel_multiplier=0,
                          allow_small_or_imprecise_dtypes=True).then_inc(sem("const"), 1)
                pool.wait_ge(sem("const"), 10)
                pool.affine_select(out=ident, in_=tmp, compare_op=ALU.not_equal, fill=1.0, base=0,
                                   pattern=[[-1, P]], channel_multiplier=1).then_inc(sem("const"), 1)
                pool.affine_select(out=hmask, in_=hmask, compare_op=ALU.is_ge, fill=0.0, base=0,
                                   pattern=[[-HD, 8]], channel_multiplier=1).then_inc(sem("const"), 1)
                pool.affine_select(out=upper, in_=onesb, compare_op=ALU.is_gt, fill=0.0, base=0,
                                   pattern=[[1, P]], channel_multiplier=-1).then_inc(sem("const"), 1)
                pool.affine_select(out=future, in_=tmp, compare_op=ALU.is_ge, fill=MASKED, base=0,
                                   pattern=[[-1, P]], channel_multiplier=1).then_inc(sem("const"), 1)
                pool.affine_select(out=futureT, in_=tmp, compare_op=ALU.is_ge, fill=MASKED, base=0,
                                   pattern=[[1, P]], channel_multiplier=-1).then_inc(sem("const"), 1)
                for j in range(G):
                    for g in range(NG):
                        blk = pick[:, g, (g * G + j) * HD:(g * G + j + 1) * HD]
                        pool.affine_select(out=blk, in_=blk, compare_op=ALU.not_equal, fill=1.0, base=-SLOT * j,
                                           pattern=[[-1, HD]], channel_multiplier=1).then_inc(sem("const"), 1)
                pool.wait_ge(sem("const"), 15 + 16)
                pool.affine_select(out=hmask, in_=hmask, compare_op=ALU.is_ge, fill=0.0, base=HD - 1,
                                   pattern=[[HD, 8]], channel_multiplier=-1).then_inc(sem("const"), 1)
                pool.tensor_copy(identb, ident).then_inc(sem("const"), 1)


            @block.vector
            def _(dve):
                dve.wait_ge(sem("w0_in"), W0_IN)
                flat = w_qkv[0].rearrange("p k (h d) -> p (k h) d", d=HD)
                dve.tensor_reduce(cmean, flat, AX.X, ALU.add).then_inc(sem("centre"), 1)
                dve.wait_ge(sem("centre"), 1)
                dve.tensor_scalar(cmean, cmean, 1.0 / HD, None, ALU.mult).then_inc(sem("centre"), 1)
                dve.wait_ge(sem("centre"), 2)
                dve.tensor_tensor(flat, flat, cmean.unsqueeze(2).to_broadcast([P, 9 * NH, HD]),
                                  ALU.subtract).then_inc(sem("centre"), 1)

            @block.tensor
            def _(pe):
                pe.wait_ge(sem("const"), CONST)
                pe.wait_ge(sem("xw_in"), XW_IN)
                for n in range(len(xw_names)):
                    if n >= 2:
                        pe.wait_ge(sem("xwT"), n - 1)
                    for ko in range(KD):
                        for ki in range(KD):
                            mm = pe.transpose(PS[:, n % 2, (ki * KD + ko) * P:(ki * KD + ko + 1) * P],
                                              xw_raw[n][:, ko, ki * P:(ki + 1) * P], ident)
                    mm.then_inc(sem("xwT_ps"), 1)
                for b in range(B):
                    for k in range(KD):
                        mm = pe.transpose(PS[:, 2, (k * B + b) * C:(k * B + b + 1) * C],
                                          ctx_raw[0:C, b, k * P:(k + 1) * P], ident[0:C, 0:C])
                mm.then_inc(sem("ctxT_ps"), 1)
                pe.wait_ge(sem("ctxT"), 1)
                pe.wait_ge(sem("xwT"), len(xw_names))
                n = 0
                for l in range(2):
                    for half in range(KD):
                        if n >= 2:
                            pe.wait_ge(sem("kt"), n - 1)
                        for k in range(KD):
                            mm = pe.matmul(PS[:, 3 + n % 2, 0:B * C], xw_t[2 * l][:, k, half * P:(half + 1) * P],
                                           ctxT[:, k, :], start=(k == 0), stop=(k == KD - 1))
                        mm.then_inc(sem("kt_ps"), 1)
                        n += 1
                n = 0
                for l in range(2):
                    for b in range(B):
                        if n >= 2:
                            pe.wait_ge(sem("vx"), n - 1)
                        for k in range(KD):
                            mm = pe.matmul(PS[0:C, 5 + n % 2, 0:D], ctxT[:, k, b * C:(b + 1) * C],
                                           xw_t[2 * l + 1][:, k, :], start=(k == 0), stop=(k == KD - 1))
                        mm.then_inc(sem("vx_ps"), 1)
                        n += 1

            @block.vector
            def _(dve):
                dve.wait_ge(sem("const"), CONST)
                for n in range(len(xw_names)):
                    dve.wait_ge(sem("xwT_ps"), n + 1)
                    src = PS[:, n % 2, 0:KD * D].rearrange("p (k n) -> p k n", k=KD)
                    if n < 4:
                        dve.tensor_copy(xw_t[n], src).then_inc(sem("xwT"), 1)
                    elif n < 6:
                        dve.tensor_copy(xwqT[n - 4], src).then_inc(sem("xwT"), 1)
                    else:
                        dve.tensor_copy(ctx_wo, src).then_inc(sem("xwT"), 1)
                dve.wait_ge(sem("ctxT_ps"), 1)
                dve.tensor_copy(ctxT, PS[:, 2, 0:KD * B * C].rearrange("p (k n) -> p k n", k=KD)).then_inc(sem("ctxT"), 1)
                n = 0
                for l in range(2):
                    for half in range(KD):
                        dve.wait_ge(sem("kt_ps"), n + 1)
                        if n:
                            dve.wait_ge(sem("kblk"), n * B)
                        dve.tensor_scalar(kt_raw[:, 0, :], PS[:, 3 + n % 2, 0:B * C], xk_b[l][:, half:half + 1], None,
                                          ALU.add).then_inc(sem("kt"), 1)
                        dve.wait_ge(sem("kt"), n + 1)
                        for b in range(B):
                            dve.tensor_tensor(kblk[l][:, b, half], kt_raw[:, 0, b * C:(b + 1) * C].unsqueeze(1).to_broadcast([P, 8, C]),
                                              hmask.unsqueeze(2).to_broadcast([P, 8, C]), ALU.mult).then_inc(sem("kblk"), 1)
                        n += 1
                n = 0
                for l in range(2):
                    for b in range(B):
                        dve.wait_ge(sem("vx_ps"), n + 1)
                        if n:
                            dve.wait_ge(sem("xv"), n)
                        dst = xv[l][0:C, b, :, 0:HD]
                        dve.tensor_tensor(vx_raw[0:C], PS[0:C, 5 + n % 2, 0:D], xv_b[l][0:C], ALU.add).then_inc(sem("vx"), 1)
                        dve.wait_ge(sem("vx"), n + 1)
                        if l == 1:
                            dve.tensor_tensor(vx_mask[0:C], vx_raw[0:C], vx_raw[0:C], ALU.is_equal).then_inc(sem("vxm"), 1)
                            dve.wait_ge(sem("vxm"), b + 1)
                            dve.copy_predicated(dst, vx_mask[0:C].rearrange("p (h d) -> p h d", h=NH),
                                                vx_raw[0:C].rearrange("p (h d) -> p h d", h=NH)).then_inc(sem("xv"), 1)
                        else:
                            dve.tensor_copy(dst, vx_raw[0:C].rearrange("p (h d) -> p h d", h=NH)).then_inc(sem("xv"), 1)
                        n += 1
                dve.wait_ge(sem("xv"), 2 * B)

            wo_rows = scratch("wo_rows", [D, D])

            @block.sync
            def _(sp):
                sp.wait_ge(sem("xwT"), len(xw_names))
                sp.dma_start(wo_rows.rearrange("(k p) n -> p k n", p=P), ctx_wo).then_inc(sem("wo_st"), 16)
                sp.wait_ge(sem("wo_st"), 16)
                sp.wait_ge(sem("const"), CONST)
                for j in range(G):
                    src = wo_rows.rearrange("(g j d) n -> j d g n", g=NG, j=G)
                    sp.dma_start(xwo[SLOT * j:SLOT * j + HD], src[j]).then_inc(sem("xwo"), 16)

        def ln(block, s, x_sem, x_val, transposed=True):
            @block.vector
            def _(dve):
                dve.wait_ge(sem(x_sem), x_val)
                for t in range(T):
                    dve.bn_stats(stats[:, t, :], x[:, t, :]).then_inc(sem(s + "_st"), 1)
                for t in range(T):
                    dve.wait_ge(sem(s + "_st"), t + 1)
                    dve.bn_aggr(mv[:, t, :], stats[:, t, :]).then_inc(sem(s + "_mv"), 1)
                dve.wait_ge(sem(s + "_mv"), T)
                dve.tensor_scalar(std, mv[:, :, 1], LN_EPS, None, ALU.add).then_inc(sem(s + "_var"), 1)
                dve.wait_ge(sem(s + "_std"), 1)
                dve.reciprocal(rstd, std).then_inc(sem(s + "_rstd"), 1)
                dve.wait_ge(sem(s + "_rstd"), 1)
                for t in range(T):
                    dve.tensor_scalar(h[:, t, :], x[:, t, :], mv[:, t, 0:1], rstd[:, t:t + 1], ALU.subtract,
                                      ALU.mult).then_inc(sem(s + "_h"), 1)

            @block.scalar
            def _(act):
                act.wait_ge(sem(s + "_var"), 1)
                act.activation(std, std, ACT.Sqrt).then_inc(sem(s + "_std"), 1)
                for t in range(T):
                    act.wait_ge(sem(s + "_tr"), t + 1)
                    act.copy(hT[:, :, t * P:(t + 1) * P],
                             PS[:, 6 + t % 2, 0:KD * P].rearrange("p (k n) -> p k n", k=KD)).then_inc(sem(s + "_hT"), 1)

            @block.tensor
            def _(pe):
                pe.wait_ge(sem("const"), CONST)
                for t in range(T):
                    pe.wait_ge(sem(s + "_h"), t + 1)
                    if t >= 2:
                        pe.wait_ge(sem(s + "_hT"), t - 1)
                    for k in range(KD):
                        mm = pe.transpose(PS[:, 6 + t % 2, k * P:(k + 1) * P], h[:, t, k * P:(k + 1) * P], ident)
                    mm.then_inc(sem(s + "_tr"), 1)

        def add_bias(block, s, bias, wsem, wval):
            @block.gpsimd
            def _(pool):
                pool.wait_ge(sem(s + "_h"), T)
                pool.wait_ge(sem(wsem), wval)
                pool.tensor_tensor(x, x, bias.unsqueeze(1).to_broadcast([P, T, D]), ALU.add).then_inc(sem(s + "_xb"), 1)

        def split_chunks(s, R_parts, u_bufs, source, dest):
            def act_part(act, i):
                if i < 16:
                    ps, bias, ready, val = source(i)
                    act.wait_ge(sem(ready), val)
                    if i >= 3:
                        act.wait_ge(sem(s + "_s3"), i - 2)
                    kw = {} if bias is None else {"bias": bias}
                    act.activation(u_bufs[i % 3], ps, ACT.Identity, **kw).then_inc(sem(s + "_u"), 1)
                    act.activation(dest(i, 0), ps if not isinstance(ps, tuple) else ps[0], ACT.Identity, **kw).then_inc(sem(s + "_s1"), 1)
                if i >= 1 and i - 1 < 16:
                    act.wait_ge(sem(s + "_r1"), i)
                    src = u_bufs[(i - 1) % 3]
                    act.activation(dest(i - 1, 1), src, ACT.Identity).then_inc(sem(s + "_s2"), 1)

            def pool_part(pool, i):
                if i < 16:
                    pool.wait_ge(sem(s + "_s1"), i + 1)
                    pool.tensor_tensor(u_bufs[i % 3], u_bufs[i % 3], dest(i, 0), ALU.subtract).then_inc(sem(s + "_r1"), 1)
                if i >= 1 and i - 1 < 16:
                    pool.wait_ge(sem(s + "_s2"), i)
                    pool.wait_ge(sem(s + "_r1"), i)
                    pool.tensor_tensor(dest(i - 1, 2), u_bufs[(i - 1) % 3], dest(i - 1, 1), ALU.subtract).then_inc(sem(s + "_s3"), 1)

            return act_part, pool_part

        def store_parts(sp, s, l, b, parts):
            sp.wait_ge(sem(s + "_s3"), 8 * (b + 1))
            sp.wait_ge(sem(s + "_s1"), 8 * (b + 1))
            sp.wait_ge(sem(s + "_s2"), 8 * (b + 1))
            for qk in range(2):
                for n in range(NPART):
                    sp.dma_start(parts_dram[l][qk, n, b * D:(b + 1) * D, :].rearrange("(k p) n -> p k n", p=P),
                                 parts[b][:, n, qk * KD:(qk + 1) * KD, :]).then_inc(sem(s + "_parts"), 16)

        PARTS_ST = 16 * 2 * NPART * B

        def qkv0(block):
            s = "q0"
            R.at = work_mark
            parts = [R.bf16(NPART * 4 * S).rearrange("p (n c t) -> p n c t", n=NPART, c=4) for _ in range(B)]
            cb = [R.f32(3 * D) for _ in range(4)]
            sq = [R.f32(3 * D) for _ in range(2)]
            ss = [R.f32(3 * NH) for _ in range(4)]
            ub = [R.f32(BANK) for _ in range(3)]
            vt = [R.f32(NH * SLOT).rearrange("p (h s) -> p h s", h=NH) for _ in range(2)]
            u_bufs = [u.rearrange("p (c n) -> p c n", c=4) for u in ub]

            def source(i):
                return PS[:, 4 + i % 2, :].rearrange("p (c n) -> p c n", c=4), None, s + "_tr", i + 1

            def dest(i, n):
                return parts[i // TB][:, n, :, (i % TB) * P:(i % TB + 1) * P]

            act_split, pool_split = split_chunks(s, parts, u_bufs, source, dest)

            @block.tensor
            def _(pe):
                pe.wait_ge(sem("centre"), 3)
                for i in range(T + 4):
                    if i < T:
                        pe.wait_ge(sem("ln0_hT"), i + 1)
                        if i >= 2:
                            pe.wait_ge(sem(s + "_c"), i - 1)
                        b0 = 2 * (i % 2)
                        for n0, nw in ((0, BANK), (BANK, 3 * D - BANK)):
                            for k in range(KD):
                                mm = pe.matmul(PS[:, b0 + n0 // BANK, 0:nw], hT[:, k, i * P:(i + 1) * P],
                                               w_qkv[0][:, k, n0:n0 + nw], start=(k == 0), stop=(k == KD - 1))
                        mm.then_inc(sem(s + "_ps"), 1)
                    if i >= 4:
                        t = i - 4
                        pe.wait_ge(sem(s + "_n"), t + 1)
                        if t >= 2:
                            pe.wait_ge(sem(s + "_s1"), t - 1)
                        for c in range(4):
                            mm = pe.transpose(PS[:, 4 + t % 2, c * P:(c + 1) * P], cb[t % 4][:, c * P:(c + 1) * P], ident)
                        mm.then_inc(sem(s + "_tr"), 1)

            @block.vector
            def _(dve):
                dve.wait_ge(sem("centre"), 3)
                for i in range(T + 2):
                    if i < T:
                        dve.wait_ge(sem(s + "_ps"), i + 1)
                        if i >= 4:
                            dve.wait_ge(sem(s + "_tr"), i - 3)
                            dve.wait_ge(sem(s + "_v"), i - 3)
                        b0 = 2 * (i % 2)
                        dve.tensor_tensor(cb[i % 4], PS[:, b0:b0 + 2, :].rearrange("p a n -> p (a n)")[:, 0:3 * D],
                                          w_qkv[0][:, 2, :], ALU.add).then_inc(sem(s + "_c"), 1)
                    if 1 <= i <= T:
                        t = i - 1
                        dve.wait_ge(sem(s + "_sq"), t + 1)
                        dve.tensor_reduce(ss[t % 4], sq[t % 2].rearrange("p (h d) -> p h d", d=HD), AX.X,
                                          ALU.add).then_inc(sem(s + "_ss"), 1)
                        dve.wait_ge(sem(s + "_ss"), t + 1)
                        dve.tensor_scalar(ss[t % 4], ss[t % 4], 1.0 / HD, L0_EPS, ALU.mult, ALU.add).then_inc(sem(s + "_var"), 1)
                    if i >= 2:
                        t = i - 2
                        dve.wait_ge(sem(s + "_std"), t + 1)
                        dve.reciprocal(ss[t % 4], ss[t % 4]).then_inc(sem(s + "_rs"), 1)

            @block.scalar
            def _(act):
                for i in range(T):
                    act.wait_ge(sem(s + "_var"), i + 1)
                    act.activation(ss[i % 4], ss[i % 4], ACT.Sqrt).then_inc(sem(s + "_std"), 1)
                    if i >= 4:
                        act_split(act, i - 4)
                for i in range(T - 4, T + 1):
                    act_split(act, i)

            @block.gpsimd
            def _(pool):
                for v in vt:
                    pool.memset(v[:, :, HD:SLOT], 1.0).then_inc(sem(s + "_vpad"), 1)

                def norm(t):
                    c, r = cb[t % 4], ss[t % 4]
                    c48 = c.rearrange("p (h d) -> p h d", d=HD)
                    pool.wait_ge(sem(s + "_rs"), t + 1)
                    pool.tensor_tensor(c48, c48, r.unsqueeze(2).to_broadcast([P, 3 * NH, HD]), ALU.mult).then_inc(sem(s + "_n1"), 1)
                    pool.wait_ge(sem(s + "_n1"), t + 1)
                    c3 = c.rearrange("p (s h d) -> p s h d", s=3, d=HD)
                    pool.tensor_tensor(c3, c3, ln_scale.unsqueeze(2).to_broadcast([P, 3, NH, HD]), ALU.mult).then_inc(sem(s + "_n2"), 1)
                    pool.wait_ge(sem(s + "_n2"), t + 1)
                    pool.tensor_tensor(c3[:, 0:2], c3[:, 0:2], ln_bias[:, 0:2].unsqueeze(2).to_broadcast([P, 2, NH, HD]),
                                       ALU.add).then_inc(sem(s + "_n"), 1)
                    if t >= 2:
                        pool.wait_ge(sem(f"{s}_vst{t % 2}"), 16 * (t // 2))
                    else:
                        pool.wait_ge(sem(s + "_vpad"), 2)
                    pool.tensor_tensor(vt[t % 2][:, :, 0:HD], c3[:, 2], ln_bias[:, 2].unsqueeze(1).to_broadcast([P, NH, HD]),
                                       ALU.add).then_inc(sem(s + "_v"), 1)

                for i in range(T + 5):
                    if i < T:
                        pool.wait_ge(sem(s + "_c"), i + 1)
                        if i >= 2:
                            pool.wait_ge(sem(s + "_ss"), i - 1)
                        pool.tensor_tensor(sq[i % 2], cb[i % 4], cb[i % 4], ALU.mult).then_inc(sem(s + "_sq"), 1)
                    if 2 <= i < T + 2:
                        norm(i - 2)
                    if i >= 4:
                        pool_split(pool, i - 4)

            @block.sync
            def _(sp):
                for t in range(T):
                    sp.wait_ge(sem(s + "_v"), t + 1)
                    b = t // TB
                    sp.dma_start(v_dram[0][b * NG:(b + 1) * NG, :, t % TB, :].rearrange("g p n -> p g n"),
                                 vt[t % 2].rearrange("p (g j) s -> p g (j s)", g=NG)).then_inc(sem(f"{s}_vst{t % 2}"), 16)
                    if t == TB + 5:
                        store_parts(sp, s, 0, 0, parts)
                store_parts(sp, s, 0, 1, parts)

        def qkv1(block):
            s = "q1"
            R.at = work_mark
            parts = [R.bf16(NPART * 4 * S).rearrange("p (n c t) -> p n c t", n=NPART, c=4) for _ in range(B)]
            u_bufs = [R.f32(BANK) for _ in range(3)]
            vt = [R.f32(NH * SLOT).rearrange("p (h s) -> p h s", h=NH) for _ in range(2)]

            def where(i):
                b, m, half = i // 8, (i % 8) // 2, i % 2
                return b, m, half

            def source(i):
                b, m, half = where(i)
                return PS[:, 4 + i % 2, :], b_qk1[:, m:m + 1], s + "_ps", i + 1

            def dest(i, n):
                b, m, half = where(i)
                return parts[b][:, n, m, half * BANK:(half + 1) * BANK]

            act_split, pool_split = split_chunks(s, parts, u_bufs, source, dest)

            @block.tensor
            def _(pe):
                pe.wait_ge(sem("w_in"), W_IN)
                pe.wait_ge(sem("ln3_hT"), T)
                for i in range(16):
                    b, m, half = where(i)
                    if i >= 2:
                        pe.wait_ge(sem(s + "_s1"), i - 1)
                    for k in range(KD):
                        mm = pe.matmul(PS[:, 4 + i % 2, :], w_qkv[1][:, k, m * P:(m + 1) * P],
                                       hT[:, k, b * S + half * BANK:b * S + (half + 1) * BANK],
                                       start=(k == 0), stop=(k == KD - 1))
                    mm.then_inc(sem(s + "_ps"), 1)
                    if i >= 2:
                        pe.wait_ge(sem(s + "_v"), i - 1)
                    for k in range(KD):
                        mm = pe.matmul(PS[:, i % 2, 0:D], hT[:, k, i * P:(i + 1) * P], w_qkv[1][:, k, 2 * D:3 * D],
                                       start=(k == 0), stop=(k == KD - 1))
                    mm.then_inc(sem(s + "_vps"), 1)

            @block.scalar
            def _(act):
                act.wait_ge(sem("w_in"), W_IN)
                for i in range(17):
                    act_split(act, i)

            @block.gpsimd
            def _(pool):
                pool.wait_ge(sem("e0_x"), T)
                for v in vt:
                    pool.memset(v[:, :, HD:SLOT], 1.0).then_inc(sem(s + "_vpad"), 1)
                for i in range(17):
                    pool_split(pool, i)

            @block.vector
            def _(dve):
                dve.wait_ge(sem("w_in"), W_IN)
                for t in range(T):
                    dve.wait_ge(sem(s + "_vps"), t + 1)
                    if t >= 2:
                        dve.wait_ge(sem(f"{s}_vst{t % 2}"), 16 * (t // 2))
                    else:
                        dve.wait_ge(sem(s + "_vpad"), 2)
                    dve.tensor_tensor(vt[t % 2][:, :, 0:HD], PS[:, t % 2, 0:D].rearrange("p (h d) -> p h d", d=HD),
                                      w_qkv[1][:, 2, 2 * D:3 * D].rearrange("p (h d) -> p h d", d=HD),
                                      ALU.add).then_inc(sem(s + "_v"), 1)

            @block.sync
            def _(sp):
                for t in range(T):
                    sp.wait_ge(sem(s + "_v"), t + 1)
                    b = t // TB
                    sp.dma_start(v_dram[1][b * NG:(b + 1) * NG, :, t % TB, :].rearrange("g p n -> p g n"),
                                 vt[t % 2].rearrange("p (g j) s -> p g (j s)", g=NG)).then_inc(sem(f"{s}_vst{t % 2}"), 16)
                for b in range(B):
                    store_parts(sp, s, 1, b, parts)

        def attention(block, l, causal):
            s, q = f"a{l}", f"q{l}"
            R.at = work_mark
            qst = [R.bf16(G * S).rearrange("p (j t) -> p j t", j=G) for _ in range(NST)]
            kst = [R.bf16(G * S).rearrange("p (j t) -> p j t", j=G) for _ in range(NST)]
            spare = hT.rearrange("p k n -> p (k n)")
            VW = TB * G * SLOT
            vst = [spare[:, r * VW:(r + 1) * VW].rearrange("p (t j s) -> p t j s", t=TB, j=G) for r in range(NST)]
            prob = [R.f32(S) for _ in range(PR)]
            osb = spare[:, NST * VW:NST * VW + S]
            m2 = R.f32(G * TB * 2).rearrange("p (j t a) -> p j t a", j=G, a=2)
            mx = R.f32(G * TB).rearrange("p (j t) -> p j t", j=G)
            mh = R.bf16(2 * G * TB)
            mhl = mh.rearrange("p (c j t) -> p c j t", c=2, j=G)
            mT = R.bf16(P)
            head_fills = fills(causal)
            unit_fills = [(j, *f) for j in range(G) for f in head_fills]
            NF = len(unit_fills)
            RING = NF + 2
            STEPS = G * TB
            score = [PS[:, 2:4, :].rearrange("p a n -> p (a n)"), PS[:, 4:6, :].rearrange("p a n -> p (a n)")]
            opsum = PS[:, 6:8, :].rearrange("p a n -> p (a n)")
            assert RING % 2 == 0

            def load(sp, u, r, n):
                if not (isinstance(n, int) and n == 0):
                    sp.wait_ge(sem(s + "_pv"), (u - NST) * TB + TB)
                for slot in range(NSLOT):
                    for st, qk, part in ((qst, 0, QUERY_PARTS[slot]), (kst, 1, KEY_PARTS[slot])):
                        sp.dma_start(st[r][slot * HD:(slot + 1) * HD],
                                     parts_dram[l][qk, part].rearrange("(u j d) t -> u d j t", j=G, d=HD)[u]
                                     ).then_inc(sem(f"{s}_in{r}"), 16)
                sp.dma_start(vst[r].rearrange("p t j s -> p (t j s)"),
                             v_dram[l].rearrange("u p t n -> u p (t n)")[u]).then_inc(sem(f"{s}_in{r}"), 16)

            IN = 16 * (2 * NSLOT + 1)

            def store_maxima(sp, u, r):
                sp.wait_ge(sem(s + "_mT"), u + 1)
                sp.dma_start(qst[r][KS:KM], mT[0:2 * G * TB]).then_inc(sem(s + "_rows"), 16)

            def store_out(sp, u):
                sp.wait_ge(sem(s + "_o"), u + 1)
                for j in range(G):
                    sp.dma_start(o_dram[l].rearrange("(u j d) t -> u j d t", j=G, d=HD)[u, j],
                                 osb[SLOT * j:SLOT * j + HD]).then_inc(sem(s + "_ost"), 16)
                    sp.dma_start(sum_dram[l].rearrange("(u j a) t -> u j (a t)", u=NU, j=G)[u, j:j + 1],
                                 osb[SLOT * j + HD:SLOT * j + HD + 1]).then_inc(sem(s + "_ost"), 16)

            @block.sync
            def _(sp):
                sp.wait_ge(sem(q + "_parts"), PARTS_ST)
                for r in range(2):
                    sp.wait_ge(sem(f"{q}_vst{r}"), 16 * T // 2)
                for u in range(NST):
                    load(sp, u, u, 0)
                sp.wait_ge(sem(s + "_ones"), NST)
                store_maxima(sp, 0, 0)

                def unit(u, r, last=False, loads=True):
                    if not last:
                        store_maxima(sp, u + 1, (r + 1) % NST)
                    store_out(sp, u)
                    if loads:
                        load(sp, u + NST, r, 1)

                with sp.Fori(0, 1) as i:
                    for r in range(NST):
                        unit(i * NST + r, r)
                unit(3, 0)
                unit(4, 1)
                unit(5, 2, loads=False)
                unit(6, 0, loads=False)
                unit(7, 1, last=True, loads=False)

            def pass1(pe, u, r, f):
                n = u * RING + f
                if not (isinstance(u, int) and u == 0 and f < 2):
                    pe.wait_ge(sem(s + "_red"), n - 1)
                if f < NF:
                    j, i, kb, w = unit_fills[f]
                    diag = causal and kb == i * P // BANK
                    mm = pe.matmul(PS[:, f % 2, 0:w], qst[r][0:KS, j, i * P:(i + 1) * P],
                                   kst[r][0:KS, j, kb * BANK:kb * BANK + w], start=True, stop=not diag)
                    if diag:
                        mm = pe.matmul(PS[:, f % 2, w - P:w], identb, future, start=False, stop=True)
                elif f == NF:
                    pe.wait_ge(sem(s + "_mh"), u + 1)
                    mm = pe.transpose(PS[0:2 * G * TB, 0, 0:P // 2].bitcast(BF16), mh, identb)
                mm.then_inc(sem(s + "_fill"), 1)

            def pass2(pe, u, r, st):
                kt, j = st // G, st % G
                n = u * STEPS + st
                if not (isinstance(u, int) and u == 0 and st < 2):
                    pe.wait_ge(sem(s + "_exp"), n - 1)
                lo = kt * P if causal else 0
                for bank in range(2):
                    c0, c1 = max(lo, bank * BANK), (bank + 1) * BANK
                    if c0 >= c1:
                        continue
                    diag = causal and c0 == lo
                    mm = pe.matmul(score[st % 2][:, c0:c1], kst[r][0:KM, j, kt * P:(kt + 1) * P],
                                   qst[r][0:KM, j, c0:c1], start=True, stop=not diag)
                    if diag:
                        mm = pe.matmul(score[st % 2][:, lo:lo + P], identb, futureT, start=False, stop=True)
                mm.then_inc(sem(s + "_sc"), 1)

            def pv(pe, u, r, kt):
                pe.wait_ge(sem(s + "_exp"), u * STEPS + (kt + 1) * G)
                if kt == 0 and not (isinstance(u, int) and u == 0):
                    pe.wait_ge(sem(s + "_o"), u)
                lo = kt * P if causal else 0
                for bank in range(2):
                    c0, c1 = max(lo, bank * BANK), (bank + 1) * BANK
                    if c0 >= c1:
                        continue
                    lastk = TB - 1 if not causal or bank == 1 else BANK // P - 1
                    for j in range(G):
                        mm = pe.matmul(opsum[SLOT * j:SLOT * (j + 1), c0:c1], vst[r][:, kt, j, :],
                                       prob[(kt * G + j) % PR][:, c0:c1], start=(kt == 0), stop=(kt == lastk))
                mm.then_inc(sem(s + "_pv"), 1)

            @block.tensor
            def _(pe):
                pe.wait_ge(sem("const"), CONST)
                pe.wait_ge(sem(s + "_in0"), IN)
                for f in range(RING - 1):
                    pass1(pe, 0, 0, f)
                pe.nop().then_inc(sem(s + "_fill"), 1)

                def unit(u, r, n, n1, last=False):
                    pe.wait_ge(sem(s + "_rows"), (u + 1) * 16)
                    if not last:
                        pe.wait_ge(sem(f"{s}_in{(r + 1) % NST}"), n1)
                    f, DONE = 0, STEPS - 5
                    for st in range(STEPS):
                        upto = min(NF, (st + 1) * NF // DONE + 1)
                        while not last and f < upto:
                            pass1(pe, u + 1, (r + 1) % NST, f)
                            f += 1
                        pass2(pe, u, r, st)
                        if st % G == 1 and st > G:
                            pv(pe, u, r, st // G - 1)
                        if not last and st == STEPS - 3:
                            pass1(pe, u + 1, (r + 1) % NST, NF)
                            pe.nop().then_inc(sem(s + "_fill"), 1)
                    pv(pe, u, r, TB - 1)

                with pe.Fori(0, 1) as i:
                    for r in range(NST):
                        unit(i * NST + r, r, None, IN * (i + 1 if r < NST - 1 else i + 2))
                unit(3, 0, None, IN * 2)
                unit(4, 1, None, IN * 2)
                unit(5, 2, None, IN * 3)
                unit(6, 0, None, IN * 3)
                unit(7, 1, None, None, last=True)

            @block.scalar
            def _(act):
                def unit(u):
                    for st in range(STEPS):
                        kt = st // G
                        n = u * STEPS + st
                        act.wait_ge(sem(s + "_sc"), n + 1)
                        first = isinstance(u, int) and u == 0
                        if not (first and kt < 2):
                            act.wait_ge(sem(s + "_pv"), u * TB + kt - 1)
                        lo = kt * P if causal else 0
                        act.activation(prob[st % PR][:, lo:S], score[st % 2][:, lo:S], ACT.Exp,
                                       scale=SCALE).then_inc(sem(s + "_exp"), 1)

                unit(0)
                with act.Fori(1, NU) as u:
                    unit(u)

            @block.vector
            def _(dve):
                dve.wait_ge(sem(q + "_parts"), PARTS_ST)
                for r in range(2):
                    dve.wait_ge(sem(f"{q}_vst{r}"), 16 * T // 2)
                for r in range(NST):
                    for st in (kst, ):
                        dve.memset(st[r][KS:KM].rearrange("p j t -> p (j t)"), 1.0).then_inc(sem(s + "_ones"), 1)
                dve.memset(m2.rearrange("p j t a -> p (j t a)"), LOWEST).then_inc(sem(s + "_m2"), 1)
                dve.wait_ge(sem(s + "_m2"), 1)

                def maxima(u):
                    for f in range(NF):
                        j, i, kb, w = unit_fills[f]
                        dve.wait_ge(sem(s + "_fill"), u * RING + f + 1)
                        dve.tensor_reduce(m2[:, j, i, kb:kb + 1], PS[:, f % 2, 0:w], AX.X, ALU.max).then_inc(sem(s + "_red"), 1)
                    dve.wait_ge(sem(s + "_red"), u * RING + NF)
                    dve.tensor_tensor(mx, m2[:, :, :, 0], m2[:, :, :, 1], ALU.max).then_inc(sem(s + "_mx"), 1)
                    dve.wait_ge(sem(s + "_mx"), u + 1)
                    dve.tensor_scalar(mhl[:, 0], mx, -1.0, None, ALU.mult).then_inc(sem(s + "_mhi"), 1)
                    dve.wait_ge(sem(s + "_mhi"), u + 1)
                    dve.scalar_tensor_tensor(out=mhl[:, 1], in0=mx, scalar=-1.0, in1=mhl[:, 0], op0=ALU.mult,
                                             op1=ALU.subtract).then_inc(sem(s + "_mh"), 1)
                    dve.wait_ge(sem(s + "_fill"), u * RING + NF + 2)
                    if not (isinstance(u, int) and u == 0):
                        dve.wait_ge(sem(s + "_rows"), 16 * u)
                    dve.tensor_copy(mT[0:2 * G * TB], PS[0:2 * G * TB, 0, 0:P // 2].bitcast(BF16)).then_inc(sem(s + "_mT"), 1)
                    dve.wait_ge(sem(s + "_mT"), u + 1)
                    dve.nop().then_inc(sem(s + "_red"), 2)

                def evacuate(u):
                    dve.wait_ge(sem(s + "_pv"), (u + 1) * TB)
                    if not (isinstance(u, int) and u == 0):
                        dve.wait_ge(sem(s + "_ost"), u * 16 * 2 * G)
                    dve.tensor_copy(osb, opsum).then_inc(sem(s + "_o"), 1)

                maxima(0)
                maxima(1)
                evacuate(0)
                with dve.Fori(1, NU - 1) as u:
                    maxima(u + 1)
                    evacuate(u)
                evacuate(NU - 1)

        def project(block, l):
            s, at, lns = f"p{l}", f"a{l}", ("ln0", "ln3")[l]
            R.at = work_mark
            sm = R.f32(B * P).rearrange("p (b t) -> p b t", b=B)
            OT = R.f32(B * KD * S).rearrange("p (c t) -> p c t", c=B * KD)
            RB = R.f32(B * KD * S).rearrange("p (c t) -> p c t", c=B * KD)

            @block.sync
            def _(sp):
                sp.wait_ge(sem(at + "_ost"), NU * 16 * 2 * G)
                sp.wait_ge(sem(at + "_pv"), NU * TB)
                sp.dma_start(sm, sum_dram[l].rearrange("(b p) t -> p b t", p=P)).then_inc(sem(s + "_sm"), 16)
                sp.dma_start(OT, o_dram[l].rearrange("(c p) t -> p c t", p=P)).then_inc(sem(s + "_ot"), 16)
                sp.wait_ge(sem(s + "_rec"), 1)
                sp.dma_start(rec_dram[l].rearrange("(b h) (a t) -> (b h a) t", b=B, a=8).rearrange("(b p) t -> p b t", p=P),
                             sm).then_inc(sem(s + "_recst"), 16)
                sp.wait_ge(sem(s + "_recst"), 16)
                for c in range(B * KD):
                    for j in range(8):
                        sp.dma_start(RB[j * HD:(j + 1) * HD, c, :],
                                     rec_dram[l][c * 8 + j, :].partition_broadcast(HD)).then_inc(sem(f"{s}_rb{c}"), 16)

            @block.vector
            def _(dve):
                dve.wait_ge(sem(s + "_sm"), 16)
                dve.reciprocal(sm, sm).then_inc(sem(s + "_rec"), 1)
                dve.wait_ge(sem(s + "_ot"), 16)
                for c in range(B * KD):
                    dve.wait_ge(sem(f"{s}_rb{c}"), 16 * 8)
                    dve.tensor_tensor(OT[:, c, :], OT[:, c, :], RB[:, c, :], ALU.mult).then_inc(sem(s + "_on"), 1)
                dve.wait_ge(sem(lns + "_xb"), 1)
                for t in range(T):
                    dve.wait_ge(sem(s + "_y"), t + 1)
                    dve.tensor_tensor(x[:, t, :], x[:, t, :], PS[:, t % 2, 0:D], ALU.add).then_inc(sem(s + "_x"), 1)

            @block.tensor
            def _(pe):
                for t in range(T):
                    b = t // TB
                    pe.wait_ge(sem(s + "_on"), (b + 1) * KD)
                    if t >= 2:
                        pe.wait_ge(sem(s + "_x"), t - 1)
                    if t == 0:
                        pe.wait_ge(sem("w_in"), W_IN)
                    for k in range(KD):
                        mm = pe.matmul(PS[:, t % 2, 0:D], OT[:, b * KD + k, (t % TB) * P:(t % TB + 1) * P],
                                       w_out[l][:, k, :], start=(k == 0), stop=(k == KD - 1))
                    mm.then_inc(sem(s + "_y"), 1)

        def cross(block, l, top):
            s, lns = f"x{l}", ("ln1", "ln4")[l]
            R.at = work_mark
            HC = 4 * C
            cell = R.f32(1)
            qt = [R.f32(KD * P).rearrange("p (k n) -> p k n", k=KD) for _ in range(2)]
            sc = [R.f32(NH * C).rearrange("p (h c) -> p h c", h=NH) for _ in range(2)]
            left = [R.f32(NH * C).rearrange("p (h c) -> p h c", h=NH) for _ in range(2)]
            ex = [R.f32(NH * C).rearrange("p (h c) -> p h c", h=NH) for _ in range(2)]
            m8 = [R.f32(NH * 8 * 4).rearrange("p (r h e) -> p r h e", r=4, h=NH) for _ in range(2)]
            rs = [R.f32(NH) for _ in range(2)]
            wT = [R.f32(NH * P).rearrange("p (h n) -> p h n", h=NH) for _ in range(2)]
            ot = [R.f32(NG * P).rearrange("p (g n) -> p g n", g=NG) for _ in range(2)]
            wo = xwo if l == 0 else pick
            if l == 1:
                z_dram = scratch("z", [B, NH, TB, P, HD])
                zb = [R.f32(D) for _ in range(2)]
                z = R.f32(T * D).rearrange("p (t d) -> p t d", t=T)
            WITH = 1 if top else 0

            def each(body):
                def run(eng, b):
                    if b == 0:
                        body(eng, 0, 0, 0, 0, 0)
                        body(eng, 0, 1, 1, 1, 0)
                        with eng.Fori(1, TB // 2) as i:
                            body(eng, 0, i * 2, 0, 2, i)
                            body(eng, 0, i * 2 + 1, 1, 3, i)
                    else:
                        with eng.Fori(TB // 2, TB) as i:
                            body(eng, 1, i * 2, 0, 2, i)
                            body(eng, 1, i * 2 + 1, 1, 3, i)
                return run

            def cols(t):
                return slice(t * P, (t + 1) * P) if isinstance(t, int) else bass.ds(t * P, P)

            def pe_front(pe, b, t, r, used):
                if used:
                    pe.wait_ge(sem(s + "_y"), t)
                    if used > 0:
                        pe.wait_ge(sem(s + "_xd"), t)
                for half in range(KD):
                    for k in range(KD):
                        mm = pe.matmul(PS[:, 6, half * P:(half + 1) * P], xwqT[l][:, k, half * P:(half + 1) * P],
                                       hT[:, k, cols(t)], start=(k == 0), stop=(k == KD - 1))
                mm.then_inc(sem(s + "_q"), 1)
                pe.wait_ge(sem(s + "_qt"), t * KD + KD)
                if used:
                    pe.wait_ge(sem(s + "_scout"), t)
                for c in range(4):
                    kb = kblk[l][:, b, c // 2, (c % 2) * 4:(c % 2) * 4 + 4, :]
                    mm = pe.matmul(PS[:, c, 0:HC], qt[r][:, c // 2, :], kb.rearrange("p j c -> p (j c)"),
                                   start=True, stop=True)
                mm.then_inc(sem(s + "_s"), 1)

            def pe_back(pe, b, t, r, used):
                pe.wait_ge(sem(s + "_w"), t + 1)
                for c in range(4):
                    if used or c >= 2:
                        pe.wait_ge(sem(s + "_wt"), t * 4 + c - 1)
                    for j in range(4):
                        mm = pe.transpose(PS[0:C, 4 + c % 2, j * P:(j + 1) * P], ex[r][:, c * 4 + j, :], ident)
                    mm.then_inc(sem(s + "_wtp"), 1)
                pe.wait_ge(sem(s + "_wt"), t * 4 + 4)
                if used:
                    pe.wait_ge(sem(s + "_ot"), t)
                for g in range(NG):
                    for j in range(G):
                        mm = pe.matmul(PS[SLOT * j:SLOT * (j + 1), 7, g * P:(g + 1) * P], xv[l][0:C, b, g * G + j, :],
                                       wT[r][0:C, g * G + j, :], start=True, stop=True)
                mm.then_inc(sem(s + "_op"), 1)
                pe.wait_ge(sem(s + "_ot"), t + 1)
                for g in range(NG):
                    mm = pe.matmul(PS[:, 6, 0:D], ot[r][:, g, :], wo[:, g, :], start=(g == 0), stop=(g == NG - 1))
                mm.then_inc(sem(s + "_y"), 1)

            @block.tensor
            def _(pe):
                pe.wait_ge(sem(lns + "_hT"), T)
                pe.wait_ge(sem("kblk"), 4 * B)
                pe.wait_ge(sem("xv"), 2 * B)
                pe.wait_ge(sem("xwo"), 16 * G)

                def body(eng, b, t, r, used, n):
                    pe_front(eng, b, t, r, used)
                    pe_back(eng, b, t, r, used)

                run = each(body)
                for b in range(B):
                    run(pe, b)

            @block.scalar
            def _(act):
                def body(act, b, t, r, used, n):
                    act.wait_ge(sem(s + "_q"), t + 1)
                    for half in range(KD):
                        act.activation(qt[r][:, half, :], PS[:, 6, half * P:(half + 1) * P], ACT.Identity,
                                       bias=xq_b[l][:, half:half + 1]).then_inc(sem(s + "_qt"), 1)
                    if top:
                        act.wait_ge(sem(s + "_s"), t + 1)
                        if used > 1:
                            act.wait_ge(sem(s + "_d"), t - 1)
                            act.wait_ge(sem(s + "_topped"), (t - 1) * NH)
                        act.copy(sc[r].rearrange("p (c j) k -> p c (j k)", c=4), PS[:, 0:4, 0:HC]).then_inc(sem(s + "_scout"), 1)
                    act.wait_ge(sem(s + "_d"), t + 1)
                    act.activation(ex[r], ex[r], ACT.Exp, scale=SCALE if top else 1.0).then_inc(sem(s + "_e"), 1)
                    for c in range(4):
                        act.wait_ge(sem(s + "_wtp"), t * 4 + c + 1)
                        act.copy(wT[r][0:C, c * 4:c * 4 + 4, :], PS[0:C, 4 + c % 2, :].rearrange("p (j n) -> p j n", j=4)
                                 ).then_inc(sem(s + "_wt"), 1)
                run = each(body)
                for b in range(B):
                    run(act, b)

            @block.gpsimd
            def _(pool):
                def body(pool, b, t, r, used, n):
                    pool.wait_ge(sem(s + "_m"), (t + 1) * (NH if top else 1))
                    if top:
                        pool.wait_ge(sem(s + "_scout"), t + 1)
                    if used > 1:
                        pool.wait_ge(sem(s + "_wtp"), (t - 1) * 4)
                    src = m8[r][:, 0, :, 0:1]
                    pool.tensor_tensor(ex[r], sc[r], src.to_broadcast([P, NH, C]), ALU.subtract).then_inc(sem(s + "_d"), 1)
                    if top:
                        pool.wait_ge(sem(s + "_rs"), t + 1)
                        pool.tensor_tensor(ex[r], ex[r], rs[r].unsqueeze(2).to_broadcast([P, NH, C]), ALU.mult).then_inc(sem(s + "_w"), 1)
                run = each(body)
                for b in range(B):
                    run(pool, b)

            @block.vector
            def _(dve):
                if l == 0:
                    dve.wait_ge(sem("ln1_xb"), 1)

                def back(dve, t, r, used, n):
                    dve.wait_ge(sem(s + "_op"), t + 1)
                    dve.tensor_copy(ot[r], PS[:, 7, :].rearrange("p (g n) -> p g n", g=NG)).then_inc(sem(s + "_ot"), 1)
                    dve.wait_ge(sem(s + "_y"), t + 1)
                    if l == 0:
                        row = x[:, t, :] if isinstance(t, int) else x[:, bass.ds(t, 1), :].rearrange("p a d -> p (a d)")
                        dve.tensor_tensor(row, row, PS[:, 6, 0:D], ALU.add).then_inc(sem(s + "_xd"), 1)
                    else:
                        if used > 1:
                            dve.wait_ge(sem(f"{s}_zst{r}"), 16 * n)
                        dve.tensor_copy(zb[r], PS[:, 6, 0:D]).then_inc(sem(s + "_xd"), 1)

                def body(dve, b, t, r, used, n):
                    hn = t * NH
                    if top:
                        dve.wait_ge(sem(s + "_scout"), t + 1)
                        if used > 1:
                            dve.wait_ge(sem(s + "_d"), t - 1)
                        dve.memset(cell, 0.0)
                        for k in range(4):
                            if k:
                                dve.wait_ge(sem(f"{s}_k{k - 1}"), hn + NH)
                                dve.memset(cell, 0.0)
                            for hd in range(NH):
                                src = (sc if k == 0 else left)[r][:, hd, :]
                                dve.max(m8[r][:, k, hd, :], src).then_inc(sem(s + "_m" if k == 0 else f"{s}_m{k}"), 1)
                            dve.wait_ge(sem(s + "_m" if k == 0 else f"{s}_m{k}"), hn + NH)
                            dve.memset(cell, 0.0)
                            for hd in range(NH):
                                src = (sc if k == 0 else left)[r][:, hd, :]
                                dve.match_replace(out=left[r][:, hd, :], in_to_replace=m8[r][:, k, hd, :], in_values=src,
                                                  imm_value=LOWEST).then_inc(sem(f"{s}_k{k}" if k < 3 else s + "_topped"), 1)
                        dve.wait_ge(sem(s + "_topped"), hn + NH)
                        dve.wait_ge(sem(s + "_e"), t + 1)
                        dve.scalar_tensor_tensor(out=ex[r], in0=left[r], scalar=LOWEST, in1=ex[r], op0=ALU.is_equal,
                                                 op1=ALU.mult).then_inc(sem(s + "_sel"), 1)
                        dve.wait_ge(sem(s + "_sel"), t + 1)
                    else:
                        dve.wait_ge(sem(s + "_s"), t + 1)
                        if used > 1:
                            dve.wait_ge(sem(s + "_d"), t - 1)
                        dve.tensor_scalar(sc[r].rearrange("p (c j) k -> p c (j k)", c=4), PS[:, 0:4, 0:HC], -3.4028234e38, None,
                                          ALU.max).then_inc(sem(s + "_scout"), 1)
                        dve.wait_ge(sem(s + "_scout"), t + 1)
                        dve.tensor_reduce(m8[r][:, 0, :, 0], sc[r], AX.X, ALU.max).then_inc(sem(s + "_m"), 1)
                        dve.wait_ge(sem(s + "_e"), t + 1)
                    dve.tensor_reduce(rs[r], ex[r], AX.X, ALU.add).then_inc(sem(s + "_sum"), 1)
                    dve.wait_ge(sem(s + "_sum"), t + 1)
                    dve.reciprocal(rs[r], rs[r]).then_inc(sem(s + "_rs"), 1)
                    if not top:
                        dve.wait_ge(sem(s + "_rs"), t + 1)
                        dve.tensor_tensor(ex[r], ex[r], rs[r].unsqueeze(2).to_broadcast([P, NH, C]), ALU.mult).then_inc(sem(s + "_nrm"), 1)
                        dve.wait_ge(sem(s + "_nrm"), t + 1)
                        dve.tensor_scalar(ex[r], ex[r], 0.0, None, ALU.max).then_inc(sem(s + "_w"), 1)
                    back(dve, t, r, used, t // 2 if isinstance(t, int) else n)
                run = each(body)
                for b in range(B):
                    run(dve, b)

            if l == 1:
                @block.sync
                def _(sp):
                    def body(sp, b, t, r, used, n):
                        sp.wait_ge(sem(s + "_xd"), t + 1)
                        sp.dma_start(z_dram[b].rearrange("h t p d -> t p h d")[t - b * TB],
                                     zb[r].rearrange("p (h d) -> p h d", h=NH)).then_inc(sem(f"{s}_zst{r}"), 16)
                    run = each(body)
                    for b in range(B):
                        run(sp, b)
                        for r in range(2):
                            sp.wait_ge(sem(f"{s}_zst{r}"), 16 * (b + 1) * TB // 2)
                        sp.dma_start(z[:, b * TB:(b + 1) * TB, :],
                                     z_dram[b].rearrange("h t p d -> (h t p d)").rearrange("(t p d) -> p t d", t=TB, p=P)
                                     ).then_inc(sem(f"{s}_z{b}"), 16)

                @block.vector
                def _(dve):
                    for b in range(B):
                        dve.wait_ge(sem(f"{s}_z{b}"), 16)
                        for t in range(b * TB, (b + 1) * TB):
                            dve.tensor_tensor(h[:, t, :], h[:, t, :], z[:, t, :], ALU.add).then_inc(sem(s + "_hz"), 1)
                    dve.wait_ge(sem(s + "_hz"), T)
                    for t in range(T):
                        dve.bn_stats(stats[:, t, :], h[:, t, :]).then_inc(sem(s + "_st2"), 1)
                    for t in range(T):
                        dve.wait_ge(sem(s + "_st2"), t + 1)
                        dve.bn_aggr(mv[:, t, :], stats[:, t, :]).then_inc(sem(s + "_mv2"), 1)
                    dve.wait_ge(sem(s + "_mv2"), T)
                    dve.tensor_scalar(std, mv[:, :, 1], LN_EPS, None, ALU.add).then_inc(sem(s + "_var2"), 1)
                    dve.wait_ge(sem(s + "_std2"), 1)
                    dve.reciprocal(rstd, std).then_inc(sem(s + "_rstd2"), 1)
                    dve.wait_ge(sem(s + "_rstd2"), 1)
                    for t in range(T):
                        dve.tensor_scalar(h[:, t, :], h[:, t, :], mv[:, t, 0:1], rstd[:, t:t + 1], ALU.subtract,
                                          ALU.mult).then_inc(sem(s + "_n2"), 1)
                    for t in range(T):
                        dve.wait_ge(sem(s + "_gb"), t + 1)
                        dve.tensor_tensor(x[:, t, :], x[:, t, :], h[:, t, :], ALU.add).then_inc(sem(s + "_x2"), 1)

                @block.scalar
                def _(act):
                    act.wait_ge(sem(s + "_var2"), 1)
                    act.activation(std, std, ACT.Sqrt).then_inc(sem(s + "_std2"), 1)

                @block.gpsimd
                def _(pool):
                    for t in range(T):
                        pool.wait_ge(sem(s + "_n2"), t + 1)
                        pool.tensor_tensor(h[:, t, :], h[:, t, :], gamma, ALU.mult).then_inc(sem(s + "_g2"), 1)
                        pool.wait_ge(sem(s + "_g2"), t + 1)
                        pool.tensor_tensor(h[:, t, :], h[:, t, :], beta, ALU.add).then_inc(sem(s + "_gb"), 1)

        def moe(block, l, free_sem, free_val):
            s, lns = f"e{l}", ("ln2", "ln5")[l]
            big = l == 1
            R.at = base_mark if big else work_mark
            wr = R.f32(KD * E).rearrange("p (k e) -> p k e", k=KD)
            br = R.f32(E)
            lg = R.f32(T * E).rearrange("p (t e) -> p t e", t=T)
            oh = R.f32(T * E).rearrange("p (t e) -> p t e", t=T)
            ohb = R.bf16(T * E).rearrange("p (t e) -> p t e", t=T)
            ta = R.f32(T * E).rearrange("p (t e) -> p t e", t=T)
            tb = R.f32(T * E).rearrange("p (t e) -> p t e", t=T)
            tot = R.f32(T * E).rearrange("p (t e) -> p t e", t=T)
            c1, c2, c3 = R.f32(E), R.f32(E), R.f32(E)
            nt = R.f32(E)
            cmp1 = R.f32(24 * T).rearrange("p (e j) -> p e j", e=24)
            m1, gate, posf = R.f32(T), R.f32(T), R.f32(T)
            posi = R.f32(T).bitcast(I32)
            eidf = R.f32(24)
            eid = R.f32(24).bitcast(I32)
            NB1 = E * F if big else E * D
            bias_raw = R.f32(NB1 // P)
            bias_part = [R.bf16(NB1 // P) for _ in range(NPART)]
            bias2_raw = R.f32(E * D // P)
            bias2_part = [R.bf16(E * D // P) for _ in range(NPART)]
            b1 = hT.rearrange("p k n -> p (k n)").bitcast(BF16)[0:NPART, 0:NB1]
            b2 = R.bf16(E * D)[0:NPART]
            yb = [R.f32(D) for _ in range(2)]
            NY = 4
            yg = [R.f32(D) for _ in range(NY)]
            H = Region(h.rearrange("p t d -> p (t d)"), T * D)
            xs = [H.f32(D) for _ in range(2)]
            xsT = [H.f32(KD * P).rearrange("p (k n) -> p k n", k=KD) for _ in range(2)]
            if big:
                h1 = [H.f32(F) for _ in range(1)]
                h1T = [H.f32(F).rearrange("p (k n) -> p k n", k=KF) for _ in range(1)]
                W1 = R.f32(E * KD * F)
                W2 = R.f32(E * KF * D)
            else:
                raw = R.f32(E * KD * D).rearrange("p (e k n) -> p e k n", e=E, k=KD)
                WeT = R.f32(E * KD * D)
                wr_raw = R.f32(D)
            bias_names = (("L1_ffn_b1", bias_raw, bias_part, b1, NB1), ("L1_ffn_b2", bias2_raw, bias2_part, b2, E * D)) \
                if big else (("L0_ffn_expert_b", bias_raw, bias_part, b1, NB1),)
            bias_rows = [scratch(f"bias{l}{i}", [NPART, n], BF16) for i, (_, _, _, _, n) in enumerate(bias_names)]

            @block.sync
            def _(sp):
                sp.wait_ge(sem(free_sem), free_val)

                def load(dst, src):
                    sp.dma_start(dst, src).then_inc(sem(s + "_win"), 16)
                for name, raw_b, _, _, n in bias_names:
                    load(raw_b, a[name].rearrange("(o e) f -> o (e f)", o=1).rearrange("o (p n) -> p (o n)", p=P))
                if big:
                    load(wr, a["L1_ffn_Wr"].rearrange("(k p) e -> p k e", p=P))
                    load(br, a["L1_ffn_br"].partition_broadcast(P))
                    for e in range(E):
                        sp.dma_start(W1[:, e * KD * F:(e + 1) * KD * F].rearrange("p (k f) -> p k f", k=KD),
                                     a["L1_ffn_W1"][e].rearrange("(k p) f -> p k f", p=P)).then_inc(sem(s + "_wbig"), 16)
                        sp.dma_start(W2[:, e * KF * D:(e + 1) * KF * D].rearrange("p (k f) -> p k f", k=KF),
                                     a["L1_ffn_W2"][e].rearrange("(k p) f -> p k f", p=P)).then_inc(sem(s + "_wbig"), 16)
                else:
                    load(wr_raw[0:E], a["L0_ffn_router_w"])
                    load(br, a["L0_ffn_router_b"].partition_broadcast(P))
                    for e in range(E):
                        load(raw[:, e], a["L0_ffn_expert_w"][e].rearrange("(k p) n -> p k n", p=P))
                sp.wait_ge(sem(s + "_bparts"), len(bias_names) * NPART)
                for (_, _, parts, _, n), rows in zip(bias_names, bias_rows):
                    for i in range(NPART):
                        sp.dma_start(rows[i].rearrange("(p n) -> p n", p=P), parts[i]).then_inc(sem(s + "_bst"), 16)
                sp.wait_ge(sem(s + "_bst"), 16 * NPART * len(bias_names))
                sp.wait_ge(sem(s + "_lg"), 1)
                for (_, _, _, dst, n), rows in zip(bias_names, bias_rows):
                    sp.dma_start(dst, rows).then_inc(sem(s + "_brow"), 16)
            WIN = 16 * (4 if big else 3 + E)

            @block.tensor
            def _(pe):
                pe.wait_ge(sem(s + "_win"), WIN)
                if not big:
                    for k in range(KD):
                        mm = pe.transpose(PS[:, 2, k * E:(k + 1) * E], wr_raw[0:E, k * P:(k + 1) * P], ident[0:E, 0:E])
                    mm.then_inc(sem(s + "_wrp"), 1)
                    for e in range(E):
                        if e >= 2:
                            pe.wait_ge(sem(s + "_weT"), e - 1)
                        for ko in range(KD):
                            for ki in range(KD):
                                mm = pe.transpose(PS[:, 4 + e % 2, (ki * KD + ko) * P:(ki * KD + ko + 1) * P],
                                                  raw[:, e, ko, ki * P:(ki + 1) * P], ident)
                        mm.then_inc(sem(s + "_wep"), 1)
                    pe.wait_ge(sem(s + "_wr"), 1)
                for t in range(T):
                    if t == 0:
                        pe.wait_ge(sem(lns + "_hT"), T)
                    for k in range(KD):
                        mm = pe.matmul(PS[:, 3, t * E:(t + 1) * E], hT[:, k, t * P:(t + 1) * P], wr[:, k, :],
                                       start=(k == 0), stop=(k == KD - 1))
                mm.then_inc(sem(s + "_lg"), 1)
                pe.wait_ge(sem(s + "_oh"), 1)
                oh2 = ohb.rearrange("p t e -> p (t e)")
                pe.matmul(PS[:, 6, 0:T * E], upper, oh2, start=True, stop=True)
                pe.matmul(PS[:, 7, 0:T * E], onesb, oh2, start=True, stop=True).then_inc(sem(s + "_rank"), 1)

            if not big:
                @block.scalar
                def _(act):
                    for e in range(E):
                        act.wait_ge(sem(s + "_wep"), e + 1)
                        act.copy(WeT[:, e * KD * D:(e + 1) * KD * D], PS[:, 4 + e % 2, :]).then_inc(sem(s + "_weT"), 1)

            @block.scalar
            def _(act):
                act.wait_ge(sem(s + "_ld"), 1)
                act.activation(tb, ta, ACT.Exp).then_inc(sem(s + "_le"), 1)

            @block.vector
            def _(dve):
                n = [0, 0]

                def link(ins):
                    n[0] += 1
                    ins.then_inc(sem(s + "_chain"), 1)
                    dve.wait_ge(sem(s + "_chain"), n[0])

                dve.wait_ge(sem(s + "_win"), WIN)
                for _, raw_b, parts, _, _ in bias_names:
                    for i in range(NPART):
                        ins = dve.tensor_copy(parts[i], raw_b)
                        ins.then_inc(sem(s + "_bparts"), 1)
                        n[1] += 1
                        if i < NPART - 1:
                            dve.wait_ge(sem(s + "_bparts"), n[1])
                            link(dve.tensor_tensor(raw_b, raw_b, parts[i], ALU.subtract))
                if not big:
                    dve.wait_ge(sem(s + "_wrp"), 1)
                    dve.tensor_copy(wr, PS[:, 2, 0:KD * E].rearrange("p (k e) -> p k e", k=KD)).then_inc(sem(s + "_wr"), 1)
                dve.wait_ge(sem(s + "_lg"), 1)
                te = [P, T, E]
                link(dve.tensor_tensor(lg, PS[:, 3, 0:T * E].rearrange("p (t e) -> p t e", t=T),
                                       br.unsqueeze(1).to_broadcast(te), ALU.add))
                link(dve.tensor_reduce(m1, lg, AX.X, ALU.max))
                m1b = m1.unsqueeze(2).to_broadcast(te)
                dve.tensor_tensor(ta, lg, m1b, ALU.subtract).then_inc(sem(s + "_ld"), 1)
                link(dve.tensor_tensor(oh, lg, m1b, ALU.is_equal))
                link(dve.tensor_tensor(lg, oh, order.unsqueeze(1).to_broadcast(te), ALU.mult))
                link(dve.tensor_reduce(posf, lg, AX.X, ALU.max))
                link(dve.tensor_tensor(oh, lg, posf.unsqueeze(2).to_broadcast(te), ALU.is_equal))
                dve.tensor_copy(ohb, oh).then_inc(sem(s + "_oh"), 1)
                dve.wait_ge(sem(s + "_le"), 1)
                link(dve.tensor_reduce(m1, tb, AX.X, ALU.add))
                link(dve.reciprocal(gate, m1))
                dve.wait_ge(sem(s + "_rank"), 1)
                link(dve.tensor_copy(tot, PS[:, 7, 0:T * E].rearrange("p (t e) -> p t e", t=T)))
                cur, nxt = tot, ta
                d = 1
                while d < T:
                    dve.tensor_copy(nxt[:, 0:d, :], cur[:, 0:d, :]).then_inc(sem(s + "_chain"), 1)
                    n[0] += 1
                    link(dve.tensor_tensor(nxt[:, d:T, :], cur[:, d:T, :], cur[:, 0:T - d, :], ALU.add))
                    cur, nxt = nxt, (tb if nxt is ta else ta)
                    d *= 2
                total = cur[:, T - 1, :]
                link(dve.tensor_scalar(c1, total, 1.0 / P, None, ALU.mult))
                link(dve.tensor_tensor(cmp1[:, 0:E, :], c1.unsqueeze(2).to_broadcast([P, E, T]),
                                       count[:, 0:T].unsqueeze(1).to_broadcast([P, E, T]), ALU.is_gt))
                link(dve.tensor_reduce(nt, cmp1[:, 0:E, :], AX.X, ALU.add))
                a0, a1 = nt, c2
                d = 1
                while d < E:
                    dve.tensor_copy(a1[:, 0:d], a0[:, 0:d]).then_inc(sem(s + "_chain"), 1)
                    n[0] += 1
                    link(dve.tensor_tensor(a1[:, d:E], a0[:, d:E], a0[:, 0:E - d], ALU.add))
                    a0, a1 = a1, (c3 if a1 is c2 else c2)
                    d *= 2
                ends = a0
                link(dve.tensor_tensor(c1, ends, nt, ALU.subtract))
                link(dve.tensor_scalar(c1, c1, float(P), None, ALU.mult))
                link(dve.tensor_tensor(lg, cur, tot, ALU.subtract))
                link(dve.tensor_tensor(lg, lg, c1.unsqueeze(1).to_broadcast(te), ALU.add))
                link(dve.tensor_tensor(lg, lg, PS[:, 6, 0:T * E].rearrange("p (t e) -> p t e", t=T), ALU.add))
                link(dve.tensor_tensor(lg, lg, oh, ALU.mult))
                link(dve.tensor_reduce(posf, lg, AX.X, ALU.add))
                dve.tensor_copy(posi, posf).then_inc(sem(s + "_pos"), 1)
                ee = cmp1.rearrange("p e j -> p (e j)")[:, 0:24 * E].rearrange("p (s e) -> p s e", s=24)
                link(dve.tensor_tensor(ee, ends.unsqueeze(1).to_broadcast([P, 24, E]),
                                       count[:, 0:24].unsqueeze(2).to_broadcast([P, 24, E]), ALU.is_le))
                link(dve.tensor_reduce(eidf, ee, AX.X, ALU.add))
                link(dve.tensor_scalar(eidf, eidf, float(E - 1), None, ALU.min))
                dve.tensor_copy(eid, eidf).then_inc(sem(s + "_eid"), 1)

            @block.gpsimd
            def _(pool):
                pool.wait_ge(sem(s + "_pos"), 1)
                pool.wait_ge(sem("xs_clear"), 16 * 2 * -(-NS * D // 2048))
                pool.wait_ge(sem(lns + "_h"), T)
                for t in range(T):
                    pool.indirect_dma_start(
                        out=xs_dram[l], out_offset=bass.IndirectOffsetOnAxis(ap=posi[:, t:t + 1], axis=0),
                        in_=h[:, t, :], in_offset=None).then_inc(sem(s + "_sc"), 16)
                pool.wait_ge(sem(s + "_yst0"), 16 * (NS // 2 + 1))
                pool.wait_ge(sem(s + "_yst1"), 16 * (NS // 2))
                for t in range(T):
                    if t >= NY:
                        pool.wait_ge(sem(s + "_x"), t - NY + 1)
                    pool.indirect_dma_start(
                        out=yg[t % NY], out_offset=None, in_=ys_dram[l],
                        in_offset=bass.IndirectOffsetOnAxis(ap=posi[:, t:t + 1], axis=0)).then_inc(sem(f"{s}_yg{t % NY}"), 16)

            @block.vector
            def _(dve):
                pass

            def tiles(eng, body):
                body(eng, 0, 0, 0, 0)
                body(eng, 1, 1, 1, 0)
                with eng.Fori(1, NS // 2) as i:
                    body(eng, i * 2, 0, 2, i)
                    body(eng, i * 2 + 1, 1, 3, i)
                body(eng, NS - 1, 0, 2, NS // 2)

            def tile_rows(ap, st):
                return ap.rearrange("(s p) d -> s p d", p=P)[st]

            @block.sync
            def _(sp):
                sp.wait_ge(sem(s + "_sc"), 16 * T)

                sp.dma_start(xs[0], tile_rows(xs_dram[l], 0)).then_inc(sem(s + "_xs0"), 16)

                def step(sp, st, r, ahead=True):
                    if ahead:
                        if not (isinstance(st, int) and st == 0):
                            sp.wait_ge(sem(s + "_tp"), st)
                        sp.dma_start(xs[1 - r], tile_rows(xs_dram[l], st + 1)).then_inc(sem(f"{s}_xs{1 - r}"), 16)
                    sp.wait_ge(sem(s + "_yb"), st + 1)
                    sp.dma_start(tile_rows(ys_dram[l], st), yb[r]).then_inc(sem(f"{s}_yst{r}"), 16)

                step(sp, 0, 0)
                step(sp, 1, 1)
                with sp.Fori(1, NS // 2) as i:
                    step(sp, i * 2, 0)
                    step(sp, i * 2 + 1, 1)
                step(sp, NS - 1, 0, ahead=False)

            @block.tensor
            def _(pe):
                pe.wait_ge(sem(s + "_eid"), 1)
                pe.wait_ge(sem(s + "_brow"), 16 * len(bias_names))
                if big:
                    pe.wait_ge(sem(s + "_wbig"), 16 * 2 * E)
                else:
                    pe.wait_ge(sem(s + "_weT"), E)

                def body(pe, st, r, used, n):
                    idx = eid[0:1, st:st + 1] if isinstance(st, int) else eid[0:1, bass.ds(st, 1)]
                    e = pe.value_load(idx, min_val=0, max_val=E - 1)
                    pe.wait_ge(sem(f"{s}_xs{r}"), 16 * (n + 1))
                    if used > 1:
                        pe.wait_ge(sem(s + "_xT"), st - 1)
                    for k in range(KD):
                        mm = pe.transpose(PS[:, r, k * P:(k + 1) * P], xs[r][:, k * P:(k + 1) * P], ident)
                    mm.then_inc(sem(s + "_tp"), 1)
                    pe.wait_ge(sem(s + "_xT"), st + 1)
                    if not big:
                        if used > 1:
                            pe.wait_ge(sem(s + "_yb"), st - 1)
                        ps = PS[:, 2 + r, 0:D]
                        for k in range(KD):
                            pe.matmul(ps, xsT[r][:, k, :], WeT[:, bass.ds(e * (KD * D) + k * D, D)], start=(k == 0), stop=False)
                        pe.matmul(ps, onesb[0:NPART, :], b1[:, bass.ds(e * D, D)], start=False, stop=True).then_inc(sem(s + "_y"), 1)
                        return
                    if used:
                        pe.wait_ge(sem(s + "_h1"), st)
                    for half in range(2):
                        ps = PS[:, 2 + half, :]
                        for k in range(KD):
                            pe.matmul(ps, xsT[r][:, k, :], W1[:, bass.ds(e * (KD * F) + k * F + half * BANK, BANK)],
                                      start=(k == 0), stop=False)
                        mm = pe.matmul(ps, onesb[0:NPART, :], b1[:, bass.ds(e * F + half * BANK, BANK)], start=False, stop=True)
                    mm.then_inc(sem(s + "_h1p"), 1)
                    pe.wait_ge(sem(s + "_h1"), st + 1)
                    for half in range(2):
                        for k in range(4):
                            c = half * 4 + k
                            mm = pe.transpose(PS[:, 4 + half, k * P:(k + 1) * P], h1[0][:, c * P:(c + 1) * P], ident)
                    mm.then_inc(sem(s + "_h1tp"), 1)
                    pe.wait_ge(sem(s + "_h1T"), st + 1)
                    if used:
                        pe.wait_ge(sem(s + "_yb"), st)
                    ps = PS[:, 6, 0:D]
                    for k in range(KF):
                        pe.matmul(ps, h1T[0][:, k, :], W2[:, bass.ds(e * (KF * D) + k * D, D)], start=(k == 0), stop=False)
                    pe.matmul(ps, onesb[0:NPART, :], b2[:, bass.ds(e * D, D)], start=False, stop=True).then_inc(sem(s + "_y"), 1)
                tiles(pe, body)

            @block.scalar
            def _(act):
                def body(act, st, r, used, n):
                    act.wait_ge(sem(s + "_tp"), st + 1)
                    act.copy(xsT[r], PS[:, r, 0:KD * P].rearrange("p (k n) -> p k n", k=KD)).then_inc(sem(s + "_xT"), 1)
                    if big:
                        act.wait_ge(sem(s + "_h1p"), st + 1)
                        act.activation(h1[0].rearrange("p (a n) -> p a n", a=2), PS[:, 2:4, :], ACT.Relu).then_inc(sem(s + "_h1"), 1)
                    act.wait_ge(sem(s + "_y"), st + 1)
                    if used > 1:
                        act.wait_ge(sem(f"{s}_yst{r}"), 16 * n)
                    act.copy(yb[r], PS[:, 6 if big else 2 + r, 0:D]).then_inc(sem(s + "_yb"), 1)
                tiles(act, body)

            @block.vector
            def _(dve):
                if big:
                    def body(dve, st, r, used, n):
                        dve.wait_ge(sem(s + "_h1tp"), st + 1)
                        dve.tensor_copy(h1T[0].rearrange("p (a k) n -> p a (k n)", a=2), PS[:, 4:6, :]).then_inc(sem(s + "_h1T"), 1)
                    tiles(dve, body)
                for t in range(T):
                    dve.wait_ge(sem(f"{s}_yg{t % NY}"), 16 * (t // NY + 1))
                    dve.scalar_tensor_tensor(out=x[:, t, :], in0=yg[t % NY], scalar=gate[:, t:t + 1], in1=x[:, t, :],
                                             op0=ALU.mult, op1=ALU.add).then_inc(sem(s + "_x"), 1)

        with nc.Block() as block:
            prepare(block)
            ln(block, "ln0", "x_in", 16 * 4)
            add_bias(block, "ln0", b_out[0], "w_in", W_IN)
            qkv0(block)
            attention(block, 0, causal=False)
            project(block, 0)
            ln(block, "ln1", "p0_x", T)
            add_bias(block, "ln1", xb_out, "w_in", W_IN)
            cross(block, 0, top=True)
            ln(block, "ln2", "x0_xd", T)
            moe(block, 0, "x0_xd", T)

        nc.clear_and_free_semaphores([sems.pop(n) for n in list(sems) if n not in KEPT])
        nc.all_engine_barrier()

        with nc.Block() as block:
            ln(block, "ln3", "e0_x", T)
            add_bias(block, "ln3", b_out[1], "w_in", W_IN)
            qkv1(block)
            attention(block, 1, causal=True)
            project(block, 1)
            ln(block, "ln4", "p1_x", T)
            cross(block, 1, top=False)
            ln(block, "ln5", "x1_x2", T)
            moe(block, 1, "x1_x2", T)

            @block.sync
            def _(sp):
                for t in range(T):
                    sp.wait_ge(sem("e1_x"), t + 1)
                    sp.dma_start(out[t // TB, (t % TB) * P:(t % TB + 1) * P, :], x[:, t, :]).then_inc(sem("out"), 16)
                sp.wait_ge(sem("out"), 16 * T)


def kernel(**inputs):
    import numpy as _np
    import concourse.bacc as _bacc
    from concourse import mybir as _mybir
    from concourse.bass_utils import run_bass_kernel_spmd as _run

    nc = _bacc.Bacc("TRN2", target_bir_lowering=False, num_devices=1)
    arrays, aps = {}, {}
    for name, value in inputs.items():
        v = _np.ascontiguousarray(value)
        arrays[f"in_{name}"] = v
        aps[name] = nc.dram_tensor(f"in_{name}", v.shape, _mybir.dt.from_np(v.dtype), kind="ExternalInput").ap()
    out = nc.dram_tensor("decoded", (B, S, D), F32, kind="ExternalOutput").ap()
    build(nc, aps, out)
    r = _run(nc, [arrays], core_ids=[0])
    return r.results[0]["decoded"]
```

```python
from contextlib import ExitStack

import concourse.bass as bass
from concourse import mybir

F32 = mybir.dt.float32
BF16 = mybir.dt.bfloat16
I32 = mybir.dt.int32
U32 = mybir.dt.uint32
ALU = mybir.AluOpType
ACT = mybir.ActivationFunctionType
AX = mybir.AxisListType

P = 128
B, S, D = 2, 1024, 256
KD = D // P
NH, HD = 16, 16
T = B * S // P
TB = T // B
C = 77
E, F = 8, 1024
KF = F // P
BANK = 512
G = 4
NG = NH // G
NU = B * NG
SLOT = 32
QUERY_PARTS = (0, 0, 0, 1, 1, 2)
KEY_PARTS = (0, 1, 2, 0, 1, 0)
NPART = 3
NSLOT = len(QUERY_PARTS)
KS = NSLOT * HD
KM = KS + 2
NST = 3
PR = 8
SCALE = HD ** -0.5
TOPK = 32
LOWEST = -3.0e38
MASKED = -1.0e30
NTB = 4
NS = T + E - 1
LN_EPS = 1e-5
L0_EPS = 1e-6


class Region:

    def __init__(self, arena, size):
        self.arena, self.size, self.at = arena, size, 0

    def f32(self, n):
        a = self.at
        self.at += n
        assert self.at <= self.size, (self.at, self.size)
        return self.arena[:, a:a + n]

    def bf16(self, n):
        return self.f32((n + 1) // 2).bitcast(BF16)


def fills(causal):
    out = []
    for i in range(TB):
        keys = (i + 1) * P if causal else S
        for k in range(0, keys, BANK):
            out.append((i, k // BANK, min(BANK, keys - k)))
    return out


def build(nc, a, out):
    ctx = ExitStack()
    with ctx:
        sems = {}
        KEPT = ("const", "w_in", "xw_in", "kblk", "xv", "xs_clear", "x_in", "out", "e0_x")

        def sem(name):
            if name not in sems:
                sems[name] = nc.alloc_semaphore(name)
            return sems[name]

        SIZE = 53200
        arena = ctx.enter_context(nc.sbuf_tensor("arena", [P, SIZE], F32))
        PS = ctx.enter_context(nc.psum_tensor("banks", [P, 8, BANK], F32))
        R = Region(arena, SIZE)

        def scratch(name, shape, dt=F32):
            return nc.dram_tensor(name, shape, dt, kind="Internal").ap()

        parts_dram = [scratch(f"parts{l}", [2, NPART, B * D, S], BF16) for l in range(2)]
        v_dram = [scratch(f"v{l}", [NU, P, TB, G * SLOT]) for l in range(2)]
        o_dram = [scratch(f"o{l}", [B * D, S]) for l in range(2)]
        sum_dram = [scratch(f"sum{l}", [B * P, P]) for l in range(2)]
        rec_dram = [scratch(f"rec{l}", [B * NH, S]) for l in range(2)]
        xs_dram = [scratch(f"sorted{l}", [NS * P, D]) for l in range(2)]
        ys_dram = [scratch(f"expert_out{l}", [NS * P, D]) for l in range(2)]

        x = R.f32(T * D).rearrange("p (t d) -> p t d", t=T)
        h = R.f32(T * D).rearrange("p (t d) -> p t d", t=T)
        hT = R.f32(KD * B * S).rearrange("p (k n) -> p k n", k=KD)
        ident = R.f32(P)
        identb = R.bf16(P)
        upper = R.bf16(P)
        onesb = R.bf16(P)
        onesf = R.f32(P)
        future = R.bf16(P)
        futureT = R.bf16(P)
        stats = R.f32(T * 6).rearrange("p (t s) -> p t s", t=T)
        mv = R.f32(T * 2).rearrange("p (t s) -> p t s", t=T)
        std = R.f32(T)
        rstd = R.f32(T)
        count = R.f32(32)
        order = R.f32(E)
        hmask = R.f32(8)
        base_mark = R.at

        w_qkv = [R.f32(3 * 3 * D).rearrange("p (k n) -> p k n", k=3) for _ in range(2)]
        w_out = [R.f32(KD * D).rearrange("p (k n) -> p k n", k=KD) for _ in range(2)]
        b_out = [R.f32(D) for _ in range(2)]
        b_qk1 = R.f32(4)
        ln_scale = R.f32(3 * HD).rearrange("p (s d) -> p s d", s=3)
        ln_bias = R.f32(3 * HD).rearrange("p (s d) -> p s d", s=3)
        cmean = R.f32(9 * NH)
        xb_out = R.f32(D)
        gamma, beta = R.f32(D), R.f32(D)
        xq_b = [R.f32(KD) for _ in range(2)]
        xk_b = [R.f32(KD) for _ in range(2)]
        xv_b = [R.f32(D) for _ in range(2)]
        xwqT = [R.f32(KD * D).rearrange("p (k n) -> p k n", k=KD) for _ in range(2)]
        xwo = R.f32(KD * D).rearrange("p (k n) -> p k n", k=KD)
        ctxT = R.f32(KD * B * C).rearrange("p (k n) -> p k n", k=KD)
        kblk = [R.f32(B * KD * 8 * C).rearrange("p (b k j c) -> p b k j c", b=B, k=KD, j=8) for _ in range(2)]
        xv = [R.f32(B * NH * SLOT).rearrange("p (b h s) -> p b h s", b=B, h=NH) for _ in range(2)]
        work_mark = R.at


        W0_IN, XW_IN, W_IN = 16 * 12, 16 * (8 + 2 * 5), 16 * 13
        CONST = 17

        def prepare(block):
            R.at = work_mark
            xw_names = [("L0_xattn_Wk", 0), ("L0_xattn_Wv", 0), ("L1_xattn_Wk", 1), ("L1_xattn_Wv", 1),
                        ("L0_xattn_Wq", 0), ("L1_xattn_Wq", 1), ("L0_xattn_Wo", 0)]
            xw_raw = [R.f32(KD * D).rearrange("p (k n) -> p k n", k=KD) for _ in xw_names]
            xw_t = [R.f32(KD * D).rearrange("p (k n) -> p k n", k=KD) for _ in range(4)]
            ctx_raw = R.f32(B * D).rearrange("p (b d) -> p b d", b=B)
            kt_raw = R.f32(KD * B * C).rearrange("p (k n) -> p k n", k=KD)
            vx_raw = R.f32(D)
            vx_mask = R.f32(D).bitcast(I32)
            ZW = 2048
            zero_tile = R.f32(ZW)
            tmp = R.f32(P)

            @block.sync
            def _(sp):
                def load(dst, src, name):
                    sp.dma_start(dst, src).then_inc(sem(name), 16)

                for b in range(B):
                    for t in range(0, TB, 4):
                        load(x[:, b * TB + t:b * TB + t + 4, :],
                             a["x"][b].rearrange("(t p) d -> p t d", p=P)[:, t:t + 4, :], "x_in")
                for i, n in enumerate(("Wq", "Wk", "Wv")):
                    load(w_qkv[0][:, 0:KD, i * D:(i + 1) * D], a[f"L0_attn_{n}"].rearrange("(k p) n -> p k n", p=P), "w0_in")
                for i, n in enumerate(("bq", "bk", "bv")):
                    load(w_qkv[0][:, 2, i * D:(i + 1) * D], a[f"L0_attn_{n}"].partition_broadcast(P), "w0_in")
                for i, n in enumerate("qkv"):
                    load(ln_scale[:, i, :], a[f"L0_attn_{n}_scale"].partition_broadcast(P), "w0_in")
                    load(ln_bias[:, i, :], a[f"L0_attn_{n}_bias"].partition_broadcast(P), "w0_in")
                for (n, _), dst in zip(xw_names, xw_raw):
                    load(dst, a[n].rearrange("(k p) n -> p k n", p=P), "xw_in")
                load(ctx_raw[0:C], a["ctx_1024"].rearrange("b c d -> c b d"), "xw_in")
                for l in range(2):
                    for dst, n in ((xq_b[l], "bq"), (xk_b[l], "bk")):
                        for k in range(KD):
                            load(dst[:, k:k + 1], a[f"L{l}_xattn_{n}"][k * P:(k + 1) * P].unsqueeze(1), "xw_in")
                    load(xv_b[l][0:C], a[f"L{l}_xattn_bv"].partition_broadcast(C), "xw_in")
                load(w_out[0], a["L0_attn_Wo"].rearrange("(k p) n -> p k n", p=P), "w_in")
                load(b_out[0], a["L0_attn_bo"].partition_broadcast(P), "w_in")
                load(xb_out, a["L0_xattn_bo"].partition_broadcast(P), "w_in")
                load(w_qkv[1][:, 0:KD, :], a["L1_attn_qkv_w"].rearrange("(k p) n -> p k n", p=P), "w_in")
                load(w_qkv[1][:, 2, :], a["L1_attn_qkv_b"].partition_broadcast(P), "w_in")
                for k in range(4):
                    load(b_qk1[:, k:k + 1], a["L1_attn_qkv_b"][k * P:(k + 1) * P].unsqueeze(1), "w_in")
                load(w_out[1], a["L1_attn_out_w"].rearrange("(k p) n -> p k n", p=P), "w_in")
                load(b_out[1], a["L1_attn_out_b"].partition_broadcast(P), "w_in")
                load(gamma, a["L1_xattn_gamma"].partition_broadcast(P), "w_in")
                load(beta, a["L1_xattn_beta"].partition_broadcast(P), "w_in")
                sp.wait_ge(sem("zeroed"), 1)
                for l in range(2):
                    rows = xs_dram[l].rearrange("(p r) d -> p (r d)", p=P)
                    for n0 in range(0, NS * D, ZW):
                        w = min(ZW, NS * D - n0)
                        sp.dma_start(rows[:, n0:n0 + w], zero_tile[:, 0:w]).then_inc(sem("xs_clear"), 16)


            @block.gpsimd
            def _(pool):
                pool.memset(zero_tile, 0.0).then_inc(sem("zeroed"), 1)
                pool.memset(tmp, 0.0).then_inc(sem("const"), 1)
                pool.memset(onesf, 1.0).then_inc(sem("const"), 1)
                pool.memset(onesb, 1.0).then_inc(sem("const"), 1)
                pool.memset(hmask, 1.0).then_inc(sem("const"), 1)
                for l in range(2):
                    pool.memset(xv[l][:, :, :, 0:HD], 0.0).then_inc(sem("const"), 1)
                    pool.memset(xv[l][:, :, :, HD:SLOT], 1.0).then_inc(sem("const"), 1)
                pool.iota(count, pattern=[[1, 32]], base=0, channel_multiplier=0,
                          allow_small_or_imprecise_dtypes=True).then_inc(sem("const"), 1)
                pool.iota(order, pattern=[[-1, E]], base=E, channel_multiplier=0,
                          allow_small_or_imprecise_dtypes=True).then_inc(sem("const"), 1)
                pool.wait_ge(sem("const"), 10)
                pool.affine_select(out=ident, in_=tmp, compare_op=ALU.not_equal, fill=1.0, base=0,
                                   pattern=[[-1, P]], channel_multiplier=1).then_inc(sem("const"), 1)
                pool.affine_select(out=hmask, in_=hmask, compare_op=ALU.is_ge, fill=0.0, base=0,
                                   pattern=[[-HD, 8]], channel_multiplier=1).then_inc(sem("const"), 1)
                pool.affine_select(out=upper, in_=onesb, compare_op=ALU.is_gt, fill=0.0, base=0,
                                   pattern=[[1, P]], channel_multiplier=-1).then_inc(sem("const"), 1)
                pool.affine_select(out=future, in_=tmp, compare_op=ALU.is_ge, fill=MASKED, base=0,
                                   pattern=[[-1, P]], channel_multiplier=1).then_inc(sem("const"), 1)
                pool.affine_select(out=futureT, in_=tmp, compare_op=ALU.is_ge, fill=MASKED, base=0,
                                   pattern=[[1, P]], channel_multiplier=-1).then_inc(sem("const"), 1)
                pool.wait_ge(sem("const"), 15)
                pool.affine_select(out=hmask, in_=hmask, compare_op=ALU.is_ge, fill=0.0, base=HD - 1,
                                   pattern=[[HD, 8]], channel_multiplier=-1).then_inc(sem("const"), 1)
                pool.tensor_copy(identb, ident).then_inc(sem("const"), 1)


            @block.vector
            def _(dve):
                dve.wait_ge(sem("w0_in"), W0_IN)
                flat = w_qkv[0].rearrange("p k (h d) -> p (k h) d", d=HD)
                dve.tensor_reduce(cmean, flat, AX.X, ALU.add).then_inc(sem("centre"), 1)
                dve.wait_ge(sem("centre"), 1)
                dve.tensor_scalar(cmean, cmean, 1.0 / HD, None, ALU.mult).then_inc(sem("centre"), 1)
                dve.wait_ge(sem("centre"), 2)
                dve.tensor_tensor(flat, flat, cmean.unsqueeze(2).to_broadcast([P, 9 * NH, HD]),
                                  ALU.subtract).then_inc(sem("centre"), 1)

            @block.tensor
            def _(pe):
                pe.wait_ge(sem("const"), CONST)
                pe.wait_ge(sem("xw_in"), XW_IN)
                for n in range(len(xw_names)):
                    if n >= 2:
                        pe.wait_ge(sem("xwT"), n - 1)
                    for ko in range(KD):
                        for ki in range(KD):
                            mm = pe.transpose(PS[:, n % 2, (ki * KD + ko) * P:(ki * KD + ko + 1) * P],
                                              xw_raw[n][:, ko, ki * P:(ki + 1) * P], ident)
                    mm.then_inc(sem("xwT_ps"), 1)
                for b in range(B):
                    for k in range(KD):
                        mm = pe.transpose(PS[:, 2, (k * B + b) * C:(k * B + b + 1) * C],
                                          ctx_raw[0:C, b, k * P:(k + 1) * P], ident[0:C, 0:C])
                mm.then_inc(sem("ctxT_ps"), 1)
                pe.wait_ge(sem("ctxT"), 1)
                pe.wait_ge(sem("xwT"), len(xw_names))
                n = 0
                for l in range(2):
                    for half in range(KD):
                        if n >= 2:
                            pe.wait_ge(sem("kt"), n - 1)
                        for k in range(KD):
                            mm = pe.matmul(PS[:, 3 + n % 2, 0:B * C], xw_t[2 * l][:, k, half * P:(half + 1) * P],
                                           ctxT[:, k, :], start=(k == 0), stop=(k == KD - 1))
                        mm.then_inc(sem("kt_ps"), 1)
                        n += 1
                n = 0
                for l in range(2):
                    for b in range(B):
                        if n >= 2:
                            pe.wait_ge(sem("vx"), n - 1)
                        for k in range(KD):
                            mm = pe.matmul(PS[0:C, 5 + n % 2, 0:D], ctxT[:, k, b * C:(b + 1) * C],
                                           xw_t[2 * l + 1][:, k, :], start=(k == 0), stop=(k == KD - 1))
                        mm.then_inc(sem("vx_ps"), 1)
                        n += 1

            @block.vector
            def _(dve):
                dve.wait_ge(sem("const"), CONST)
                for n in range(len(xw_names)):
                    dve.wait_ge(sem("xwT_ps"), n + 1)
                    src = PS[:, n % 2, 0:KD * D].rearrange("p (k n) -> p k n", k=KD)
                    if n < 4:
                        dve.tensor_copy(xw_t[n], src).then_inc(sem("xwT"), 1)
                    elif n < 6:
                        dve.tensor_copy(xwqT[n - 4], src).then_inc(sem("xwT"), 1)
                    else:
                        dve.tensor_copy(xwo, src).then_inc(sem("xwT"), 1)
                dve.wait_ge(sem("ctxT_ps"), 1)
                dve.tensor_copy(ctxT, PS[:, 2, 0:KD * B * C].rearrange("p (k n) -> p k n", k=KD)).then_inc(sem("ctxT"), 1)
                n = 0
                for l in range(2):
                    for half in range(KD):
                        dve.wait_ge(sem("kt_ps"), n + 1)
                        if n:
                            dve.wait_ge(sem("kblk"), n * B)
                        dve.tensor_scalar(kt_raw[:, 0, :], PS[:, 3 + n % 2, 0:B * C], xk_b[l][:, half:half + 1], None,
                                          ALU.add).then_inc(sem("kt"), 1)
                        dve.wait_ge(sem("kt"), n + 1)
                        for b in range(B):
                            dve.tensor_tensor(kblk[l][:, b, half], kt_raw[:, 0, b * C:(b + 1) * C].unsqueeze(1).to_broadcast([P, 8, C]),
                                              hmask.unsqueeze(2).to_broadcast([P, 8, C]), ALU.mult).then_inc(sem("kblk"), 1)
                        n += 1
                n = 0
                for l in range(2):
                    for b in range(B):
                        dve.wait_ge(sem("vx_ps"), n + 1)
                        if n:
                            dve.wait_ge(sem("xv"), n)
                        dst = xv[l][0:C, b, :, 0:HD]
                        dve.tensor_tensor(vx_raw[0:C], PS[0:C, 5 + n % 2, 0:D], xv_b[l][0:C], ALU.add).then_inc(sem("vx"), 1)
                        dve.wait_ge(sem("vx"), n + 1)
                        if l == 1:
                            dve.tensor_tensor(vx_mask[0:C], vx_raw[0:C], vx_raw[0:C], ALU.is_equal).then_inc(sem("vxm"), 1)
                            dve.wait_ge(sem("vxm"), b + 1)
                            dve.copy_predicated(dst, vx_mask[0:C].rearrange("p (h d) -> p h d", h=NH),
                                                vx_raw[0:C].rearrange("p (h d) -> p h d", h=NH)).then_inc(sem("xv"), 1)
                        else:
                            dve.tensor_copy(dst, vx_raw[0:C].rearrange("p (h d) -> p h d", h=NH)).then_inc(sem("xv"), 1)
                        n += 1
                dve.wait_ge(sem("xv"), 2 * B)

        def ln(block, s, x_sem, x_val, transposed=True):
            @block.vector
            def _(dve):
                dve.wait_ge(sem(x_sem), x_val)
                for t in range(T):
                    dve.bn_stats(stats[:, t, :], x[:, t, :]).then_inc(sem(s + "_st"), 1)
                for t in range(T):
                    dve.wait_ge(sem(s + "_st"), t + 1)
                    dve.bn_aggr(mv[:, t, :], stats[:, t, :]).then_inc(sem(s + "_mv"), 1)
                dve.wait_ge(sem(s + "_mv"), T)
                dve.tensor_scalar(std, mv[:, :, 1], LN_EPS, None, ALU.add).then_inc(sem(s + "_var"), 1)
                dve.wait_ge(sem(s + "_std"), 1)
                dve.reciprocal(rstd, std).then_inc(sem(s + "_rstd"), 1)
                dve.wait_ge(sem(s + "_rstd"), 1)
                for t in range(T):
                    dve.tensor_scalar(h[:, t, :], x[:, t, :], mv[:, t, 0:1], rstd[:, t:t + 1], ALU.subtract,
                                      ALU.mult).then_inc(sem(s + "_h"), 1)

            @block.scalar
            def _(act):
                act.wait_ge(sem(s + "_var"), 1)
                act.activation(std, std, ACT.Sqrt).then_inc(sem(s + "_std"), 1)
                for t in range(T):
                    act.wait_ge(sem(s + "_tr"), t + 1)
                    act.copy(hT[:, :, t * P:(t + 1) * P],
                             PS[:, 6 + t % 2, 0:KD * P].rearrange("p (k n) -> p k n", k=KD)).then_inc(sem(s + "_hT"), 1)

            @block.tensor
            def _(pe):
                pe.wait_ge(sem("const"), CONST)
                for t in range(T):
                    pe.wait_ge(sem(s + "_h"), t + 1)
                    if t >= 2:
                        pe.wait_ge(sem(s + "_hT"), t - 1)
                    for k in range(KD):
                        mm = pe.transpose(PS[:, 6 + t % 2, k * P:(k + 1) * P], h[:, t, k * P:(k + 1) * P], ident)
                    mm.then_inc(sem(s + "_tr"), 1)

        def add_bias(block, s, bias, wsem, wval):
            @block.gpsimd
            def _(pool):
                pool.wait_ge(sem(s + "_h"), T)
                pool.wait_ge(sem(wsem), wval)
                pool.tensor_tensor(x, x, bias.unsqueeze(1).to_broadcast([P, T, D]), ALU.add).then_inc(sem(s + "_xb"), 1)

        def split_chunks(s, R_parts, u_bufs, source, dest):
            def act_part(act, i):
                if i < 16:
                    ps, bias, ready, val = source(i)
                    act.wait_ge(sem(ready), val)
                    if i >= 3:
                        act.wait_ge(sem(s + "_s3"), i - 2)
                    kw = {} if bias is None else {"bias": bias}
                    act.activation(u_bufs[i % 3], ps, ACT.Identity, **kw).then_inc(sem(s + "_u"), 1)
                    act.activation(dest(i, 0), ps, ACT.Identity, **kw).then_inc(sem(s + "_s1"), 1)
                if i >= 1 and i - 1 < 16:
                    act.wait_ge(sem(s + "_r1"), i)
                    src = u_bufs[(i - 1) % 3]
                    act.activation(dest(i - 1, 1), src, ACT.Identity).then_inc(sem(s + "_s2"), 1)

            def pool_part(pool, i):
                if i < 16:
                    pool.wait_ge(sem(s + "_s1"), i + 1)
                    pool.tensor_tensor(u_bufs[i % 3], u_bufs[i % 3], dest(i, 0), ALU.subtract).then_inc(sem(s + "_r1"), 1)
                if i >= 1 and i - 1 < 16:
                    pool.wait_ge(sem(s + "_s2"), i)
                    pool.wait_ge(sem(s + "_r1"), i)
                    pool.tensor_tensor(dest(i - 1, 2), u_bufs[(i - 1) % 3], dest(i - 1, 1), ALU.subtract).then_inc(sem(s + "_s3"), 1)

            return act_part, pool_part

        def store_parts(sp, s, l, b, parts):
            sp.wait_ge(sem(s + "_s3"), 8 * (b + 1))
            sp.wait_ge(sem(s + "_s1"), 8 * (b + 1))
            sp.wait_ge(sem(s + "_s2"), 8 * (b + 1))
            for qk in range(2):
                for n in range(NPART):
                    sp.dma_start(parts_dram[l][qk, n, b * D:(b + 1) * D, :].rearrange("(k p) n -> p k n", p=P),
                                 parts[b][:, n, qk * KD:(qk + 1) * KD, :]).then_inc(sem(s + "_parts"), 16)

        PARTS_ST = 16 * 2 * NPART * B

        def qkv0(block):
            s = "q0"
            R.at = work_mark
            parts = [R.bf16(NPART * 4 * S).rearrange("p (n c t) -> p n c t", n=NPART, c=4) for _ in range(B)]
            cb = [R.f32(3 * D) for _ in range(4)]
            sq = [R.f32(3 * D) for _ in range(2)]
            ss = [R.f32(3 * NH) for _ in range(4)]
            ub = [R.f32(BANK) for _ in range(3)]
            vt = [R.f32(NH * SLOT).rearrange("p (h s) -> p h s", h=NH) for _ in range(2)]
            u_bufs = [u.rearrange("p (c n) -> p c n", c=4) for u in ub]

            def source(i):
                return PS[:, 4 + i % 2, :].rearrange("p (c n) -> p c n", c=4), None, s + "_tr", i + 1

            def dest(i, n):
                return parts[i // TB][:, n, :, (i % TB) * P:(i % TB + 1) * P]

            act_split, pool_split = split_chunks(s, parts, u_bufs, source, dest)

            @block.tensor
            def _(pe):
                pe.wait_ge(sem("centre"), 3)
                for i in range(T + 4):
                    if i < T:
                        pe.wait_ge(sem("ln0_hT"), i + 1)
                        if i >= 2:
                            pe.wait_ge(sem(s + "_c"), i - 1)
                        b0 = 2 * (i % 2)
                        for n0, nw in ((0, BANK), (BANK, 3 * D - BANK)):
                            for k in range(KD):
                                mm = pe.matmul(PS[:, b0 + n0 // BANK, 0:nw], hT[:, k, i * P:(i + 1) * P],
                                               w_qkv[0][:, k, n0:n0 + nw], start=(k == 0), stop=(k == KD - 1))
                        mm.then_inc(sem(s + "_ps"), 1)
                    if i >= 4:
                        t = i - 4
                        pe.wait_ge(sem(s + "_n"), t + 1)
                        if t >= 2:
                            pe.wait_ge(sem(s + "_s1"), t - 1)
                        for c in range(4):
                            mm = pe.transpose(PS[:, 4 + t % 2, c * P:(c + 1) * P], cb[t % 4][:, c * P:(c + 1) * P], ident)
                        mm.then_inc(sem(s + "_tr"), 1)

            @block.vector
            def _(dve):
                dve.wait_ge(sem("centre"), 3)
                for i in range(T + 2):
                    if i < T:
                        dve.wait_ge(sem(s + "_ps"), i + 1)
                        if i >= 4:
                            dve.wait_ge(sem(s + "_tr"), i - 3)
                            dve.wait_ge(sem(s + "_v"), i - 3)
                        b0 = 2 * (i % 2)
                        dve.tensor_tensor(cb[i % 4], PS[:, b0:b0 + 2, :].rearrange("p a n -> p (a n)")[:, 0:3 * D],
                                          w_qkv[0][:, 2, :], ALU.add).then_inc(sem(s + "_c"), 1)
                    if 1 <= i <= T:
                        t = i - 1
                        dve.wait_ge(sem(s + "_sq"), t + 1)
                        dve.tensor_reduce(ss[t % 4], sq[t % 2].rearrange("p (h d) -> p h d", d=HD), AX.X,
                                          ALU.add).then_inc(sem(s + "_ss"), 1)
                        dve.wait_ge(sem(s + "_ss"), t + 1)
                        dve.tensor_scalar(ss[t % 4], ss[t % 4], 1.0 / HD, L0_EPS, ALU.mult, ALU.add).then_inc(sem(s + "_var"), 1)
                    if i >= 2:
                        t = i - 2
                        dve.wait_ge(sem(s + "_std"), t + 1)
                        dve.reciprocal(ss[t % 4], ss[t % 4]).then_inc(sem(s + "_rs"), 1)

            @block.scalar
            def _(act):
                for i in range(T):
                    act.wait_ge(sem(s + "_var"), i + 1)
                    act.activation(ss[i % 4], ss[i % 4], ACT.Sqrt).then_inc(sem(s + "_std"), 1)
                    if i >= 4:
                        act_split(act, i - 4)
                for i in range(T - 4, T + 1):
                    act_split(act, i)

            @block.gpsimd
            def _(pool):
                for v in vt:
                    pool.memset(v[:, :, HD:SLOT], 1.0).then_inc(sem(s + "_vpad"), 1)

                def norm(t):
                    c, r = cb[t % 4], ss[t % 4]
                    c48 = c.rearrange("p (h d) -> p h d", d=HD)
                    pool.wait_ge(sem(s + "_rs"), t + 1)
                    pool.tensor_tensor(c48, c48, r.unsqueeze(2).to_broadcast([P, 3 * NH, HD]), ALU.mult).then_inc(sem(s + "_n1"), 1)
                    pool.wait_ge(sem(s + "_n1"), t + 1)
                    c3 = c.rearrange("p (s h d) -> p s h d", s=3, d=HD)
                    pool.tensor_tensor(c3, c3, ln_scale.unsqueeze(2).to_broadcast([P, 3, NH, HD]), ALU.mult).then_inc(sem(s + "_n2"), 1)
                    pool.wait_ge(sem(s + "_n2"), t + 1)
                    pool.tensor_tensor(c3[:, 0:2], c3[:, 0:2], ln_bias[:, 0:2].unsqueeze(2).to_broadcast([P, 2, NH, HD]),
                                       ALU.add).then_inc(sem(s + "_n"), 1)
                    if t >= 2:
                        pool.wait_ge(sem(f"{s}_vst{t % 2}"), 16 * (t // 2))
                    else:
                        pool.wait_ge(sem(s + "_vpad"), 2)
                    pool.tensor_tensor(vt[t % 2][:, :, 0:HD], c3[:, 2], ln_bias[:, 2].unsqueeze(1).to_broadcast([P, NH, HD]),
                                       ALU.add).then_inc(sem(s + "_v"), 1)

                for i in range(T + 5):
                    if i < T:
                        pool.wait_ge(sem(s + "_c"), i + 1)
                        if i >= 2:
                            pool.wait_ge(sem(s + "_ss"), i - 1)
                        pool.tensor_tensor(sq[i % 2], cb[i % 4], cb[i % 4], ALU.mult).then_inc(sem(s + "_sq"), 1)
                    if 2 <= i < T + 2:
                        norm(i - 2)
                    if i >= 4:
                        pool_split(pool, i - 4)

            @block.sync
            def _(sp):
                for t in range(T):
                    sp.wait_ge(sem(s + "_v"), t + 1)
                    b = t // TB
                    sp.dma_start(v_dram[0][b * NG:(b + 1) * NG, :, t % TB, :].rearrange("g p n -> p g n"),
                                 vt[t % 2].rearrange("p (g j) s -> p g (j s)", g=NG)).then_inc(sem(f"{s}_vst{t % 2}"), 16)
                    if t == TB + 5:
                        store_parts(sp, s, 0, 0, parts)
                store_parts(sp, s, 0, 1, parts)

        def qkv1(block):
            s = "q1"
            R.at = work_mark
            parts = [R.bf16(NPART * 4 * S).rearrange("p (n c t) -> p n c t", n=NPART, c=4) for _ in range(B)]
            u_bufs = [R.f32(BANK) for _ in range(3)]
            vt = [R.f32(NH * SLOT).rearrange("p (h s) -> p h s", h=NH) for _ in range(2)]

            def where(i):
                b, m, half = i // 8, (i % 8) // 2, i % 2
                return b, m, half

            def source(i):
                b, m, half = where(i)
                return PS[:, 4 + i % 2, :], b_qk1[:, m:m + 1], s + "_ps", i + 1

            def dest(i, n):
                b, m, half = where(i)
                return parts[b][:, n, m, half * BANK:(half + 1) * BANK]

            act_split, pool_split = split_chunks(s, parts, u_bufs, source, dest)

            @block.tensor
            def _(pe):
                pe.wait_ge(sem("w_in"), W_IN)
                pe.wait_ge(sem("ln3_hT"), T)
                for i in range(16):
                    b, m, half = where(i)
                    if i >= 2:
                        pe.wait_ge(sem(s + "_s1"), i - 1)
                    for k in range(KD):
                        mm = pe.matmul(PS[:, 4 + i % 2, :], w_qkv[1][:, k, m * P:(m + 1) * P],
                                       hT[:, k, b * S + half * BANK:b * S + (half + 1) * BANK],
                                       start=(k == 0), stop=(k == KD - 1))
                    mm.then_inc(sem(s + "_ps"), 1)
                    if i >= 2:
                        pe.wait_ge(sem(s + "_v"), i - 1)
                    for k in range(KD):
                        mm = pe.matmul(PS[:, i % 2, 0:D], hT[:, k, i * P:(i + 1) * P], w_qkv[1][:, k, 2 * D:3 * D],
                                       start=(k == 0), stop=(k == KD - 1))
                    mm.then_inc(sem(s + "_vps"), 1)

            @block.scalar
            def _(act):
                act.wait_ge(sem("w_in"), W_IN)
                for i in range(17):
                    act_split(act, i)

            @block.gpsimd
            def _(pool):
                pool.wait_ge(sem("e0_x"), T)
                for v in vt:
                    pool.memset(v[:, :, HD:SLOT], 1.0).then_inc(sem(s + "_vpad"), 1)
                for i in range(17):
                    pool_split(pool, i)

            @block.vector
            def _(dve):
                dve.wait_ge(sem("w_in"), W_IN)
                for t in range(T):
                    dve.wait_ge(sem(s + "_vps"), t + 1)
                    if t >= 2:
                        dve.wait_ge(sem(f"{s}_vst{t % 2}"), 16 * (t // 2))
                    else:
                        dve.wait_ge(sem(s + "_vpad"), 2)
                    dve.tensor_tensor(vt[t % 2][:, :, 0:HD], PS[:, t % 2, 0:D].rearrange("p (h d) -> p h d", d=HD),
                                      w_qkv[1][:, 2, 2 * D:3 * D].rearrange("p (h d) -> p h d", d=HD),
                                      ALU.add).then_inc(sem(s + "_v"), 1)

            @block.sync
            def _(sp):
                for t in range(T):
                    sp.wait_ge(sem(s + "_v"), t + 1)
                    b = t // TB
                    sp.dma_start(v_dram[1][b * NG:(b + 1) * NG, :, t % TB, :].rearrange("g p n -> p g n"),
                                 vt[t % 2].rearrange("p (g j) s -> p g (j s)", g=NG)).then_inc(sem(f"{s}_vst{t % 2}"), 16)
                for b in range(B):
                    store_parts(sp, s, 1, b, parts)

        def attention(block, l, causal):
            s, q = f"a{l}", f"q{l}"
            R.at = work_mark
            qst = [R.bf16(G * S).rearrange("p (j t) -> p j t", j=G) for _ in range(NST)]
            kst = [R.bf16(G * S).rearrange("p (j t) -> p j t", j=G) for _ in range(NST)]
            spare = hT.rearrange("p k n -> p (k n)")
            VW = TB * G * SLOT
            vst = [spare[:, r * VW:(r + 1) * VW].rearrange("p (t j s) -> p t j s", t=TB, j=G) for r in range(NST)]
            prob = [R.f32(S) for _ in range(PR)]
            osb = spare[:, NST * VW:NST * VW + S]
            m2 = R.f32(G * TB * 2).rearrange("p (j t a) -> p j t a", j=G, a=2)
            mx = R.f32(G * TB).rearrange("p (j t) -> p j t", j=G)
            mh = R.bf16(2 * G * TB)
            mhl = mh.rearrange("p (c j t) -> p c j t", c=2, j=G)
            mT = R.bf16(P)
            head_fills = fills(causal)
            unit_fills = [(j, *f) for j in range(G) for f in head_fills]
            NF = len(unit_fills)
            RING = NF + 2
            STEPS = G * TB
            score = [PS[:, 2:4, :].rearrange("p a n -> p (a n)"), PS[:, 4:6, :].rearrange("p a n -> p (a n)")]
            opsum = PS[:, 6:8, :].rearrange("p a n -> p (a n)")
            assert RING % 2 == 0

            def load(sp, u, r, n):
                if not (isinstance(n, int) and n == 0):
                    sp.wait_ge(sem(s + "_pv"), (u - NST) * TB + TB)
                for slot in range(NSLOT):
                    for st, qk, part in ((qst, 0, QUERY_PARTS[slot]), (kst, 1, KEY_PARTS[slot])):
                        sp.dma_start(st[r][slot * HD:(slot + 1) * HD],
                                     parts_dram[l][qk, part].rearrange("(u j d) t -> u d j t", j=G, d=HD)[u]
                                     ).then_inc(sem(f"{s}_in{r}"), 16)
                sp.dma_start(vst[r].rearrange("p t j s -> p (t j s)"),
                             v_dram[l].rearrange("u p t n -> u p (t n)")[u]).then_inc(sem(f"{s}_in{r}"), 16)

            IN = 16 * (2 * NSLOT + 1)

            def store_maxima(sp, u, r):
                sp.wait_ge(sem(s + "_mT"), u + 1)
                sp.dma_start(qst[r][KS:KM], mT[0:2 * G * TB]).then_inc(sem(s + "_rows"), 16)

            def store_out(sp, u):
                sp.wait_ge(sem(s + "_o"), u + 1)
                for j in range(G):
                    sp.dma_start(o_dram[l].rearrange("(u j d) t -> u j d t", j=G, d=HD)[u, j],
                                 osb[SLOT * j:SLOT * j + HD]).then_inc(sem(s + "_ost"), 16)
                    sp.dma_start(sum_dram[l].rearrange("(u j a) t -> u j (a t)", u=NU, j=G)[u, j:j + 1],
                                 osb[SLOT * j + HD:SLOT * j + HD + 1]).then_inc(sem(s + "_ost"), 16)

            @block.sync
            def _(sp):
                sp.wait_ge(sem(q + "_parts"), PARTS_ST)
                for r in range(2):
                    sp.wait_ge(sem(f"{q}_vst{r}"), 16 * T // 2)
                for u in range(NST):
                    load(sp, u, u, 0)
                sp.wait_ge(sem(s + "_ones"), NST)
                store_maxima(sp, 0, 0)

                def unit(u, r, last=False, loads=True):
                    if not last:
                        store_maxima(sp, u + 1, (r + 1) % NST)
                    store_out(sp, u)
                    if loads:
                        load(sp, u + NST, r, 1)

                with sp.Fori(0, 1) as i:
                    for r in range(NST):
                        unit(i * NST + r, r)
                unit(3, 0)
                unit(4, 1)
                unit(5, 2, loads=False)
                unit(6, 0, loads=False)
                unit(7, 1, last=True, loads=False)

            def pass1(pe, u, r, f):
                n = u * RING + f
                if not (isinstance(u, int) and u == 0 and f < 2):
                    pe.wait_ge(sem(s + "_red"), n - 1)
                if f < NF:
                    j, i, kb, w = unit_fills[f]
                    diag = causal and kb == i * P // BANK
                    mm = pe.matmul(PS[:, f % 2, 0:w], qst[r][0:KS, j, i * P:(i + 1) * P],
                                   kst[r][0:KS, j, kb * BANK:kb * BANK + w], start=True, stop=not diag)
                    if diag:
                        mm = pe.matmul(PS[:, f % 2, w - P:w], identb, future, start=False, stop=True)
                elif f == NF:
                    pe.wait_ge(sem(s + "_mh"), u + 1)
                    mm = pe.transpose(PS[0:2 * G * TB, 0, 0:P // 2].bitcast(BF16), mh, identb)
                mm.then_inc(sem(s + "_fill"), 1)

            def pass2(pe, u, r, st):
                kt, j = st // G, st % G
                n = u * STEPS + st
                if not (isinstance(u, int) and u == 0 and st < 2):
                    pe.wait_ge(sem(s + "_exp"), n - 1)
                lo = kt * P if causal else 0
                for bank in range(2):
                    c0, c1 = max(lo, bank * BANK), (bank + 1) * BANK
                    if c0 >= c1:
                        continue
                    diag = causal and c0 == lo
                    mm = pe.matmul(score[st % 2][:, c0:c1], kst[r][0:KM, j, kt * P:(kt + 1) * P],
                                   qst[r][0:KM, j, c0:c1], start=True, stop=not diag)
                    if diag:
                        mm = pe.matmul(score[st % 2][:, lo:lo + P], identb, futureT, start=False, stop=True)
                mm.then_inc(sem(s + "_sc"), 1)

            def pv(pe, u, r, kt):
                pe.wait_ge(sem(s + "_exp"), u * STEPS + (kt + 1) * G)
                if kt == 0 and not (isinstance(u, int) and u == 0):
                    pe.wait_ge(sem(s + "_o"), u)
                lo = kt * P if causal else 0
                for bank in range(2):
                    c0, c1 = max(lo, bank * BANK), (bank + 1) * BANK
                    if c0 >= c1:
                        continue
                    lastk = TB - 1 if not causal or bank == 1 else BANK // P - 1
                    for j in range(G):
                        mm = pe.matmul(opsum[SLOT * j:SLOT * (j + 1), c0:c1], vst[r][:, kt, j, :],
                                       prob[(kt * G + j) % PR][:, c0:c1], start=(kt == 0), stop=(kt == lastk))
                mm.then_inc(sem(s + "_pv"), 1)

            @block.tensor
            def _(pe):
                pe.wait_ge(sem("const"), CONST)
                pe.wait_ge(sem(s + "_in0"), IN)
                for f in range(RING - 1):
                    pass1(pe, 0, 0, f)
                pe.nop().then_inc(sem(s + "_fill"), 1)

                def unit(u, r, n, n1, last=False):
                    pe.wait_ge(sem(s + "_rows"), (u + 1) * 16)
                    if not last:
                        pe.wait_ge(sem(f"{s}_in{(r + 1) % NST}"), n1)
                    f, DONE = 0, STEPS - 5
                    for st in range(STEPS):
                        upto = min(NF, (st + 1) * NF // DONE + 1)
                        while not last and f < upto:
                            pass1(pe, u + 1, (r + 1) % NST, f)
                            f += 1
                        pass2(pe, u, r, st)
                        if st % G == 1 and st > G:
                            pv(pe, u, r, st // G - 1)
                        if not last and st == STEPS - 3:
                            pass1(pe, u + 1, (r + 1) % NST, NF)
                            pe.nop().then_inc(sem(s + "_fill"), 1)
                    pv(pe, u, r, TB - 1)

                with pe.Fori(0, 1) as i:
                    for r in range(NST):
                        unit(i * NST + r, r, None, IN * (i + 1 if r < NST - 1 else i + 2))
                unit(3, 0, None, IN * 2)
                unit(4, 1, None, IN * 2)
                unit(5, 2, None, IN * 3)
                unit(6, 0, None, IN * 3)
                unit(7, 1, None, None, last=True)

            @block.scalar
            def _(act):
                def unit(u):
                    for st in range(STEPS):
                        kt = st // G
                        n = u * STEPS + st
                        act.wait_ge(sem(s + "_sc"), n + 1)
                        first = isinstance(u, int) and u == 0
                        if not (first and kt < 2):
                            act.wait_ge(sem(s + "_pv"), u * TB + kt - 1)
                        lo = kt * P if causal else 0
                        act.activation(prob[st % PR][:, lo:S], score[st % 2][:, lo:S], ACT.Exp,
                                       scale=SCALE).then_inc(sem(s + "_exp"), 1)

                unit(0)
                with act.Fori(1, NU) as u:
                    unit(u)

            @block.vector
            def _(dve):
                dve.wait_ge(sem(q + "_parts"), PARTS_ST)
                for r in range(2):
                    dve.wait_ge(sem(f"{q}_vst{r}"), 16 * T // 2)
                for r in range(NST):
                    for st in (kst, ):
                        dve.memset(st[r][KS:KM].rearrange("p j t -> p (j t)"), 1.0).then_inc(sem(s + "_ones"), 1)
                dve.memset(m2.rearrange("p j t a -> p (j t a)"), LOWEST).then_inc(sem(s + "_m2"), 1)
                dve.wait_ge(sem(s + "_m2"), 1)

                def maxima(u):
                    for f in range(NF):
                        j, i, kb, w = unit_fills[f]
                        dve.wait_ge(sem(s + "_fill"), u * RING + f + 1)
                        dve.tensor_reduce(m2[:, j, i, kb:kb + 1], PS[:, f % 2, 0:w], AX.X, ALU.max).then_inc(sem(s + "_red"), 1)
                    dve.wait_ge(sem(s + "_red"), u * RING + NF)
                    dve.tensor_tensor(mx, m2[:, :, :, 0], m2[:, :, :, 1], ALU.max).then_inc(sem(s + "_mx"), 1)
                    dve.wait_ge(sem(s + "_mx"), u + 1)
                    dve.tensor_scalar(mhl[:, 0], mx, -1.0, None, ALU.mult).then_inc(sem(s + "_mhi"), 1)
                    dve.wait_ge(sem(s + "_mhi"), u + 1)
                    dve.scalar_tensor_tensor(out=mhl[:, 1], in0=mx, scalar=-1.0, in1=mhl[:, 0], op0=ALU.mult,
                                             op1=ALU.subtract).then_inc(sem(s + "_mh"), 1)
                    dve.wait_ge(sem(s + "_fill"), u * RING + NF + 2)
                    if not (isinstance(u, int) and u == 0):
                        dve.wait_ge(sem(s + "_rows"), 16 * u)
                    dve.tensor_copy(mT[0:2 * G * TB], PS[0:2 * G * TB, 0, 0:P // 2].bitcast(BF16)).then_inc(sem(s + "_mT"), 1)
                    dve.wait_ge(sem(s + "_mT"), u + 1)
                    dve.nop().then_inc(sem(s + "_red"), 2)

                def evacuate(u):
                    dve.wait_ge(sem(s + "_pv"), (u + 1) * TB)
                    if not (isinstance(u, int) and u == 0):
                        dve.wait_ge(sem(s + "_ost"), u * 16 * 2 * G)
                    dve.tensor_copy(osb, opsum).then_inc(sem(s + "_o"), 1)

                maxima(0)
                maxima(1)
                evacuate(0)
                with dve.Fori(1, NU - 1) as u:
                    maxima(u + 1)
                    evacuate(u)
                evacuate(NU - 1)

        def project(block, l):
            s, at, lns = f"p{l}", f"a{l}", ("ln0", "ln3")[l]
            R.at = work_mark
            sm = R.f32(B * P).rearrange("p (b t) -> p b t", b=B)
            OT = R.f32(B * KD * S).rearrange("p (c t) -> p c t", c=B * KD)
            RB = R.f32(B * KD * S).rearrange("p (c t) -> p c t", c=B * KD)

            @block.sync
            def _(sp):
                sp.wait_ge(sem(at + "_ost"), NU * 16 * 2 * G)
                sp.wait_ge(sem(at + "_pv"), NU * TB)
                sp.dma_start(sm, sum_dram[l].rearrange("(b p) t -> p b t", p=P)).then_inc(sem(s + "_sm"), 16)
                sp.dma_start(OT, o_dram[l].rearrange("(c p) t -> p c t", p=P)).then_inc(sem(s + "_ot"), 16)
                sp.wait_ge(sem(s + "_rec"), 1)
                sp.dma_start(rec_dram[l].rearrange("(b h) (a t) -> (b h a) t", b=B, a=8).rearrange("(b p) t -> p b t", p=P),
                             sm).then_inc(sem(s + "_recst"), 16)
                sp.wait_ge(sem(s + "_recst"), 16)
                for c in range(B * KD):
                    for j in range(8):
                        sp.dma_start(RB[j * HD:(j + 1) * HD, c, :],
                                     rec_dram[l][c * 8 + j, :].partition_broadcast(HD)).then_inc(sem(f"{s}_rb{c}"), 16)

            @block.vector
            def _(dve):
                dve.wait_ge(sem(s + "_sm"), 16)
                dve.reciprocal(sm, sm).then_inc(sem(s + "_rec"), 1)
                dve.wait_ge(sem(s + "_ot"), 16)
                for c in range(B * KD):
                    dve.wait_ge(sem(f"{s}_rb{c}"), 16 * 8)
                    dve.tensor_tensor(OT[:, c, :], OT[:, c, :], RB[:, c, :], ALU.mult).then_inc(sem(s + "_on"), 1)
                dve.wait_ge(sem(lns + "_xb"), 1)
                for t in range(T):
                    dve.wait_ge(sem(s + "_y"), t + 1)
                    dve.tensor_tensor(x[:, t, :], x[:, t, :], PS[:, t % 2, 0:D], ALU.add).then_inc(sem(s + "_x"), 1)

            @block.tensor
            def _(pe):
                for t in range(T):
                    b = t // TB
                    pe.wait_ge(sem(s + "_on"), (b + 1) * KD)
                    if t >= 2:
                        pe.wait_ge(sem(s + "_x"), t - 1)
                    if t == 0:
                        pe.wait_ge(sem("w_in"), W_IN)
                    for k in range(KD):
                        mm = pe.matmul(PS[:, t % 2, 0:D], OT[:, b * KD + k, (t % TB) * P:(t % TB + 1) * P],
                                       w_out[l][:, k, :], start=(k == 0), stop=(k == KD - 1))
                    mm.then_inc(sem(s + "_y"), 1)

        def cross(block, l, top):
            s, lns = f"x{l}", ("ln1", "ln4")[l]
            R.at = work_mark
            cell = R.f32(2 * 10).rearrange("p (r n) -> p r n", r=2)
            qt = [R.f32(KD * P).rearrange("p (k n) -> p k n", k=KD) for _ in range(2)]
            sc = [R.f32(NH * C).rearrange("p (h c) -> p h c", h=NH) for _ in range(2)]
            ex = [R.f32(NH * C).rearrange("p (h c) -> p h c", h=NH) for _ in range(2)]
            left = [R.f32(NH * C).rearrange("p (h c) -> p h c", h=NH) for _ in range(2)] if top else None
            m8 = [R.f32(NH * 8 * 4).rearrange("p (r h e) -> p r h e", r=4, h=NH) for _ in range(2)]
            rs = [R.f32(NH) for _ in range(2)]
            wT = [R.f32(NH * P).rearrange("p (h n) -> p h n", h=NH) for _ in range(2)]
            ot = [R.f32(NG * P).rearrange("p (g n) -> p g n", g=NG) for _ in range(2)]
            cx = [R.f32(D) for _ in range(2)]
            ct = [R.f32(KD * P).rearrange("p (k n) -> p k n", k=KD) for _ in range(2)]
            if l == 1:
                z_dram = scratch("z", [B, NH, TB, P, HD])
                z = R.f32(T * D).rearrange("p (t d) -> p t d", t=T)
            GROUPS = ((0, 6, 0, 0), (6, 2, 1, 0), (8, 4, 1, 2 * C), (12, 4, 2, 0))
            OUTS = ((0, 0, 2, 6 * C), (12 * C, 2, 1, 4 * C))
            QB, WB, OB, TB7 = 3, 4, 6, 7
            NLAG = 2 if top else 3

            def late(v):
                return not isinstance(v, int) or v > 0

            def inside(t):
                return not isinstance(t, int) or 0 <= t < T

            def each(body):
                def run(eng):
                    for t in range(-1, 4):
                        body(eng, t, t % 2)
                    with eng.Fori(2, 7) as i:
                        body(eng, i * 2, 0)
                        body(eng, i * 2 + 1, 1)
                    for t in range(14, T + 3):
                        body(eng, t, t % 2)
                return run

            @block.tensor
            def _(pe):
                pe.wait_ge(sem(lns + "_hT"), T)
                pe.wait_ge(sem("kblk"), 4 * B)
                pe.wait_ge(sem("xv"), 2 * B)

                def query(t, r):
                    if late(t - 4) and l == 0:
                        pe.wait_ge(sem(s + "_xd"), t - 4)
                    if late(t):
                        pe.wait_ge(sem(s + "_qt"), t * KD)
                    for half in range(KD):
                        for k in range(KD):
                            mm = pe.matmul(PS[:, QB, half * P:(half + 1) * P], xwqT[l][:, k, half * P:(half + 1) * P],
                                           hT[:, k, t * P:(t + 1) * P], start=(k == 0), stop=(k == KD - 1))
                    mm.then_inc(sem(s + "_q"), 1)

                def scores(t, r, b):
                    pe.wait_ge(sem(s + "_qt"), t * KD + KD)
                    if late(t):
                        pe.wait_ge(sem(s + "_scout"), t * 2)
                    for h0, hn, bank, col in GROUPS:
                        kb = kblk[l][:, b, h0 // 8, h0 % 8:h0 % 8 + hn, :]
                        mm = pe.matmul(PS[:, bank, col:col + hn * C], qt[r][:, h0 // 8, :],
                                       kb.rearrange("p j c -> p (j c)"), start=True, stop=True)
                    mm.then_inc(sem(s + "_s"), 1)

                def turn_weights(t, r, c):
                    if c == 0:
                        pe.wait_ge(sem(s + "_w"), t + 1)
                    if late(t * 4 + c - 1):
                        pe.wait_ge(sem(s + "_wt"), t * 4 + c - 1)
                    for j in range(4):
                        mm = pe.transpose(PS[0:C, WB + c % 2, j * P:(j + 1) * P], ex[r][:, c * 4 + j, :], ident)
                    mm.then_inc(sem(s + "_wtp"), 1)

                def context(t, r, b):
                    pe.wait_ge(sem(s + "_wt"), t * 4 + 4)
                    if late(t):
                        pe.wait_ge(sem(s + "_ot"), t)
                    for g in range(NG):
                        for j in range(G):
                            mm = pe.matmul(PS[SLOT * j:SLOT * (j + 1), OB, g * P:(g + 1) * P], xv[l][0:C, b, g * G + j, :],
                                           wT[r][0:C, g * G + j, :], start=True, stop=True)
                    mm.then_inc(sem(s + "_op"), 1)

                def turn_context(t, r):
                    pe.wait_ge(sem(s + "_ot"), t + 1)
                    if late(t):
                        pe.wait_ge(sem(s + "_n"), t)
                    for g in range(NG):
                        mm = pe.transpose(PS[:, TB7, g * P:(g + 1) * P], ot[r][:, g, :], ident)
                    mm.then_inc(sem(s + "_otp"), 1)

                def output(t, r):
                    pe.wait_ge(sem(s + "_n"), t + 1)
                    if late(t):
                        pe.wait_ge(sem(s + "_xd"), t)
                    if late(min(t + 5, T) * KD):
                        pe.wait_ge(sem(s + "_qt"), min(t + 5, T) * KD)
                    for k in range(KD):
                        mm = pe.transpose(PS[:, QB, k * P:(k + 1) * P], cx[r][:, k * P:(k + 1) * P], ident)
                    mm.then_inc(sem(s + "_ctp"), 1)
                    pe.wait_ge(sem(s + "_ct"), t + 1)
                    for k in range(KD):
                        mm = pe.matmul(PS[:, QB, D:2 * D], ct[r][:, k, :], xwo[:, k, :], start=(k == 0), stop=(k == KD - 1))
                    mm.then_inc(sem(s + "_y"), 1)

                for t in range(-1, T + 3):
                    r, o = t % 2, (t + 1) % 2
                    if inside(t + 1):
                        query(t + 1, o)
                    if inside(t - 1):
                        turn_weights(t - 1, o, 0)
                        turn_weights(t - 1, o, 1)
                    if inside(t + 1):
                        scores(t + 1, o, (t + 1) // TB)
                    if inside(t - 1):
                        turn_weights(t - 1, o, 2)
                        turn_weights(t - 1, o, 3)
                        context(t - 1, o, (t - 1) // TB)
                    if inside(t - 2):
                        turn_context(t - 2, r)
                    if inside(t - 3) and l == 0:
                        output(t - 3, o)

            @block.scalar
            def _(act):
                def queries(t, r):
                    act.wait_ge(sem(s + "_q"), t + 1)
                    for half in range(KD):
                        act.activation(qt[r][:, half, :], PS[:, QB, half * P:(half + 1) * P], ACT.Identity,
                                       bias=xq_b[l][:, half:half + 1]).then_inc(sem(s + "_qt"), 1)

                def copy_weights(t, r, c):
                    act.wait_ge(sem(s + "_wtp"), t * 4 + c + 1)
                    if late(t - 1):
                        act.wait_ge(sem(s + "_op"), t - 1)
                    act.copy(wT[r][0:C, c * 4:c * 4 + 4, :], PS[0:C, WB + c % 2, :].rearrange("p (j n) -> p j n", j=4)
                             ).then_inc(sem(s + "_wt"), 1)

                def body(act, t, r):
                    o = 1 - r
                    if top and inside(t - 1):
                        act.wait_ge(sem(s + "_d2"), t)
                        act.activation(left[o], left[o], ACT.Exp, scale=SCALE).then_inc(sem(s + "_e2"), 1)
                    if inside(t + 1):
                        queries(t + 1, o)
                    if inside(t - 1):
                        copy_weights(t - 1, o, 0)
                        copy_weights(t - 1, o, 1)
                    if top and inside(t + 1):
                        act.wait_ge(sem(s + "_s"), t + 2)
                        if late(t):
                            act.wait_ge(sem(s + "_d"), t)
                            act.wait_ge(sem(s + "_k0"), t * NH)
                        for c0, bank, nb, w in OUTS:
                            act.copy(sc[o].rearrange("p h c -> p (h c)")[:, c0:c0 + nb * w].rearrange("p (a n) -> p a n", a=nb),
                                     PS[:, bank:bank + nb, 0:w]).then_inc(sem(s + "_scout"), 1)
                    if inside(t - 1):
                        copy_weights(t - 1, o, 2)
                        copy_weights(t - 1, o, 3)
                    if inside(t):
                        act.wait_ge(sem(s + "_d"), t + 1)
                        act.activation(ex[r], ex[r], ACT.Exp, scale=SCALE if top else 1.0).then_inc(sem(s + "_e"), 1)
                    if inside(t - 1):
                        act.wait_ge(sem(s + "_op"), t)
                        if late(t - 2):
                            act.wait_ge(sem(s + "_otp"), t - 2)
                        act.copy(ot[o], PS[:, OB, :].rearrange("p (g n) -> p g n", g=NG)).then_inc(sem(s + "_ot"), 1)
                    if l == 0 and inside(t - 3):
                        act.wait_ge(sem(s + "_ctp"), t - 2)
                        if late(t - 4):
                            act.wait_ge(sem(s + "_y"), t - 4)
                        act.copy(ct[o], PS[:, QB, 0:D].rearrange("p (k n) -> p k n", k=KD)).then_inc(sem(s + "_ct"), 1)
                each(body)(act)

            @block.gpsimd
            def _(pool):
                def less_max(dst, src, r):
                    return pool.tensor_tensor(dst, src, m8[r][:, 0, :, 0:1].to_broadcast([P, NH, C]), ALU.subtract)

                def body(pool, t, r):
                    o = 1 - r
                    if top and inside(t - 1):
                        pool.wait_ge(sem(s + "_topped"), t * NH)
                        less_max(left[o], left[o], o).then_inc(sem(s + "_d2"), 1)
                        pool.wait_ge(sem(s + "_e2"), t)
                        pool.wait_ge(sem(s + "_e"), t)
                        pool.tensor_tensor(ex[o], ex[o], left[o], ALU.subtract).then_inc(sem(s + "_w"), 1)
                    if inside(t):
                        pool.wait_ge(sem(s + "_m"), (t + 1) * (NH if top else 1))
                        if late(t - 1):
                            pool.wait_ge(sem(s + "_wtp"), (t - 1) * 4)
                        less_max(ex[r], sc[r], r).then_inc(sem(s + "_d"), 1)
                each(body)(pool)

            @block.vector
            def _(dve):
                if l == 0:
                    dve.wait_ge(sem("ln1_xb"), 1)
                else:
                    dve.wait_ge(sem(lns + "_h"), T)

                def largest(t, r):
                    hn = t * NH
                    dve.wait_ge(sem(s + "_scout"), t * 2 + 2)
                    dve.memset(cell[:, r, 8:9], 0.0)
                    if late(t - 1):
                        dve.wait_ge(sem(s + "_w"), t - 1)
                        dve.memset(cell[:, r, 9:10], 0.0)
                    for k in range(4):
                        if k:
                            dve.wait_ge(sem(f"{s}_k{k - 1}"), hn + NH)
                            dve.memset(cell[:, r, 2 * k:2 * k + 1], 0.0)
                        for hd in range(NH):
                            src = (sc if k == 0 else left)[r][:, hd, :]
                            dve.max(m8[r][:, k, hd, :], src).then_inc(sem(s + "_m" if k == 0 else f"{s}_m{k}"), 1)
                        dve.wait_ge(sem(s + "_m" if k == 0 else f"{s}_m{k}"), hn + NH)
                        dve.memset(cell[:, r, 2 * k + 1:2 * k + 2], 0.0)
                        for hd in range(NH):
                            src = (sc if k == 0 else left)[r][:, hd, :]
                            dve.match_replace(out=left[r][:, hd, :], in_to_replace=m8[r][:, k, hd, :], in_values=src,
                                              imm_value=LOWEST).then_inc(sem(f"{s}_k{k}" if k < 3 else s + "_topped"), 1)

                def maxima(t, r):
                    dve.wait_ge(sem(s + "_s"), t + 1)
                    if late(t - 1):
                        dve.wait_ge(sem(s + "_d"), t - 1)
                    for c0, bank, nb, w in OUTS:
                        dve.tensor_scalar(sc[r].rearrange("p h c -> p (h c)")[:, c0:c0 + nb * w].rearrange("p (a n) -> p a n", a=nb),
                                          PS[:, bank:bank + nb, 0:w], -3.4028234e38, None, ALU.max).then_inc(sem(s + "_scout"), 1)
                    dve.wait_ge(sem(s + "_scout"), t * 2 + 2)
                    dve.tensor_reduce(m8[r][:, 0, :, 0], sc[r], AX.X, ALU.max).then_inc(sem(s + "_m"), 1)

                def normalize(t, r):
                    o = PS[:, TB7, :].rearrange("p (h s) -> p h s", h=NH)
                    dve.wait_ge(sem(s + "_otp"), t + 1)
                    dve.tensor_scalar(rs[r], o[:, :, HD], 1e-30, None, ALU.max).then_inc(sem(s + "_sum"), 1)
                    dve.wait_ge(sem(s + "_sum"), t + 1)
                    dve.reciprocal(rs[r], rs[r]).then_inc(sem(s + "_rs"), 1)
                    dve.wait_ge(sem(s + "_rs"), t + 1)
                    if late(t - 1):
                        if l == 0:
                            dve.wait_ge(sem(s + "_ctp"), t - 1)
                        else:
                            dve.wait_ge(sem(f"{s}_zst{r}"), (t - r) * 8)
                    dve.tensor_tensor(cx[r].rearrange("p (h d) -> p h d", h=NH), o[:, :, 0:HD],
                                      rs[r].unsqueeze(2).to_broadcast([P, NH, HD]), ALU.mult).then_inc(sem(s + "_n"), 1)

                def body(dve, t, r):
                    o = 1 - r
                    if inside(t):
                        if top:
                            largest(t, r)
                        else:
                            maxima(t, r)
                    if inside(t - NLAG):
                        normalize(t - NLAG, r if NLAG == 2 else o)
                    if not top and inside(t):
                        dve.wait_ge(sem(s + "_e"), t + 1)
                        dve.tensor_scalar(ex[r], ex[r], 0.0, None, ALU.max).then_inc(sem(s + "_w"), 1)
                    if l == 0 and inside(t - 3):
                        dve.wait_ge(sem(s + "_y"), t - 2)
                        row = x[:, t - 3, :] if isinstance(t, int) else x[:, bass.ds(t - 3, 1), :].rearrange("p a d -> p (a d)")
                        dve.tensor_tensor(row, row, PS[:, QB, D:2 * D], ALU.add).then_inc(sem(s + "_xd"), 1)
                each(body)(dve)

            if l == 1:
                @block.sync
                def _(sp):
                    def store(t, r):
                        sp.wait_ge(sem(s + "_n"), t + 1)
                        sp.dma_start(z_dram[b].rearrange("h t p d -> t p h d")[t - b * TB],
                                     cx[r].rearrange("p (h d) -> p h d", h=NH)).then_inc(sem(f"{s}_zst{r}"), 16)

                    for b in range(B):
                        with sp.Fori(b * TB // 2, (b + 1) * TB // 2) as i:
                            store(i * 2, 0)
                            store(i * 2 + 1, 1)
                        for r in range(2):
                            sp.wait_ge(sem(f"{s}_zst{r}"), 16 * (b + 1) * TB // 2)
                        sp.dma_start(z[:, b * TB:(b + 1) * TB, :],
                                     z_dram[b].rearrange("h t p d -> (h t p d)").rearrange("(t p d) -> p t d", t=TB, p=P)
                                     ).then_inc(sem(f"{s}_z{b}"), 16)

                @block.vector
                def _(dve):
                    for b in range(B):
                        dve.wait_ge(sem(f"{s}_z{b}"), 16)
                        for t in range(b * TB, (b + 1) * TB):
                            dve.tensor_tensor(h[:, t, :], h[:, t, :], z[:, t, :], ALU.add).then_inc(sem(s + "_hz"), 1)
                    dve.wait_ge(sem(s + "_hz"), T)
                    for t in range(T):
                        dve.bn_stats(stats[:, t, :], h[:, t, :]).then_inc(sem(s + "_st2"), 1)
                    for t in range(T):
                        dve.wait_ge(sem(s + "_st2"), t + 1)
                        dve.bn_aggr(mv[:, t, :], stats[:, t, :]).then_inc(sem(s + "_mv2"), 1)
                    dve.wait_ge(sem(s + "_mv2"), T)
                    dve.tensor_scalar(std, mv[:, :, 1], LN_EPS, None, ALU.add).then_inc(sem(s + "_var2"), 1)
                    dve.wait_ge(sem(s + "_std2"), 1)
                    dve.reciprocal(rstd, std).then_inc(sem(s + "_rstd2"), 1)
                    dve.wait_ge(sem(s + "_rstd2"), 1)
                    for t in range(T):
                        dve.tensor_scalar(h[:, t, :], h[:, t, :], mv[:, t, 0:1], rstd[:, t:t + 1], ALU.subtract,
                                          ALU.mult).then_inc(sem(s + "_n2"), 1)
                    for t in range(T):
                        dve.wait_ge(sem(s + "_gb"), t + 1)
                        dve.tensor_tensor(x[:, t, :], x[:, t, :], h[:, t, :], ALU.add).then_inc(sem(s + "_x2"), 1)

                @block.scalar
                def _(act):
                    act.wait_ge(sem(s + "_var2"), 1)
                    act.activation(std, std, ACT.Sqrt).then_inc(sem(s + "_std2"), 1)

                @block.gpsimd
                def _(pool):
                    for t in range(T):
                        pool.wait_ge(sem(s + "_n2"), t + 1)
                        pool.tensor_tensor(h[:, t, :], h[:, t, :], gamma, ALU.mult).then_inc(sem(s + "_g2"), 1)
                        pool.wait_ge(sem(s + "_g2"), t + 1)
                        pool.tensor_tensor(h[:, t, :], h[:, t, :], beta, ALU.add).then_inc(sem(s + "_gb"), 1)

        def moe(block, l, free_sem, free_val):
            s, lns = f"e{l}", ("ln2", "ln5")[l]
            big = l == 1
            R.at = base_mark if big else work_mark
            wr = R.f32(KD * E).rearrange("p (k e) -> p k e", k=KD)
            br = R.f32(E)
            lg = R.f32(T * E).rearrange("p (t e) -> p t e", t=T)
            oh = R.f32(T * E).rearrange("p (t e) -> p t e", t=T)
            ohb = R.bf16(T * E).rearrange("p (t e) -> p t e", t=T)
            ta = R.f32(T * E).rearrange("p (t e) -> p t e", t=T)
            tb = R.f32(T * E).rearrange("p (t e) -> p t e", t=T)
            tot = R.f32(T * E).rearrange("p (t e) -> p t e", t=T)
            c1, c2, c3 = R.f32(E), R.f32(E), R.f32(E)
            nt = R.f32(E)
            cmp1 = R.f32(24 * T).rearrange("p (e j) -> p e j", e=24)
            m1, gate, posf = R.f32(T), R.f32(T), R.f32(T)
            posi = R.f32(T).bitcast(I32)
            eidf = R.f32(24)
            eid = R.f32(24).bitcast(I32)
            NB1 = E * F if big else E * D
            bias_raw = R.f32(NB1 // P)
            bias_part = [R.bf16(NB1 // P) for _ in range(NPART)]
            bias2_raw = R.f32(E * D // P)
            bias2_part = [R.bf16(E * D // P) for _ in range(NPART)]
            b1 = hT.rearrange("p k n -> p (k n)").bitcast(BF16)[0:NPART, 0:NB1]
            b2 = R.bf16(E * D)[0:NPART]
            yb = [R.f32(D) for _ in range(NTB)]
            NY = 4
            yg = [R.f32(D) for _ in range(NY)]
            H = Region(h.rearrange("p t d -> p (t d)"), T * D)
            xs = [H.f32(D) for _ in range(NTB)]
            xsT = [H.f32(KD * P).rearrange("p (k n) -> p k n", k=KD) for _ in range(NTB)]
            if big:
                h1 = H.f32(F)
                h1T = H.f32(F).rearrange("p (k n) -> p k n", k=KF)
                W1 = R.f32(E * KD * F)
                W2 = R.f32(E * KF * D)
            else:
                raw = R.f32(E * KD * D).rearrange("p (e k n) -> p e k n", e=E, k=KD)
                WeT = R.f32(E * KD * D)
                wr_raw = R.f32(D)
            bias_names = (("L1_ffn_b1", bias_raw, bias_part, b1, NB1), ("L1_ffn_b2", bias2_raw, bias2_part, b2, E * D)) \
                if big else (("L0_ffn_expert_b", bias_raw, bias_part, b1, NB1),)
            bias_rows = [scratch(f"bias{l}{i}", [NPART, n], BF16) for i, (_, _, _, _, n) in enumerate(bias_names)]

            @block.sync
            def _(sp):
                sp.wait_ge(sem(free_sem), free_val)

                def load(dst, src):
                    sp.dma_start(dst, src).then_inc(sem(s + "_win"), 16)
                for name, raw_b, _, _, n in bias_names:
                    load(raw_b, a[name].rearrange("(o e) f -> o (e f)", o=1).rearrange("o (p n) -> p (o n)", p=P))
                if big:
                    load(wr, a["L1_ffn_Wr"].rearrange("(k p) e -> p k e", p=P))
                    load(br, a["L1_ffn_br"].partition_broadcast(P))
                    for e in range(E):
                        sp.dma_start(W1[:, e * KD * F:(e + 1) * KD * F].rearrange("p (k f) -> p k f", k=KD),
                                     a["L1_ffn_W1"][e].rearrange("(k p) f -> p k f", p=P)).then_inc(sem(s + "_wbig"), 16)
                        sp.dma_start(W2[:, e * KF * D:(e + 1) * KF * D].rearrange("p (k f) -> p k f", k=KF),
                                     a["L1_ffn_W2"][e].rearrange("(k p) f -> p k f", p=P)).then_inc(sem(s + "_wbig"), 16)
                else:
                    load(wr_raw[0:E], a["L0_ffn_router_w"])
                    load(br, a["L0_ffn_router_b"].partition_broadcast(P))
                    for e in range(E):
                        load(raw[:, e], a["L0_ffn_expert_w"][e].rearrange("(k p) n -> p k n", p=P))
                sp.wait_ge(sem(s + "_bparts"), len(bias_names) * NPART)
                for (_, _, parts, _, n), rows in zip(bias_names, bias_rows):
                    for i in range(NPART):
                        sp.dma_start(rows[i].rearrange("(p n) -> p n", p=P), parts[i]).then_inc(sem(s + "_bst"), 16)
                sp.wait_ge(sem(s + "_bst"), 16 * NPART * len(bias_names))
                sp.wait_ge(sem(s + "_lg"), 1)
                for (_, _, _, dst, n), rows in zip(bias_names, bias_rows):
                    sp.dma_start(dst, rows).then_inc(sem(s + "_brow"), 16)
            WIN = 16 * (4 if big else 3 + E)

            @block.tensor
            def _(pe):
                pe.wait_ge(sem(s + "_win"), WIN)
                if not big:
                    for k in range(KD):
                        mm = pe.transpose(PS[:, 2, k * E:(k + 1) * E], wr_raw[0:E, k * P:(k + 1) * P], ident[0:E, 0:E])
                    mm.then_inc(sem(s + "_wrp"), 1)
                    for e in range(E):
                        if e >= 2:
                            pe.wait_ge(sem(s + "_weT"), e - 1)
                        for ko in range(KD):
                            for ki in range(KD):
                                mm = pe.transpose(PS[:, 4 + e % 2, (ki * KD + ko) * P:(ki * KD + ko + 1) * P],
                                                  raw[:, e, ko, ki * P:(ki + 1) * P], ident)
                        mm.then_inc(sem(s + "_wep"), 1)
                    pe.wait_ge(sem(s + "_wr"), 1)
                for t in range(T):
                    if t == 0:
                        pe.wait_ge(sem(lns + "_hT"), T)
                    for k in range(KD):
                        mm = pe.matmul(PS[:, 3, t * E:(t + 1) * E], hT[:, k, t * P:(t + 1) * P], wr[:, k, :],
                                       start=(k == 0), stop=(k == KD - 1))
                mm.then_inc(sem(s + "_lg"), 1)
                pe.wait_ge(sem(s + "_oh"), 1)
                oh2 = ohb.rearrange("p t e -> p (t e)")
                pe.matmul(PS[:, 6, 0:T * E], upper, oh2, start=True, stop=True)
                pe.matmul(PS[:, 7, 0:T * E], onesb, oh2, start=True, stop=True).then_inc(sem(s + "_rank"), 1)

            if not big:
                @block.scalar
                def _(act):
                    for e in range(E):
                        act.wait_ge(sem(s + "_wep"), e + 1)
                        act.copy(WeT[:, e * KD * D:(e + 1) * KD * D], PS[:, 4 + e % 2, :]).then_inc(sem(s + "_weT"), 1)

            @block.scalar
            def _(act):
                act.wait_ge(sem(s + "_ld"), 1)
                act.activation(tb, ta, ACT.Exp).then_inc(sem(s + "_le"), 1)

            @block.vector
            def _(dve):
                n = [0, 0]

                def link(ins):
                    n[0] += 1
                    ins.then_inc(sem(s + "_chain"), 1)
                    dve.wait_ge(sem(s + "_chain"), n[0])

                dve.wait_ge(sem(s + "_win"), WIN)
                for _, raw_b, parts, _, _ in bias_names:
                    for i in range(NPART):
                        ins = dve.tensor_copy(parts[i], raw_b)
                        ins.then_inc(sem(s + "_bparts"), 1)
                        n[1] += 1
                        if i < NPART - 1:
                            dve.wait_ge(sem(s + "_bparts"), n[1])
                            link(dve.tensor_tensor(raw_b, raw_b, parts[i], ALU.subtract))
                if not big:
                    dve.wait_ge(sem(s + "_wrp"), 1)
                    dve.tensor_copy(wr, PS[:, 2, 0:KD * E].rearrange("p (k e) -> p k e", k=KD)).then_inc(sem(s + "_wr"), 1)
                dve.wait_ge(sem(s + "_lg"), 1)
                te = [P, T, E]
                link(dve.tensor_tensor(lg, PS[:, 3, 0:T * E].rearrange("p (t e) -> p t e", t=T),
                                       br.unsqueeze(1).to_broadcast(te), ALU.add))
                link(dve.tensor_reduce(m1, lg, AX.X, ALU.max))
                m1b = m1.unsqueeze(2).to_broadcast(te)
                dve.tensor_tensor(ta, lg, m1b, ALU.subtract).then_inc(sem(s + "_ld"), 1)
                link(dve.tensor_tensor(oh, lg, m1b, ALU.is_equal))
                link(dve.tensor_tensor(lg, oh, order.unsqueeze(1).to_broadcast(te), ALU.mult))
                link(dve.tensor_reduce(posf, lg, AX.X, ALU.max))
                link(dve.tensor_tensor(oh, lg, posf.unsqueeze(2).to_broadcast(te), ALU.is_equal))
                dve.tensor_copy(ohb, oh).then_inc(sem(s + "_oh"), 1)
                dve.wait_ge(sem(s + "_le"), 1)
                link(dve.tensor_reduce(m1, tb, AX.X, ALU.add))
                link(dve.reciprocal(gate, m1))
                dve.wait_ge(sem(s + "_rank"), 1)
                link(dve.tensor_copy(tot, PS[:, 7, 0:T * E].rearrange("p (t e) -> p t e", t=T)))
                cur, nxt = tot, ta
                d = 1
                while d < T:
                    dve.tensor_copy(nxt[:, 0:d, :], cur[:, 0:d, :]).then_inc(sem(s + "_chain"), 1)
                    n[0] += 1
                    link(dve.tensor_tensor(nxt[:, d:T, :], cur[:, d:T, :], cur[:, 0:T - d, :], ALU.add))
                    cur, nxt = nxt, (tb if nxt is ta else ta)
                    d *= 2
                total = cur[:, T - 1, :]
                link(dve.tensor_scalar(c1, total, 1.0 / P, None, ALU.mult))
                link(dve.tensor_tensor(cmp1[:, 0:E, :], c1.unsqueeze(2).to_broadcast([P, E, T]),
                                       count[:, 0:T].unsqueeze(1).to_broadcast([P, E, T]), ALU.is_gt))
                link(dve.tensor_reduce(nt, cmp1[:, 0:E, :], AX.X, ALU.add))
                a0, a1 = nt, c2
                d = 1
                while d < E:
                    dve.tensor_copy(a1[:, 0:d], a0[:, 0:d]).then_inc(sem(s + "_chain"), 1)
                    n[0] += 1
                    link(dve.tensor_tensor(a1[:, d:E], a0[:, d:E], a0[:, 0:E - d], ALU.add))
                    a0, a1 = a1, (c3 if a1 is c2 else c2)
                    d *= 2
                ends = a0
                link(dve.tensor_tensor(c1, ends, nt, ALU.subtract))
                link(dve.tensor_scalar(c1, c1, float(P), None, ALU.mult))
                link(dve.tensor_tensor(lg, cur, tot, ALU.subtract))
                link(dve.tensor_tensor(lg, lg, c1.unsqueeze(1).to_broadcast(te), ALU.add))
                link(dve.tensor_tensor(lg, lg, PS[:, 6, 0:T * E].rearrange("p (t e) -> p t e", t=T), ALU.add))
                link(dve.tensor_tensor(lg, lg, oh, ALU.mult))
                link(dve.tensor_reduce(posf, lg, AX.X, ALU.add))
                dve.tensor_copy(posi, posf).then_inc(sem(s + "_pos"), 1)
                ee = cmp1.rearrange("p e j -> p (e j)")[:, 0:24 * E].rearrange("p (s e) -> p s e", s=24)
                link(dve.tensor_tensor(ee, ends.unsqueeze(1).to_broadcast([P, 24, E]),
                                       count[:, 0:24].unsqueeze(2).to_broadcast([P, 24, E]), ALU.is_le))
                link(dve.tensor_reduce(eidf, ee, AX.X, ALU.add))
                link(dve.tensor_scalar(eidf, eidf, float(E - 1), None, ALU.min))
                dve.tensor_copy(eid, eidf).then_inc(sem(s + "_eid"), 1)

            @block.gpsimd
            def _(pool):
                pool.wait_ge(sem(s + "_pos"), 1)
                pool.wait_ge(sem("xs_clear"), 16 * 2 * -(-NS * D // 2048))
                pool.wait_ge(sem(lns + "_h"), T)
                for t in range(T):
                    pool.indirect_dma_start(
                        out=xs_dram[l], out_offset=bass.IndirectOffsetOnAxis(ap=posi[:, t:t + 1], axis=0),
                        in_=h[:, t, :], in_offset=None).then_inc(sem(s + "_sc"), 16)
                for r in range(NTB):
                    pool.wait_ge(sem(f"{s}_yst{r}"), 16 * len(range(r, NS, NTB)))
                for t in range(T):
                    if t >= NY:
                        pool.wait_ge(sem(s + "_x"), t - NY + 1)
                    pool.indirect_dma_start(
                        out=yg[t % NY], out_offset=None, in_=ys_dram[l],
                        in_offset=bass.IndirectOffsetOnAxis(ap=posi[:, t:t + 1], axis=0)).then_inc(sem(f"{s}_yg{t % NY}"), 16)

            TBANK = (0, 1, 0, 1) if big else (0, 1, 2, 3)
            YBANK = (6, 7, 6, 7) if big else (4, 5, 6, 7)
            BANKS = len(set(TBANK))

            def late(v):
                return not isinstance(v, int) or v > 0

            def inside(t):
                return not isinstance(t, int) or 0 <= t < NS

            def each(eng, body):
                for t in range(-2, NTB):
                    body(t, t % NTB)
                with eng.Fori(1, NS // NTB) as i:
                    for r in range(NTB):
                        body(i * NTB + r, r)
                for t in range(NS // NTB * NTB, NS):
                    body(t, t % NTB)

            def tile_rows(ap, t):
                return ap.rearrange("(s p) d -> s p d", p=P)[t]

            def expert(t):
                return eid[0:1, t:t + 1] if isinstance(t, int) else eid[0:1, bass.ds(t, 1)]

            @block.sync
            def _(sp):
                sp.wait_ge(sem(s + "_sc"), 16 * T)

                def load(t, r):
                    if late(t - NTB + 1):
                        sp.wait_ge(sem(s + "_tp"), t - NTB + 1)
                    sp.dma_start(xs[r], tile_rows(xs_dram[l], t)).then_inc(sem(f"{s}_xs{r}"), 16)

                def store(t, r):
                    sp.wait_ge(sem(s + "_yb"), t + 1)
                    sp.dma_start(tile_rows(ys_dram[l], t), yb[r]).then_inc(sem(f"{s}_yst{r}"), 16)

                AHEAD = NTB + 1
                for t in range(AHEAD):
                    load(t, t % NTB)
                for t in range(NTB):
                    load(t + AHEAD, (t + AHEAD) % NTB)
                    store(t, t)
                with sp.Fori(1, (NS - AHEAD) // NTB) as i:
                    for r in range(NTB):
                        load(i * NTB + r + AHEAD, (r + AHEAD) % NTB)
                        store(i * NTB + r, r)
                for t in range((NS - AHEAD) // NTB * NTB, NS):
                    if t + AHEAD < NS:
                        load(t + AHEAD, (t + AHEAD) % NTB)
                    store(t, t % NTB)

            @block.tensor
            def _(pe):
                pe.wait_ge(sem(s + "_eid"), 1)
                pe.wait_ge(sem(s + "_brow"), 16 * len(bias_names))
                if big:
                    pe.wait_ge(sem(s + "_wbig"), 16 * 2 * E)
                else:
                    pe.wait_ge(sem(s + "_weT"), E)

                def turn(t, r):
                    pe.wait_ge(sem(f"{s}_xs{r}"), (t - r) * (16 // NTB) + 16)
                    if late(t - BANKS + 1):
                        pe.wait_ge(sem(s + "_xT"), t - BANKS + 1)
                    for k in range(KD):
                        mm = pe.transpose(PS[:, TBANK[r], k * P:(k + 1) * P], xs[r][:, k * P:(k + 1) * P], ident)
                    mm.then_inc(sem(s + "_tp"), 1)

                def hidden(t, r):
                    e = pe.value_load(expert(t), min_val=0, max_val=E - 1)
                    pe.wait_ge(sem(s + "_xT"), t + 1)
                    if late(t):
                        pe.wait_ge(sem(s + "_h1"), t)
                    for half in range(2):
                        ps = PS[:, 2 + half, :]
                        for k in range(KD):
                            pe.matmul(ps, xsT[r][:, k, :], W1[:, bass.ds(e * (KD * F) + k * F + half * BANK, BANK)],
                                      start=(k == 0), stop=False)
                        mm = pe.matmul(ps, onesb[0:NPART, :], b1[:, bass.ds(e * F + half * BANK, BANK)], start=False, stop=True)
                    mm.then_inc(sem(s + "_h1p"), 1)

                def turn_hidden(t):
                    pe.wait_ge(sem(s + "_h1"), t + 1)
                    if late(t):
                        pe.wait_ge(sem(s + "_h1T"), t)
                    for k in range(KF):
                        mm = pe.transpose(PS[:, 4 + k // 4, (k % 4) * P:(k % 4 + 1) * P], h1[:, k * P:(k + 1) * P], ident)
                    mm.then_inc(sem(s + "_h1tp"), 1)

                def output(t, r):
                    e = pe.value_load(expert(t), min_val=0, max_val=E - 1)
                    if big:
                        pe.wait_ge(sem(s + "_h1T"), t + 1)
                        lhs, W, nk, b = h1T, W2, KF, b2
                    else:
                        pe.wait_ge(sem(s + "_xT"), t + 1)
                        lhs, W, nk, b = xsT[r], WeT, KD, b1
                    if late(t - BANKS + 1):
                        pe.wait_ge(sem(s + "_yb"), t - BANKS + 1)
                    ps = PS[:, YBANK[r], 0:D]
                    for k in range(nk):
                        pe.matmul(ps, lhs[:, k, :], W[:, bass.ds(e * (nk * D) + k * D, D)], start=(k == 0), stop=False)
                    pe.matmul(ps, onesb[0:NPART, :], b[:, bass.ds(e * D, D)], start=False, stop=True).then_inc(sem(s + "_y"), 1)

                def step(t, r):
                    if big and inside(t):
                        turn_hidden(t)
                    if inside(t + 2):
                        turn(t + 2, (r + 2) % NTB)
                    if big and inside(t + 1):
                        hidden(t + 1, (r + 1) % NTB)
                    if inside(t):
                        output(t, r)
                each(pe, step)

            @block.scalar
            def _(act):
                def step(t, r):
                    if inside(t + 2):
                        o = (r + 2) % NTB
                        act.wait_ge(sem(s + "_tp"), t + 3)
                        if late(t + 3 - NTB):
                            act.wait_ge(sem(s + ("_h1p" if big else "_y")), t + 3 - NTB)
                        act.copy(xsT[o], PS[:, TBANK[o], 0:KD * P].rearrange("p (k n) -> p k n", k=KD)).then_inc(sem(s + "_xT"), 1)
                    if big and inside(t + 1):
                        act.wait_ge(sem(s + "_h1p"), t + 2)
                        if late(t + 1):
                            act.wait_ge(sem(s + "_h1tp"), t + 1)
                        act.activation(h1.rearrange("p (a n) -> p a n", a=2), PS[:, 2:4, :], ACT.Relu).then_inc(sem(s + "_h1"), 1)
                    if big and inside(t):
                        act.wait_ge(sem(s + "_y"), t + 1)
                        if late(t - NTB + 1):
                            act.wait_ge(sem(f"{s}_yst{r}"), (t - r) * (16 // NTB))
                        act.copy(yb[r], PS[:, YBANK[r], 0:D]).then_inc(sem(s + "_yb"), 1)
                each(act, step)

            @block.vector
            def _(dve):
                def step(t, r):
                    if big and inside(t):
                        dve.wait_ge(sem(s + "_h1tp"), t + 1)
                        if late(t):
                            dve.wait_ge(sem(s + "_y"), t)
                        dve.tensor_copy(h1T.rearrange("p (a k) n -> p a (k n)", a=2), PS[:, 4:6, :]).then_inc(sem(s + "_h1T"), 1)
                    if not big and inside(t):
                        dve.wait_ge(sem(s + "_y"), t + 1)
                        if late(t - NTB + 1):
                            dve.wait_ge(sem(f"{s}_yst{r}"), (t - r) * (16 // NTB))
                        dve.tensor_copy(yb[r], PS[:, YBANK[r], 0:D]).then_inc(sem(s + "_yb"), 1)
                each(dve, step)
                for t in range(T):
                    dve.wait_ge(sem(f"{s}_yg{t % NY}"), 16 * (t // NY + 1))
                    dve.scalar_tensor_tensor(out=x[:, t, :], in0=yg[t % NY], scalar=gate[:, t:t + 1], in1=x[:, t, :],
                                             op0=ALU.mult, op1=ALU.add).then_inc(sem(s + "_x"), 1)

        with nc.Block() as block:
            prepare(block)
            ln(block, "ln0", "x_in", 16 * 4)
            add_bias(block, "ln0", b_out[0], "w_in", W_IN)
            qkv0(block)
            attention(block, 0, causal=False)
            project(block, 0)
            ln(block, "ln1", "p0_x", T)
            add_bias(block, "ln1", xb_out, "w_in", W_IN)
            cross(block, 0, top=True)
            ln(block, "ln2", "x0_xd", T)
            moe(block, 0, "x0_xd", T)

        nc.clear_and_free_semaphores([sems.pop(n) for n in list(sems) if n not in KEPT])
        nc.all_engine_barrier()

        with nc.Block() as block:
            ln(block, "ln3", "e0_x", T)
            add_bias(block, "ln3", b_out[1], "w_in", W_IN)
            qkv1(block)
            attention(block, 1, causal=True)
            project(block, 1)
            ln(block, "ln4", "p1_x", T)
            cross(block, 1, top=False)
            ln(block, "ln5", "x1_x2", T)
            moe(block, 1, "x1_x2", T)

            @block.sync
            def _(sp):
                for t in range(T):
                    sp.wait_ge(sem("e1_x"), t + 1)
                    sp.dma_start(out[t // TB, (t % TB) * P:(t % TB + 1) * P, :], x[:, t, :]).then_inc(sem("out"), 16)
                sp.wait_ge(sem("out"), 16 * T)


def kernel(**inputs):
    import numpy as _np
    import concourse.bacc as _bacc
    from concourse import mybir as _mybir
    from concourse.bass_utils import run_bass_kernel_spmd as _run

    nc = _bacc.Bacc("TRN2", target_bir_lowering=False, num_devices=1)
    arrays, aps = {}, {}
    for name, value in inputs.items():
        v = _np.ascontiguousarray(value)
        arrays[f"in_{name}"] = v
        aps[name] = nc.dram_tensor(f"in_{name}", v.shape, _mybir.dt.from_np(v.dtype), kind="ExternalInput").ap()
    out = nc.dram_tensor("decoded", (B, S, D), F32, kind="ExternalOutput").ap()
    build(nc, aps, out)
    r = _run(nc, [arrays], core_ids=[0])
    return r.results[0]["decoded"]
```

```python
from contextlib import ExitStack

import concourse.bass as bass
from concourse import mybir

F32 = mybir.dt.float32
BF16 = mybir.dt.bfloat16
I32 = mybir.dt.int32
U32 = mybir.dt.uint32
ALU = mybir.AluOpType
ACT = mybir.ActivationFunctionType
AX = mybir.AxisListType

P = 128
B, S, D = 2, 1024, 256
KD = D // P
NH, HD = 16, 16
T = B * S // P
TB = T // B
C = 77
E, F = 8, 1024
KF = F // P
BANK = 512
G = 4
NG = NH // G
NU = B * NG
SLOT = 32
QUERY_PARTS = (0, 0, 0, 1, 1, 2)
KEY_PARTS = (0, 1, 2, 0, 1, 0)
NPART = 3
NSLOT = len(QUERY_PARTS)
KS = NSLOT * HD
KM = KS + 2
NST = 3
PR = 8
SCALE = HD ** -0.5
TOPK = 32
LOWEST = -3.0e38
MASKED = -1.0e30
NTB = 4
NS = T + E - 1
LN_EPS = 1e-5
L0_EPS = 1e-6


class Region:

    def __init__(self, arena, size):
        self.arena, self.size, self.at = arena, size, 0

    def f32(self, n):
        a = self.at
        self.at += n
        assert self.at <= self.size, (self.at, self.size)
        return self.arena[:, a:a + n]

    def bf16(self, n):
        return self.f32((n + 1) // 2).bitcast(BF16)


def fills(causal):
    out = []
    for i in range(TB):
        keys = (i + 1) * P if causal else S
        for k in range(0, keys, BANK):
            out.append((i, k // BANK, min(BANK, keys - k)))
    return out


def build(nc, a, out):
    ctx = ExitStack()
    with ctx:
        sems = {}
        KEPT = ("const", "w_in", "w1_in", "xw_in", "kblk", "xv", "wr", "xs_clear", "x_in", "out", "e0_x", "ln3_st")

        def sem(name):
            if name not in sems:
                sems[name] = nc.alloc_semaphore(name)
            return sems[name]

        SIZE = 53200
        arena = ctx.enter_context(nc.sbuf_tensor("arena", [P, SIZE], F32))
        PS = ctx.enter_context(nc.psum_tensor("banks", [P, 8, BANK], F32))
        R = Region(arena, SIZE)

        def scratch(name, shape, dt=F32):
            return nc.dram_tensor(name, shape, dt, kind="Internal").ap()

        parts_dram = [scratch(f"parts{l}", [2, NPART, B * D, S], BF16) for l in range(2)]
        v_dram = [scratch(f"v{l}", [NU, P, TB, G * SLOT]) for l in range(2)]
        xs_dram = [scratch(f"sorted{l}", [NS * P, D]) for l in range(2)]
        ys_dram = [scratch(f"expert_out{l}", [NS * P, D]) for l in range(2)]

        x = R.f32(T * D).rearrange("p (t d) -> p t d", t=T)
        h = R.f32(T * D).rearrange("p (t d) -> p t d", t=T)
        ctx = h.rearrange("p t d -> p (t d)")
        hT = R.f32(KD * B * S).rearrange("p (k n) -> p k n", k=KD)
        ident = R.f32(P)
        identb = R.bf16(P)
        upper = R.bf16(P)
        onesb = R.bf16(P)
        future = R.bf16(P)
        futureT = R.bf16(P)
        stats = R.f32(T * 6).rearrange("p (t s) -> p t s", t=T)
        mv = R.f32(T * 2).rearrange("p (t s) -> p t s", t=T)
        std = R.f32(T)
        rstd = R.f32(T)
        count = R.f32(32)
        order = R.f32(E)
        hmask = R.f32(8)
        wr = [R.f32(KD * E).rearrange("p (k e) -> p k e", k=KD) for _ in range(2)]
        br = [R.f32(E) for _ in range(2)]
        base_mark = R.at

        w_qkv = [R.f32(3 * 3 * D).rearrange("p (k n) -> p k n", k=3) for _ in range(2)]
        w_out = [R.f32(KD * D).rearrange("p (k n) -> p k n", k=KD) for _ in range(2)]
        b_out = [R.f32(D) for _ in range(2)]
        b_qk1 = R.f32(4)
        ln_scale = R.f32(3 * HD).rearrange("p (s d) -> p s d", s=3)
        ln_bias = R.f32(3 * HD).rearrange("p (s d) -> p s d", s=3)
        cmean = R.f32(9 * NH)
        xb_out = R.f32(D)
        gamma, beta = R.f32(D), R.f32(D)
        xq_b = [R.f32(KD) for _ in range(2)]
        xk_b = [R.f32(KD) for _ in range(2)]
        xv_b = [R.f32(D) for _ in range(2)]
        xwqT = [R.f32(KD * D).rearrange("p (k n) -> p k n", k=KD) for _ in range(2)]
        xwo = R.f32(KD * D).rearrange("p (k n) -> p k n", k=KD)
        ctxT = R.f32(KD * B * C).rearrange("p (k n) -> p k n", k=KD)
        kblk = [R.f32(B * KD * 8 * C).rearrange("p (b k j c) -> p b k j c", b=B, k=KD, j=8) for _ in range(2)]
        xv = [R.f32(B * NH * SLOT).rearrange("p (b h s) -> p b h s", b=B, h=NH) for _ in range(2)]
        work_mark = R.at


        PW = NPART * 4 * S // 2
        KST_AT = work_mark + PW
        PROB_AT = work_mark + 2 * PW
        SMALL_AT = PROB_AT + PR * S
        SPARE = 1024
        assert PW == NST * G * S // 2

        W0_IN, XW_IN, W_IN = 16 * 12, 16 * (9 + 2 * 5), 16 * 14
        CONST = 16
        W1_IN = 16 * 2
        ZW = 1024
        XS_CLEAR = 16 * 2 * -(-NS * D // ZW)

        def prepare(block):
            R.at = SIZE - ZW - P
            zero_tile = R.f32(ZW)
            tmp = R.f32(P)

            @block.sync
            def _(sp):
                def load(dst, src, name):
                    sp.dma_start(dst, src).then_inc(sem(name), 16)

                for b in range(B):
                    for t in range(0, TB, 4):
                        load(x[:, b * TB + t:b * TB + t + 4, :],
                             a["x"][b].rearrange("(t p) d -> p t d", p=P)[:, t:t + 4, :], "x_in")
                for i, n in enumerate(("Wq", "Wk", "Wv")):
                    load(w_qkv[0][:, 0:KD, i * D:(i + 1) * D], a[f"L0_attn_{n}"].rearrange("(k p) n -> p k n", p=P), "w0_in")
                for i, n in enumerate(("bq", "bk", "bv")):
                    load(w_qkv[0][:, 2, i * D:(i + 1) * D], a[f"L0_attn_{n}"].partition_broadcast(P), "w0_in")
                for i, n in enumerate("qkv"):
                    load(ln_scale[:, i, :], a[f"L0_attn_{n}_scale"].partition_broadcast(P), "w0_in")
                    load(ln_bias[:, i, :], a[f"L0_attn_{n}_bias"].partition_broadcast(P), "w0_in")
                load(w_out[0], a["L0_attn_Wo"].rearrange("(k p) n -> p k n", p=P), "w_in")
                load(b_out[0], a["L0_attn_bo"].partition_broadcast(P), "w_in")
                load(xb_out, a["L0_xattn_bo"].partition_broadcast(P), "w_in")
                for k in range(4):
                    load(b_qk1[:, k:k + 1], a["L1_attn_qkv_b"][k * P:(k + 1) * P].unsqueeze(1), "w_in")
                load(w_out[1], a["L1_attn_out_w"].rearrange("(k p) n -> p k n", p=P), "w_in")
                load(b_out[1], a["L1_attn_out_b"].partition_broadcast(P), "w_in")
                load(gamma, a["L1_xattn_gamma"].partition_broadcast(P), "w_in")
                load(beta, a["L1_xattn_beta"].partition_broadcast(P), "w_in")
                load(wr[1], a["L1_ffn_Wr"].rearrange("(k p) e -> p k e", p=P), "w_in")
                load(br[0], a["L0_ffn_router_b"].partition_broadcast(P), "w_in")
                load(br[1], a["L1_ffn_br"].partition_broadcast(P), "w_in")
                sp.wait_ge(sem("zeroed"), 1)
                for l in range(2):
                    rows = xs_dram[l].rearrange("(p r) d -> p (r d)", p=P)
                    for n0 in range(0, NS * D, ZW):
                        w = min(ZW, NS * D - n0)
                        sp.dma_start(rows[:, n0:n0 + w], zero_tile[:, 0:w]).then_inc(sem("xs_clear"), 16)


            @block.gpsimd
            def _(pool):
                pool.memset(zero_tile, 0.0).then_inc(sem("zeroed"), 1)
                pool.memset(tmp, 0.0).then_inc(sem("const"), 1)
                pool.memset(onesb, 1.0).then_inc(sem("const"), 1)
                pool.memset(hmask, 1.0).then_inc(sem("const"), 1)
                for l in range(2):
                    pool.memset(xv[l][:, :, :, 0:HD], 0.0).then_inc(sem("const"), 1)
                    pool.memset(xv[l][:, :, :, HD:SLOT], 1.0).then_inc(sem("const"), 1)
                pool.iota(count, pattern=[[1, 32]], base=0, channel_multiplier=0,
                          allow_small_or_imprecise_dtypes=True).then_inc(sem("const"), 1)
                pool.iota(order, pattern=[[-1, E]], base=E, channel_multiplier=0,
                          allow_small_or_imprecise_dtypes=True).then_inc(sem("const"), 1)
                pool.wait_ge(sem("const"), 9)
                pool.affine_select(out=ident, in_=tmp, compare_op=ALU.not_equal, fill=1.0, base=0,
                                   pattern=[[-1, P]], channel_multiplier=1).then_inc(sem("const"), 1)
                pool.affine_select(out=hmask, in_=hmask, compare_op=ALU.is_ge, fill=0.0, base=0,
                                   pattern=[[-HD, 8]], channel_multiplier=1).then_inc(sem("const"), 1)
                pool.affine_select(out=upper, in_=onesb, compare_op=ALU.is_gt, fill=0.0, base=0,
                                   pattern=[[1, P]], channel_multiplier=-1).then_inc(sem("const"), 1)
                pool.affine_select(out=future, in_=tmp, compare_op=ALU.is_ge, fill=MASKED, base=0,
                                   pattern=[[-1, P]], channel_multiplier=1).then_inc(sem("const"), 1)
                pool.affine_select(out=futureT, in_=tmp, compare_op=ALU.is_ge, fill=MASKED, base=0,
                                   pattern=[[1, P]], channel_multiplier=-1).then_inc(sem("const"), 1)
                pool.wait_ge(sem("const"), 14)
                pool.affine_select(out=hmask, in_=hmask, compare_op=ALU.is_ge, fill=0.0, base=HD - 1,
                                   pattern=[[HD, 8]], channel_multiplier=-1).then_inc(sem("const"), 1)
                pool.tensor_copy(identb, ident).then_inc(sem("const"), 1)


        def centre(block):
            @block.vector
            def _(dve):
                dve.wait_ge(sem("w0_in"), W0_IN)
                flat = w_qkv[0].rearrange("p k (h d) -> p (k h) d", d=HD)
                dve.tensor_reduce(cmean, flat, AX.X, ALU.add).then_inc(sem("centre"), 1)
                dve.wait_ge(sem("centre"), 1)
                dve.tensor_scalar(cmean, cmean, 1.0 / HD, None, ALU.mult).then_inc(sem("centre"), 1)
                dve.wait_ge(sem("centre"), 2)
                dve.tensor_tensor(flat, flat, cmean.unsqueeze(2).to_broadcast([P, 9 * NH, HD]),
                                  ALU.subtract).then_inc(sem("centre"), 1)

        def prepare_cross(block):
            H = Region(h.rearrange("p t d -> p (t d)"), T * D)
            W = Region(w_qkv[1].rearrange("p k n -> p (k n)"), 3 * 3 * D)
            R.at = SMALL_AT
            xw_names = [("L0_xattn_Wk", 0), ("L0_xattn_Wv", 0), ("L1_xattn_Wk", 1), ("L1_xattn_Wv", 1),
                        ("L0_xattn_Wq", 0), ("L1_xattn_Wq", 1), ("L0_xattn_Wo", 0)]
            xw_raw = [H.f32(KD * D).rearrange("p (k n) -> p k n", k=KD) for _ in xw_names]
            xw_t = [W.f32(KD * D).rearrange("p (k n) -> p k n", k=KD) for _ in range(4)]
            ctx_raw = H.f32(B * D).rearrange("p (b d) -> p b d", b=B)
            kt_raw = R.f32(KD * B * C).rearrange("p (k n) -> p k n", k=KD)
            vx_raw = R.f32(D)
            vx_mask = R.f32(D).bitcast(I32)
            wr_raw = W.f32(D)

            @block.sync
            def _(sp):
                def load(dst, src, name):
                    sp.dma_start(dst, src).then_inc(sem(name), 16)

                sp.wait_ge(sem("ln0_tr"), T)
                for (n, _), dst in zip(xw_names, xw_raw):
                    load(dst, a[n].rearrange("(k p) n -> p k n", p=P), "xw_in")
                load(ctx_raw[0:C], a["ctx_1024"].rearrange("b c d -> c b d"), "xw_in")
                load(wr_raw[0:E], a["L0_ffn_router_w"], "xw_in")
                for l in range(2):
                    for dst, n in ((xq_b[l], "bq"), (xk_b[l], "bk")):
                        for k in range(KD):
                            load(dst[:, k:k + 1], a[f"L{l}_xattn_{n}"][k * P:(k + 1) * P].unsqueeze(1), "xw_in")
                    load(xv_b[l][0:C], a[f"L{l}_xattn_bv"].partition_broadcast(C), "xw_in")

            def turn():
                @block.tensor
                def _(pe):
                    pe.wait_ge(sem("const"), CONST)
                    pe.wait_ge(sem("xw_in"), XW_IN)
                    for n in range(len(xw_names)):
                        if n >= 2:
                            pe.wait_ge(sem("xwT"), n - 1)
                        for ko in range(KD):
                            for ki in range(KD):
                                mm = pe.transpose(PS[:, n % 2, (ki * KD + ko) * P:(ki * KD + ko + 1) * P],
                                                  xw_raw[n][:, ko, ki * P:(ki + 1) * P], ident)
                        mm.then_inc(sem("xwT_ps"), 1)
                    for b in range(B):
                        for k in range(KD):
                            mm = pe.transpose(PS[:, 2, (k * B + b) * C:(k * B + b + 1) * C],
                                              ctx_raw[0:C, b, k * P:(k + 1) * P], ident[0:C, 0:C])
                    for k in range(KD):
                        mm = pe.transpose(PS[:, 2, BANK - (2 - k) * E:BANK - (1 - k) * E], wr_raw[0:E, k * P:(k + 1) * P], ident[0:E, 0:E])
                    mm.then_inc(sem("ctxT_ps"), 1)
                    pe.wait_ge(sem("ctxT"), 1)
                    pe.wait_ge(sem("xwT"), len(xw_names))
                    pe.wait_ge(sem("q0_s1"), 2 * T)
                    n = 0
                    for l in range(2):
                        for half in range(KD):
                            if n >= 2:
                                pe.wait_ge(sem("kt"), n - 1)
                            for k in range(KD):
                                mm = pe.matmul(PS[:, 3 + n % 2, 0:B * C], xw_t[2 * l][:, k, half * P:(half + 1) * P],
                                               ctxT[:, k, :], start=(k == 0), stop=(k == KD - 1))
                            mm.then_inc(sem("kt_ps"), 1)
                            n += 1
                    n = 0
                    for l in range(2):
                        for b in range(B):
                            if n >= 2:
                                pe.wait_ge(sem("vx"), n - 1)
                            for k in range(KD):
                                mm = pe.matmul(PS[0:C, 5 + n % 2, 0:D], ctxT[:, k, b * C:(b + 1) * C],
                                               xw_t[2 * l + 1][:, k, :], start=(k == 0), stop=(k == KD - 1))
                            mm.then_inc(sem("vx_ps"), 1)
                            n += 1

                @block.vector
                def _(dve):
                    dve.wait_ge(sem("xs_clear"), XS_CLEAR)
                    dve.wait_ge(sem("const"), CONST)
                    for n in range(len(xw_names)):
                        dve.wait_ge(sem("xwT_ps"), n + 1)
                        src = PS[:, n % 2, 0:KD * D].rearrange("p (k n) -> p k n", k=KD)
                        if n < 4:
                            dve.tensor_copy(xw_t[n], src).then_inc(sem("xwT"), 1)
                        elif n < 6:
                            dve.tensor_copy(xwqT[n - 4], src).then_inc(sem("xwT"), 1)
                        else:
                            dve.tensor_copy(xwo, src).then_inc(sem("xwT"), 1)
                    dve.wait_ge(sem("ctxT_ps"), 1)
                    dve.tensor_copy(wr[0], PS[:, 2, BANK - KD * E:BANK].rearrange("p (k e) -> p k e", k=KD)).then_inc(sem("wr"), 1)
                    dve.tensor_copy(ctxT, PS[:, 2, 0:KD * B * C].rearrange("p (k n) -> p k n", k=KD)).then_inc(sem("ctxT"), 1)
                    n = 0
                    for l in range(2):
                        for half in range(KD):
                            dve.wait_ge(sem("kt_ps"), n + 1)
                            if n:
                                dve.wait_ge(sem("kblk"), n * B)
                            dve.tensor_scalar(kt_raw[:, 0, :], PS[:, 3 + n % 2, 0:B * C], xk_b[l][:, half:half + 1], None,
                                              ALU.add).then_inc(sem("kt"), 1)
                            dve.wait_ge(sem("kt"), n + 1)
                            for b in range(B):
                                dve.tensor_tensor(kblk[l][:, b, half], kt_raw[:, 0, b * C:(b + 1) * C].unsqueeze(1).to_broadcast([P, 8, C]),
                                                  hmask.unsqueeze(2).to_broadcast([P, 8, C]), ALU.mult).then_inc(sem("kblk"), 1)
                            n += 1
                    n = 0
                    for l in range(2):
                        for b in range(B):
                            dve.wait_ge(sem("vx_ps"), n + 1)
                            if n:
                                dve.wait_ge(sem("xv"), n)
                            dst = xv[l][0:C, b, :, 0:HD]
                            dve.tensor_tensor(vx_raw[0:C], PS[0:C, 5 + n % 2, 0:D], xv_b[l][0:C], ALU.add).then_inc(sem("vx"), 1)
                            dve.wait_ge(sem("vx"), n + 1)
                            if l == 1:
                                dve.tensor_tensor(vx_mask[0:C], vx_raw[0:C], vx_raw[0:C], ALU.is_equal).then_inc(sem("vxm"), 1)
                                dve.wait_ge(sem("vxm"), b + 1)
                                dve.copy_predicated(dst, vx_mask[0:C].rearrange("p (h d) -> p h d", h=NH),
                                                    vx_raw[0:C].rearrange("p (h d) -> p h d", h=NH)).then_inc(sem("xv"), 1)
                            else:
                                dve.tensor_copy(dst, vx_raw[0:C].rearrange("p (h d) -> p h d", h=NH)).then_inc(sem("xv"), 1)
                            n += 1
                    dve.wait_ge(sem("xv"), 2 * B)

            return turn

        def lgT(l):
            at = work_mark if l == 0 else base_mark
            return arena[:, at:at + BANK]

        def row_stats(dve, s, t, x_sem):
            dve.wait_ge(sem(x_sem), t + 1)
            dve.bn_stats(stats[:, t, :], x[:, t, :]).then_inc(sem(s + "_st"), 1)

        def ln(block, s, x_sem, x_val, stats_due=True, router=None, banks=(4, 5, 6, 7)):
            NBT = len(banks)

            @block.vector
            def _(dve):
                if stats_due:
                    dve.wait_ge(sem(x_sem), x_val)
                    for t in range(T):
                        dve.bn_stats(stats[:, t, :], x[:, t, :]).then_inc(sem(s + "_st"), 1)
                for t in range(T):
                    dve.wait_ge(sem(s + "_st"), t + 1)
                    dve.bn_aggr(mv[:, t, :], stats[:, t, :]).then_inc(sem(s + "_mv"), 1)
                dve.wait_ge(sem(s + "_mv"), T)
                dve.tensor_scalar(std, mv[:, :, 1], LN_EPS, None, ALU.add).then_inc(sem(s + "_var"), 1)
                dve.wait_ge(sem(s + "_std"), 1)
                dve.reciprocal(rstd, std).then_inc(sem(s + "_rstd"), 1)
                dve.wait_ge(sem(s + "_rstd"), 1)
                for t in range(T):
                    dve.tensor_scalar(h[:, t, :], x[:, t, :], mv[:, t, 0:1], rstd[:, t:t + 1], ALU.subtract,
                                      ALU.mult).then_inc(sem(s + "_h"), 1)

                if router is not None:
                    for q in range(T // 4):
                        dve.wait_ge(sem(s + "_lp"), q + 1)
                        if q:
                            dve.wait_ge(sem(s + "_lt"), q)
                        dve.tensor_copy(lgT(router)[0:E], PS[0:E, q % 2, :]).then_inc(sem(s + "_lc"), 1)

            @block.scalar
            def _(act):
                act.wait_ge(sem(s + "_var"), 1)
                act.activation(std, std, ACT.Sqrt).then_inc(sem(s + "_std"), 1)
                for t in range(T):
                    act.wait_ge(sem(s + "_tr"), t + 1)
                    act.copy(hT[:, :, t * P:(t + 1) * P],
                             PS[:, banks[t % NBT], 0:KD * P].rearrange("p (k n) -> p k n", k=KD)).then_inc(sem(s + "_hT"), 1)

            @block.tensor
            def _(pe):
                def logits(q):
                    pe.wait_ge(sem(s + "_hT"), 4 * q + 4)
                    for k in range(KD):
                        mm = pe.matmul(PS[0:E, q % 2, :], wr[router][:, k, :], hT[:, k, q * BANK:(q + 1) * BANK],
                                       start=(k == 0), stop=(k == KD - 1))
                    mm.then_inc(sem(s + "_lp"), 1)

                def turn_logits(q):
                    pe.wait_ge(sem(s + "_lc"), q + 1)
                    for t in range(4 * q, 4 * q + 4):
                        mm = pe.transpose(PS[:, 3, t * E:(t + 1) * E], lgT(router)[0:E, (t % 4) * P:(t % 4 + 1) * P],
                                          ident[0:E, 0:E])
                    mm.then_inc(sem(s + "_lt"), 1)

                pe.wait_ge(sem("const"), CONST)
                if router is not None:
                    pe.wait_ge(sem("w_in"), W_IN)
                    pe.wait_ge(sem("wr"), 1)
                for t in range(T):
                    pe.wait_ge(sem(s + "_h"), t + 1)
                    if t >= NBT:
                        pe.wait_ge(sem(s + "_hT"), t - NBT + 1)
                    for k in range(KD):
                        mm = pe.transpose(PS[:, banks[t % NBT], k * P:(k + 1) * P], h[:, t, k * P:(k + 1) * P], ident)
                    mm.then_inc(sem(s + "_tr"), 1)
                    if router is not None and t >= 4 and t % 4 == 1:
                        logits(t // 4 - 1)
                    if router is not None and t >= 4 and t % 4 == 3:
                        turn_logits(t // 4 - 1)
                if router is not None:
                    logits(T // 4 - 1)
                    turn_logits(T // 4 - 1)

        def add_bias(block, s, bias, wsem, wval):
            @block.gpsimd
            def _(pool):
                pool.wait_ge(sem(s + "_h"), T)
                pool.wait_ge(sem(wsem), wval)
                pool.tensor_tensor(x, x, bias.unsqueeze(1).to_broadcast([P, T, D]), ALU.add).then_inc(sem(s + "_xb"), 1)

        def split_chunks(s, u_bufs, source, dest):
            def act_part(act, i):
                if i < 16:
                    views, ready, val = source(i)
                    act.wait_ge(sem(ready), val)
                    if i >= 3:
                        act.wait_ge(sem(s + "_s3"), i - 2)
                    for at, ps, bias, scale in views:
                        act.activation(u_bufs[i % 3][at], ps, ACT.Identity, bias=bias, scale=scale).then_inc(sem(s + "_u"), 1)
                    for at, ps, bias, scale in views:
                        act.activation(dest(i, 0)[at], ps, ACT.Identity, bias=bias, scale=scale).then_inc(sem(s + "_s1"), 1)
                if i >= 1 and i - 1 < 16:
                    act.wait_ge(sem(s + "_r1"), i)
                    src = u_bufs[(i - 1) % 3]
                    act.activation(dest(i - 1, 1), src, ACT.Identity).then_inc(sem(s + "_s2"), 1)

            def second_rest(pool, i):
                if i < 16:
                    pool.wait_ge(sem(s + "_s1"), (i + 1) * len(source(i)[0]))
                    pool.tensor_tensor(u_bufs[i % 3], u_bufs[i % 3], dest(i, 0), ALU.subtract).then_inc(sem(s + "_r1"), 1)

            def third_rest(eng, i):
                if i >= 1 and i - 1 < 16:
                    eng.wait_ge(sem(s + "_s2"), i)
                    eng.wait_ge(sem(s + "_r1"), i)
                    eng.tensor_tensor(dest(i - 1, 2), u_bufs[(i - 1) % 3], dest(i - 1, 1), ALU.subtract).then_inc(sem(s + "_s3"), 1)

            return act_part, second_rest, third_rest

        def store_parts(sp, s, l, b, parts):
            sp.wait_ge(sem(s + "_s3"), 8 * (b + 1))
            sp.wait_ge(sem(s + "_s1"), 8 * (b + 1) * (2 if l == 0 else 1))
            sp.wait_ge(sem(s + "_s2"), 8 * (b + 1))
            for qk in range(2):
                for n in range(NPART):
                    sp.dma_start(parts_dram[l][qk, n, b * D:(b + 1) * D, :].rearrange("(k p) n -> p k n", p=P),
                                 parts[b][:, n, qk * KD:(qk + 1) * KD, :]).then_inc(sem(s + "_parts"), 16)

        PARTS_ST = 16 * 2 * NPART * B

        def parts_buffers():
            R.at = work_mark
            first = R.bf16(NPART * 4 * S)
            R.at = PROB_AT
            second = R.bf16(NPART * 4 * S)
            return [p.rearrange("p (n c t) -> p n c t", n=NPART, c=4) for p in (first, second)]

        def stack_buffers():
            R.at = work_mark
            qst = [R.bf16(G * S).rearrange("p (j t) -> p j t", j=G) for _ in range(NST)]
            kst = [R.bf16(G * S).rearrange("p (j t) -> p j t", j=G) for _ in range(NST)]
            spare = hT.rearrange("p k n -> p (k n)")
            VW = TB * G * SLOT
            vst = [spare[:, r * VW:(r + 1) * VW].rearrange("p (t j s) -> p t j s", t=TB, j=G) for r in range(NST)]
            return qst, kst, vst, spare[:, NST * VW:NST * VW + S]

        STACK_IN = 16 * (2 * NSLOT + 1)

        def load_unit(sp, l, u):
            r = u % NST
            qst, kst, vst, _ = stack_buffers()
            for slot in range(NSLOT):
                for st, qk, part in ((qst, 0, QUERY_PARTS[slot]), (kst, 1, KEY_PARTS[slot])):
                    sp.dma_start(st[r][slot * HD:(slot + 1) * HD],
                                 parts_dram[l][qk, part].rearrange("(u j d) t -> u d j t", j=G, d=HD)[u]
                                 ).then_inc(sem(f"a{l}_in{r}"), 16)
            sp.dma_start(vst[r].rearrange("p t j s -> p (t j s)"),
                         v_dram[l].rearrange("u p t n -> u p (t n)")[u]).then_inc(sem(f"a{l}_in{r}"), 16)

        def store_projections(sp, s, l, parts, vt):
            for t in range(T):
                sp.wait_ge(sem(s + "_v"), t + 1)
                b = t // TB
                sp.dma_start(v_dram[l][b * NG:(b + 1) * NG, :, t % TB, :].rearrange("g p n -> p g n"),
                             vt[t % 2].rearrange("p (g j) s -> p g (j s)", g=NG)).then_inc(sem(f"{s}_vst{t % 2}"), 16)
                if t == TB - 1:
                    for r in range(2):
                        sp.wait_ge(sem(f"{s}_vst{r}"), 16 * TB // 2)
                if t == TB + (5 if l == 0 else 1):
                    store_parts(sp, s, l, 0, parts)
            sp.wait_ge(sem(s + "_parts"), PARTS_ST // B)
            if l == 0:
                sp.wait_ge(sem(s + "_ps"), T)
                sp.wait_ge(sem(s + "_tr"), T)
                sp.wait_ge(sem(s + "_sq"), T)
                sp.wait_ge(sem(s + "_ss"), T)
                for r in range(2):
                    sp.wait_ge(sem(f"{s}_vst{r}"), 16 * T // 2)
            else:
                sp.wait_ge(sem(s + "_ps"), T)
                sp.wait_ge(sem(s + "_vps"), T)
            load_unit(sp, l, 0)
            store_parts(sp, s, l, 1, parts)

        def qkv0(block):
            s = "q0"
            parts = parts_buffers()
            ss = [R.f32(3 * NH) for _ in range(4)]
            ub = [R.f32(BANK) for _ in range(3)]
            K = Region(arena, PROB_AT)
            K.at = KST_AT
            cb = [K.f32(3 * D) for _ in range(4)]
            sq = [K.f32(3 * D) for _ in range(2)]
            vt = [K.f32(NH * SLOT).rearrange("p (h s) -> p h s", h=NH) for _ in range(2)]
            u_bufs = [u.rearrange("p (c n) -> p c n", c=4) for u in ub]
            scale_bias = R.f32(4)
            ln_rep = ub[0]

            def source(i):
                ps = PS[:, 4 + i % 2, :].rearrange("p (c n) -> p c n", c=4)
                views = [((slice(None), slice(KD * n, KD * n + KD)), ps[:, KD * n:KD * n + KD], scale_bias[:, 2 + n:3 + n],
                          scale_bias[:, n:n + 1]) for n in range(2)]
                return views, s + "_tr", i + 1

            def dest(i, n):
                return parts[i // TB][:, n, :, (i % TB) * P:(i % TB + 1) * P]

            act_split, second_rest, third_rest = split_chunks(s, u_bufs, source, dest)

            @block.tensor
            def _(pe):
                pe.wait_ge(sem(s + "_lnb"), 4)
                for n in range(4):
                    mm = pe.transpose(PS[:, 4, n * P:(n + 1) * P], ln_rep[:, n * P:(n + 1) * P], ident)
                mm.then_inc(sem(s + "_lnt"), 1)

            @block.vector
            def _(dve):
                dve.wait_ge(sem("w0_in"), W0_IN)
                for n, src in enumerate((ln_scale[:, 0], ln_scale[:, 1], ln_bias[:, 0], ln_bias[:, 1])):
                    dve.tensor_copy(ln_rep[:, n * P:(n + 1) * P].rearrange("p (j d) -> p j d", d=HD),
                                    src.unsqueeze(1).to_broadcast([P, 8, HD])).then_inc(sem(s + "_lnb"), 1)
                dve.wait_ge(sem(s + "_lnt"), 1)
                dve.tensor_copy(scale_bias, PS[:, 4, :].rearrange("p (n j) -> p n j", n=4)[:, :, 0]).then_inc(sem(s + "_lns"), 1)

            @block.tensor
            def _(pe):
                pe.wait_ge(sem("centre"), 3)
                for i in range(T + 4):
                    if i < T:
                        pe.wait_ge(sem("ln0_hT"), i + 1)
                        if i >= 2:
                            pe.wait_ge(sem(s + "_c"), i - 1)
                        b0 = 2 * (i % 2)
                        for n0, nw in ((0, BANK), (BANK, 3 * D - BANK)):
                            for k in range(KD):
                                mm = pe.matmul(PS[:, b0 + n0 // BANK, 0:nw], hT[:, k, i * P:(i + 1) * P],
                                               w_qkv[0][:, k, n0:n0 + nw], start=(k == 0), stop=(k == KD - 1))
                        mm.then_inc(sem(s + "_ps"), 1)
                    if i >= 4:
                        t = i - 4
                        pe.wait_ge(sem(s + "_n"), t + 1)
                        if t >= 2:
                            pe.wait_ge(sem(s + "_s1"), 2 * (t - 1))
                        for c in range(4):
                            mm = pe.transpose(PS[:, 4 + t % 2, c * P:(c + 1) * P], cb[t % 4][:, c * P:(c + 1) * P], ident)
                        mm.then_inc(sem(s + "_tr"), 1)

            @block.vector
            def _(dve):
                dve.wait_ge(sem("centre"), 3)
                for i in range(T + 2):
                    if i < T:
                        dve.wait_ge(sem(s + "_ps"), i + 1)
                        if i >= 4:
                            dve.wait_ge(sem(s + "_tr"), i - 3)
                            dve.wait_ge(sem(s + "_v"), i - 3)
                        b0 = 2 * (i % 2)
                        dve.tensor_tensor(cb[i % 4], PS[:, b0:b0 + 2, :].rearrange("p a n -> p (a n)")[:, 0:3 * D],
                                          w_qkv[0][:, 2, :], ALU.add).then_inc(sem(s + "_c"), 1)
                    if 1 <= i <= T:
                        t = i - 1
                        dve.wait_ge(sem(s + "_sq"), t + 1)
                        dve.tensor_reduce(ss[t % 4], sq[t % 2].rearrange("p (h d) -> p h d", d=HD), AX.X,
                                          ALU.add).then_inc(sem(s + "_ss"), 1)
                        dve.wait_ge(sem(s + "_ss"), t + 1)
                        dve.tensor_scalar(ss[t % 4], ss[t % 4], 1.0 / HD, L0_EPS, ALU.mult, ALU.add).then_inc(sem(s + "_var"), 1)
                    if i >= 2:
                        t = i - 2
                        dve.wait_ge(sem(s + "_std"), t + 1)
                        dve.reciprocal(ss[t % 4], ss[t % 4]).then_inc(sem(s + "_rs"), 1)
                        dve.wait_ge(sem(s + "_rs"), t + 1)
                        c48 = cb[t % 4].rearrange("p (h d) -> p h d", d=HD)
                        dve.tensor_tensor(c48, c48, ss[t % 4].unsqueeze(2).to_broadcast([P, 3 * NH, HD]),
                                          ALU.mult).then_inc(sem(s + "_n"), 1)

            @block.scalar
            def _(act):
                act.wait_ge(sem(s + "_lns"), 1)
                for i in range(T + 5):
                    if i < T:
                        act.wait_ge(sem(s + "_c"), i + 1)
                        if i >= 2:
                            act.wait_ge(sem(s + "_ss"), i - 1)
                        act.activation(sq[i % 2], cb[i % 4], ACT.Square).then_inc(sem(s + "_sq"), 1)
                    if 1 <= i <= T:
                        act.wait_ge(sem(s + "_var"), i)
                        act.activation(ss[(i - 1) % 4], ss[(i - 1) % 4], ACT.Sqrt).then_inc(sem(s + "_std"), 1)
                    if i >= 4:
                        act_split(act, i - 4)

            @block.gpsimd
            def _(pool):
                for v in vt:
                    pool.memset(v[:, :, HD:SLOT], 1.0).then_inc(sem(s + "_vpad"), 1)

                def values(t):
                    v = cb[t % 4].rearrange("p (s h d) -> p s h d", s=3, d=HD)[:, 2]
                    pool.wait_ge(sem(s + "_n"), t + 1)
                    pool.tensor_tensor(v, v, ln_scale[:, 2].unsqueeze(1).to_broadcast([P, NH, HD]), ALU.mult).then_inc(sem(s + "_n2"), 1)
                    pool.wait_ge(sem(s + "_n2"), t + 1)
                    if t >= 2:
                        pool.wait_ge(sem(f"{s}_vst{t % 2}"), 16 * (t // 2))
                    else:
                        pool.wait_ge(sem(s + "_vpad"), 2)
                    pool.tensor_tensor(vt[t % 2][:, :, 0:HD], v, ln_bias[:, 2].unsqueeze(1).to_broadcast([P, NH, HD]),
                                       ALU.add).then_inc(sem(s + "_v"), 1)

                for i in range(T + 5):
                    if 2 <= i < T + 2:
                        values(i - 2)
                    if i >= 4:
                        second_rest(pool, i - 4)
                        third_rest(pool, i - 4)

            @block.sync
            def _(sp):
                store_projections(sp, s, 0, parts, vt)

        def qkv1(block):
            s = "q1"
            parts = parts_buffers()
            u_bufs = [R.f32(BANK) for _ in range(3)]
            vt = [R.f32(NH * SLOT).rearrange("p (h s) -> p h s", h=NH) for _ in range(2)]

            def where(i):
                b, m, half = i // 8, (i % 8) // 2, i % 2
                return b, m, half

            def source(i):
                b, m, half = where(i)
                return [(slice(None), PS[:, 4 + i % 2, :], b_qk1[:, m:m + 1], 1.0)], s + "_ps", i + 1

            def dest(i, n):
                b, m, half = where(i)
                return parts[b][:, n, m, half * BANK:(half + 1) * BANK]

            act_split, second_rest, third_rest = split_chunks(s, u_bufs, source, dest)

            @block.tensor
            def _(pe):
                pe.wait_ge(sem("w1_in"), W1_IN)
                pe.wait_ge(sem("ln3_hT"), T)
                for i in range(16):
                    b, m, half = where(i)
                    if i >= 2:
                        pe.wait_ge(sem(s + "_s1"), i - 1)
                    for k in range(KD):
                        mm = pe.matmul(PS[:, 4 + i % 2, :], w_qkv[1][:, k, m * P:(m + 1) * P],
                                       hT[:, k, b * S + half * BANK:b * S + (half + 1) * BANK],
                                       start=(k == 0), stop=(k == KD - 1))
                    mm.then_inc(sem(s + "_ps"), 1)
                    if i >= 2:
                        pe.wait_ge(sem(s + "_v"), i - 1)
                    for k in range(KD):
                        mm = pe.matmul(PS[:, 6 + i % 2, 0:D], hT[:, k, i * P:(i + 1) * P], w_qkv[1][:, k, 2 * D:3 * D],
                                       start=(k == 0), stop=(k == KD - 1))
                    mm.then_inc(sem(s + "_vps"), 1)

            @block.scalar
            def _(act):
                act.wait_ge(sem("w_in"), W_IN)
                for i in range(17):
                    act_split(act, i)

            @block.gpsimd
            def _(pool):
                pool.wait_ge(sem("e0_x"), T)
                for v in vt:
                    pool.memset(v[:, :, HD:SLOT], 1.0).then_inc(sem(s + "_vpad"), 1)
                for i in range(16):
                    second_rest(pool, i)

            @block.vector
            def _(dve):
                dve.wait_ge(sem("w1_in"), W1_IN)
                for t in range(T + 1):
                    third_rest(dve, t)
                    if t == T:
                        break
                    dve.wait_ge(sem(s + "_vps"), t + 1)
                    if t >= 2:
                        dve.wait_ge(sem(f"{s}_vst{t % 2}"), 16 * (t // 2))
                    else:
                        dve.wait_ge(sem(s + "_vpad"), 2)
                    dve.tensor_tensor(vt[t % 2][:, :, 0:HD], PS[:, 6 + t % 2, 0:D].rearrange("p (h d) -> p h d", d=HD),
                                      w_qkv[1][:, 2, 2 * D:3 * D].rearrange("p (h d) -> p h d", d=HD),
                                      ALU.add).then_inc(sem(s + "_v"), 1)

            @block.sync
            def _(sp):
                store_projections(sp, s, 1, parts, vt)

        def attention(block, l, causal):
            s, q = f"a{l}", f"q{l}"
            qst, kst, vst, osb = stack_buffers()
            prob = [R.f32(S) for _ in range(PR)]
            R.at = SMALL_AT + SPARE
            m2 = R.f32(G * TB * 2).rearrange("p (j t a) -> p j t a", j=G, a=2)
            mx = R.f32(G * TB).rearrange("p (j t) -> p j t", j=G)
            mh = R.bf16(2 * G * TB)
            mhl = mh.rearrange("p (c j t) -> p c j t", c=2, j=G)
            mT = R.bf16(P)
            rs = R.f32(TB * G).rearrange("p (t j) -> p t j", t=TB)
            head_fills = fills(causal)
            unit_fills = [(j, *f) for j in range(G) for f in head_fills]
            NF = len(unit_fills)
            NBK = 3
            RING = -(-(NF + 1) // NBK) * NBK
            AHEAD = NF // 4
            items = []
            for kt in range(TB):
                lo = kt * P if causal else 0
                for j in range(G):
                    for c0 in range(0, S, BANK):
                        if c0 + BANK > lo:
                            items.append((kt, j, max(lo, c0), c0 + BANK))
            NI = len(items)
            SRING = -(-NI // NBK) * NBK
            if SRING == RING:
                SRING += NBK
            upto_kt = [sum(1 for it in items if it[0] <= kt) for kt in range(TB)]

            def pv_width(kt, bank):
                return 4 * min(BANK, max(0, (bank + 1) * BANK - (kt * P if causal else 0)))

            WORK = sum(c1 - c0 for _, _, c0, c1 in items) + BANK + sum(pv_width(kt, 0) + pv_width(kt, 1) for kt in range(TB - 1))
            opsum = PS[:, 6:8, :].rearrange("p a n -> p (a n)")
            OUT_FILL = AHEAD + NF // 16

            IN = STACK_IN

            @block.sync
            def _(sp):
                sp.wait_ge(sem(q + "_parts"), PARTS_ST)
                for u in range(1, NST):
                    load_unit(sp, l, u)
                sp.wait_ge(sem(s + "_ones"), NST)
                for u in range(NU):
                    sp.wait_ge(sem(s + "_mT"), u + 1)
                    sp.dma_start(qst[u % NST][KS:KM], mT[0:2 * G * TB]).then_inc(sem(s + "_rows"), 16)
                    if 1 <= u <= NU - NST:
                        sp.wait_ge(sem(s + "_pv"), u * TB)
                        load_unit(sp, l, u - 1 + NST)

                if l == 0:
                    sp.wait_ge(sem("xv"), 2 * B)
                    sp.dma_start(w_qkv[1][:, 0:KD, :], a["L1_attn_qkv_w"].rearrange("(k p) n -> p k n", p=P)).then_inc(sem("w1_in"), 16)
                    sp.dma_start(w_qkv[1][:, 2, :], a["L1_attn_qkv_b"].partition_broadcast(P)).then_inc(sem("w1_in"), 16)

            @block.tensor
            def _(pe):
                def count(u, each, more=0):
                    return u[0] * (NST * each) + (u[1] * each + more)

                def after(u, k):
                    return u[0], u[1] + k

                def pass1(u, f):
                    r = u[1] % NST
                    if not (isinstance(u[0], int) and u[0] == 0 and u[1] == 0 and f < NBK):
                        pe.wait_ge(sem(s + "_red"), count(u, RING, f - NBK + 1))
                    if f == 0:
                        pe.wait_ge(sem(f"{s}_in{r}"), u[0] * IN + (u[1] // NST + 1) * IN)
                    if f < NF:
                        j, i, kb, w = unit_fills[f]
                        diag = causal and kb == i * P // BANK
                        mm = pe.matmul(PS[:, f % NBK, 0:w], qst[r][0:KS, j, i * P:(i + 1) * P],
                                       kst[r][0:KS, j, kb * BANK:kb * BANK + w], start=True, stop=not diag)
                        if diag:
                            mm = pe.matmul(PS[:, f % NBK, w - P:w], identb, future, start=False, stop=True)
                        mm.then_inc(sem(s + "_fill"), 1)
                    else:
                        pe.wait_ge(sem(s + "_mh"), count(u, 1, 1))
                        pe.transpose(PS[0:2 * G * TB, f % NBK, 0:P // 2].bitcast(BF16), mh, identb
                                     ).then_inc(sem(s + "_fill"), RING - NF)

                def pass2(u, n):
                    r = u[1] % NST
                    kt, j, c0, c1 = items[n]
                    pe.wait_ge(sem(s + "_exp"), count(u, SRING, n + 1))
                    diag = causal and c0 == kt * P
                    bank = PS[:, NBK + n % NBK, 0:c1 - c0]
                    mm = pe.matmul(bank, kst[r][0:KM, j, kt * P:(kt + 1) * P], qst[r][0:KM, j, c0:c1],
                                   start=True, stop=not diag)
                    if diag:
                        mm = pe.matmul(bank[:, 0:P], identb, futureT, start=False, stop=True)
                    mm.then_inc(sem(s + "_sc"), 1)

                def pv(u, kt, bank):
                    r = u[1] % NST
                    lo = kt * P if causal else 0
                    c0, c1 = max(lo, bank * BANK), (bank + 1) * BANK
                    if c0 < c1:
                        pe.wait_ge(sem(s + "_exp"), count(u, SRING, (upto_kt[kt] if kt < TB - 1 else SRING) + NBK))
                        if kt == 0 and bank == 0:
                            pe.wait_ge(sem(s + "_n"), count(u, 1, 1))
                        lastk = TB - 1 if not causal or bank == 1 else BANK // P - 1
                        for j in range(G):
                            mm = pe.matmul(opsum[SLOT * j:SLOT * (j + 1), c0:c1], vst[r][:, kt, j, :],
                                           prob[(kt * G + j) % PR][:, c0:c1], start=(kt == 0), stop=(kt == lastk))
                        if bank == 1:
                            mm.then_inc(sem(s + "_pv"), 1)

                def turn_output(u):
                    pe.wait_ge(sem(s + "_o"), count(u, 1, 2))
                    for t in range(TB):
                        mm = pe.transpose(opsum[:, t * P:(t + 1) * P], osb[:, t * P:(t + 1) * P], ident)
                    mm.then_inc(sem(s + "_ot"), 1)

                pe.wait_ge(sem("const"), CONST)
                for f in range(NF + 1):
                    pass1((0, 0), f)
                for f in range(AHEAD):
                    pass1((0, 1), f)

                def unit(u, units_left=2):
                    pe.wait_ge(sem(s + "_rows"), count(u, 16, 16))
                    queue = []
                    if units_left >= 1:
                        queue += [(after(u, 1), f) for f in range(AHEAD, NF + 1)]
                    if units_left >= 2:
                        queue += [(after(u, 2), f) for f in range(AHEAD)]
                    at, past = 0, 0

                    def first_pass(columns):
                        nonlocal at, past
                        while at < min(1, (past + columns / 2) / WORK) * len(queue):
                            pass1(*queue[at])
                            at += 1
                        past += columns

                    for n, (kt, j, c0, c1) in enumerate(items):
                        first_pass(c1 - c0)
                        pass2(u, n)
                        begun = n + 1 - (upto_kt[kt - 1] if kt else 0)
                        size = upto_kt[kt] - n - 1 + begun
                        if kt == 0 and begun == size // 2:
                            first_pass(BANK)
                            turn_output(after(u, -1))
                        if kt and begun in (size // 4, 3 * size // 4):
                            first_pass(pv_width(kt - 1, int(begun > size // 4)))
                            pv(u, kt - 1, int(begun > size // 4))
                    first_pass(2 * WORK)
                    pv(u, TB - 1, 0)
                    pv(u, TB - 1, 1)

                with pe.Fori(0, 2) as i:
                    for r in range(NST):
                        unit((i, r))
                unit((2, 0), units_left=1)
                unit((2, 1), units_left=0)
                turn_output((2, 1))

            @block.scalar
            def _(act):
                if l == 0:
                    act.wait_ge(sem("xv"), 2 * B)
                act.wait_ge(sem(q + "_parts"), PARTS_ST)
                act.nop().then_inc(sem(s + "_exp"), NBK)

                def unit(u, first=False):
                    for n, (kt, j, c0, c1) in enumerate(items):
                        act.wait_ge(sem(s + "_sc"), u * NI + n + 1)
                        if not (first and kt < 2):
                            act.wait_ge(sem(s + "_pv"), u * TB + kt - 1)
                        act.activation(prob[(kt * G + j) % PR][:, c0:c1], PS[:, NBK + n % NBK, 0:c1 - c0], ACT.Exp,
                                       scale=SCALE).then_inc(sem(s + "_exp"), 1 if n < NI - 1 else SRING - NI + 1)
                        if n == 1:
                            if first:
                                act.nop().then_inc(sem(s + "_o"), 1)
                            else:
                                copy_out(u - 1)

                def copy_out(u):
                    act.wait_ge(sem(s + "_pv"), (u + 1) * TB)
                    act.wait_ge(sem(s + "_ot"), u + 1)
                    act.copy(osb, opsum).then_inc(sem(s + "_o"), 1)

                unit(0, first=True)
                with act.Fori(1, NU) as u:
                    unit(u)
                copy_out(NU - 1)

            @block.gpsimd
            def _(pool):
                if l == 0:
                    pool.wait_ge(sem("q0_s3"), T)
                else:
                    pool.wait_ge(sem("ln3_xb"), 1)
                if l == 0:
                    pool.wait_ge(sem("q0_tr"), T)
                    pool.wait_ge(sem("q0_ss"), T)
                    for r in range(2):
                        pool.wait_ge(sem(f"q0_vst{r}"), 16 * T // 2)
                for r in range(NST):
                    pool.memset(kst[r][KS:KM].rearrange("p j t -> p (j t)"), 1.0).then_inc(sem(s + "_ones"), 1)

            @block.vector
            def _(dve):
                def reduce(u, f):
                    j, i, kb, w = unit_fills[f]
                    dve.wait_ge(sem(s + "_fill"), u * RING + f + 1)
                    dve.tensor_reduce(m2[:, j, i, kb:kb + 1], PS[:, f % NBK, 0:w], AX.X, ALU.max).then_inc(sem(s + "_red"), 1)

                def maxima(u, first=False):
                    dve.wait_ge(sem(s + "_red"), u * RING + NF)
                    dve.tensor_tensor(mx, m2[:, :, :, 0], m2[:, :, :, 1], ALU.max).then_inc(sem(s + "_mx"), 1)
                    dve.wait_ge(sem(s + "_mx"), u + 1)
                    dve.tensor_scalar(mhl[:, 0], mx, -1.0, None, ALU.mult).then_inc(sem(s + "_mhi"), 1)
                    dve.wait_ge(sem(s + "_mhi"), u + 1)
                    dve.scalar_tensor_tensor(out=mhl[:, 1], in0=mx, scalar=-1.0, in1=mhl[:, 0], op0=ALU.mult,
                                             op1=ALU.subtract).then_inc(sem(s + "_mh"), 1)
                    dve.wait_ge(sem(s + "_fill"), (u + 1) * RING)
                    if not first:
                        dve.wait_ge(sem(s + "_rows"), 16 * u)
                    dve.tensor_copy(mT[0:2 * G * TB], PS[0:2 * G * TB, NF % NBK, 0:P // 2].bitcast(BF16)).then_inc(sem(s + "_mT"), 1)
                    dve.wait_ge(sem(s + "_mT"), u + 1)
                    dve.nop().then_inc(sem(s + "_red"), RING - NF)

                def normalize(u, pair, half):
                    o = opsum.rearrange("p (t j s) -> p t j s", t=TB, j=G)
                    dve.wait_ge(sem(s + "_ot"), u + 2)
                    dve.reciprocal(rs, o[:, :, :, HD]).then_inc(sem(s + "_rs"), 1)
                    dve.wait_ge(sem(s + "_rs"), u + 1)
                    PW = TB * P
                    dst = ctx[:, pair * PW:(pair + 1) * PW] if isinstance(pair, int) else ctx[:, bass.ds(pair * PW, PW)]
                    dst = dst.rearrange("p (t a j d) -> p t a j d", t=TB, a=2, j=G)[:, :, half]
                    dve.tensor_tensor(dst, o[:, :, :, 0:HD],
                                      rs.unsqueeze(3).to_broadcast([P, TB, G, HD]), ALU.mult).then_inc(sem(s + "_n"), 1)

                dve.memset(m2.rearrange("p j t a -> p (j t a)"), LOWEST).then_inc(sem(s + "_m2"), 1)
                dve.wait_ge(sem(s + "_m2"), 1)
                dve.nop().then_inc(sem(s + "_n"), 1)

                for f in range(NF):
                    reduce(0, f)
                maxima(0, first=True)
                for f in range(AHEAD):
                    reduce(1, f)

                def unit(u, pair=None, half=None, before_last=False):
                    for f in range(AHEAD, NF):
                        reduce(u + 1, f)
                        if f == OUT_FILL and pair is not None:
                            normalize(u - 1, pair, half)
                    maxima(u + 1)
                    if not before_last:
                        for f in range(AHEAD):
                            reduce(u + 2, f)

                unit(0)
                with dve.Fori(0, NU // 2 - 2) as i:
                    unit(i * 2 + 1, i, 0)
                    unit(i * 2 + 2, i, 1)
                unit(NU - 3, NU // 2 - 2, 0)
                unit(NU - 2, NU // 2 - 2, 1, before_last=True)
                normalize(NU - 2, NU // 2 - 1, 0)
                normalize(NU - 1, NU // 2 - 1, 1)

        def project(block, l):
            s, at, lns, next_ln = f"p{l}", f"a{l}", ("ln0", "ln3")[l], ("ln1", "ln4")[l]
            R.at = work_mark
            ct = [R.f32(KD * P).rearrange("p (k n) -> p k n", k=KD) for _ in range(2)]
            blocks = ctx.rearrange("p (b k t n) -> p b k t n", b=B, k=KD, t=TB)

            @block.tensor
            def _(pe):
                pe.wait_ge(sem("w_in"), W_IN)
                pe.wait_ge(sem(at + "_n"), NU + 1)

                def turn(t):
                    if t >= 2:
                        pe.wait_ge(sem(s + "_ct"), t - 1)
                    for k in range(KD):
                        mm = pe.transpose(PS[:, t % 2, k * P:(k + 1) * P], blocks[:, t // TB, k, t % TB, :], ident)
                    mm.then_inc(sem(s + "_ctp"), 1)

                turn(0)
                for t in range(T):
                    if t + 1 < T:
                        turn(t + 1)
                    pe.wait_ge(sem(s + "_ct"), t + 1)
                    if t >= 2:
                        pe.wait_ge(sem(s + "_x"), t - 1)
                    for k in range(KD):
                        mm = pe.matmul(PS[:, 2 + t % 2, 0:D], ct[t % 2][:, k, :], w_out[l][:, k, :],
                                       start=(k == 0), stop=(k == KD - 1))
                    mm.then_inc(sem(s + "_y"), 1)

            @block.scalar
            def _(act):
                for t in range(T):
                    act.wait_ge(sem(s + "_ctp"), t + 1)
                    if t >= 2:
                        act.wait_ge(sem(s + "_y"), t - 1)
                    act.copy(ct[t % 2], PS[:, t % 2, 0:D].rearrange("p (k n) -> p k n", k=KD)).then_inc(sem(s + "_ct"), 1)

            @block.vector
            def _(dve):
                dve.wait_ge(sem(lns + "_xb"), 1)
                for t in range(T):
                    dve.wait_ge(sem(s + "_y"), t + 1)
                    dve.tensor_tensor(x[:, t, :], x[:, t, :], PS[:, 2 + t % 2, 0:D], ALU.add).then_inc(sem(s + "_x"), 1)
                    if t:
                        row_stats(dve, next_ln, t - 1, s + "_x")
                row_stats(dve, next_ln, T - 1, s + "_x")

        def cross(block, l, top):
            s, lns = f"x{l}", ("ln1", "ln4")[l]
            R.at = work_mark
            cell = R.f32(2 * 10).rearrange("p (r n) -> p r n", r=2)
            qt = [R.f32(KD * P).rearrange("p (k n) -> p k n", k=KD) for _ in range(2)]
            sc = [R.f32(NH * C).rearrange("p (h c) -> p h c", h=NH) for _ in range(2)]
            ex = [R.f32(NH * C).rearrange("p (h c) -> p h c", h=NH) for _ in range(2)]
            left = [R.f32(NH * C).rearrange("p (h c) -> p h c", h=NH) for _ in range(2)] if top else None
            m8 = [R.f32(NH * 8 * 4).rearrange("p (r h e) -> p r h e", r=4, h=NH) for _ in range(2)]
            rs = [R.f32(NH) for _ in range(2)]
            wT = [R.f32(NH * P).rearrange("p (h n) -> p h n", h=NH) for _ in range(2)]
            ot = [R.f32(NG * P).rearrange("p (g n) -> p g n", g=NG) for _ in range(2)]
            cx = [R.f32(D) for _ in range(2)]
            ct = [R.f32(KD * P).rearrange("p (k n) -> p k n", k=KD) for _ in range(2)]
            if l == 1:
                z_dram = scratch("z", [B, NH, TB, P, HD])
                z = R.f32(T * D).rearrange("p (t d) -> p t d", t=T)
            GROUPS = ((0, 6, 0, 0), (6, 2, 1, 0), (8, 4, 1, 2 * C), (12, 4, 2, 0))
            OUTS = ((0, 0, 2, 6 * C), (12 * C, 2, 1, 4 * C))
            QB, WB, OB, TB7 = 3, 4, 6, 7
            NLAG = 2 if top else 3

            def late(v):
                return not isinstance(v, int) or v > 0

            def inside(t):
                return not isinstance(t, int) or 0 <= t < T

            def each(body):
                def run(eng):
                    for t in range(-1, 4):
                        body(eng, t, t % 2)
                    with eng.Fori(2, 7) as i:
                        body(eng, i * 2, 0)
                        body(eng, i * 2 + 1, 1)
                    for t in range(14, T + 3):
                        body(eng, t, t % 2)
                return run

            def row_of(buf, t):
                return buf[:, t, :] if isinstance(t, int) else buf[:, bass.ds(t, 1), :].rearrange("p a d -> p (a d)")

            @block.tensor
            def _(pe):
                pe.wait_ge(sem(lns + "_hT"), T)
                pe.wait_ge(sem("kblk"), 4 * B)
                pe.wait_ge(sem("xv"), 2 * B)

                def query(t, r):
                    if late(t - 4) and l == 0:
                        pe.wait_ge(sem(s + "_xd"), t - 4)
                    if late(t):
                        pe.wait_ge(sem(s + "_qt"), t * KD)
                    for half in range(KD):
                        for k in range(KD):
                            mm = pe.matmul(PS[:, QB, half * P:(half + 1) * P], xwqT[l][:, k, half * P:(half + 1) * P],
                                           hT[:, k, t * P:(t + 1) * P], start=(k == 0), stop=(k == KD - 1))
                    mm.then_inc(sem(s + "_q"), 1)

                def scores(t, r, b):
                    pe.wait_ge(sem(s + "_qt"), t * KD + KD)
                    if late(t):
                        pe.wait_ge(sem(s + "_scout"), t * 2)
                    for h0, hn, bank, col in GROUPS:
                        kb = kblk[l][:, b, h0 // 8, h0 % 8:h0 % 8 + hn, :]
                        mm = pe.matmul(PS[:, bank, col:col + hn * C], qt[r][:, h0 // 8, :],
                                       kb.rearrange("p j c -> p (j c)"), start=True, stop=True)
                    mm.then_inc(sem(s + "_s"), 1)

                def turn_weights(t, r, c):
                    if c == 0:
                        pe.wait_ge(sem(s + "_w"), t + 1)
                    if late(t * 4 + c - 1):
                        pe.wait_ge(sem(s + "_wt"), t * 4 + c - 1)
                    for j in range(4):
                        mm = pe.transpose(PS[0:C, WB + c % 2, j * P:(j + 1) * P], ex[r][:, c * 4 + j, :], ident)
                    mm.then_inc(sem(s + "_wtp"), 1)

                def context(t, r, b):
                    pe.wait_ge(sem(s + "_wt"), t * 4 + 4)
                    if late(t):
                        pe.wait_ge(sem(s + "_ot"), t)
                    for g in range(NG):
                        for j in range(G):
                            mm = pe.matmul(PS[SLOT * j:SLOT * (j + 1), OB, g * P:(g + 1) * P], xv[l][0:C, b, g * G + j, :],
                                           wT[r][0:C, g * G + j, :], start=True, stop=True)
                    mm.then_inc(sem(s + "_op"), 1)

                def turn_context(t, r):
                    pe.wait_ge(sem(s + "_ot"), t + 1)
                    if late(t):
                        pe.wait_ge(sem(s + "_n"), t)
                    for g in range(NG):
                        mm = pe.transpose(PS[:, TB7, g * P:(g + 1) * P], ot[r][:, g, :], ident)
                    mm.then_inc(sem(s + "_otp"), 1)

                def output(t, r):
                    pe.wait_ge(sem(s + "_n"), t + 1)
                    if late(t):
                        pe.wait_ge(sem(s + "_xd"), t)
                    if late(min(t + 5, T) * KD):
                        pe.wait_ge(sem(s + "_qt"), min(t + 5, T) * KD)
                    for k in range(KD):
                        mm = pe.transpose(PS[:, QB, k * P:(k + 1) * P], cx[r][:, k * P:(k + 1) * P], ident)
                    mm.then_inc(sem(s + "_ctp"), 1)
                    pe.wait_ge(sem(s + "_ct"), t + 1)
                    for k in range(KD):
                        pe.matmul(PS[:, QB, D:2 * D], ct[r][:, k, :], xwo[:, k, :], start=(k == 0), stop=False)
                    if t == 0:
                        pe.wait_ge(sem(lns + "_xb"), 1)
                    pe.matmul(PS[:, QB, D:2 * D], ident, x[:, t, :], start=False, stop=True).then_inc(sem(s + "_y"), 1)

                for t in range(-1, T + 3):
                    r, o = t % 2, (t + 1) % 2
                    if inside(t + 1):
                        query(t + 1, o)
                    if inside(t - 1):
                        turn_weights(t - 1, o, 0)
                        turn_weights(t - 1, o, 1)
                    if inside(t + 1):
                        scores(t + 1, o, (t + 1) // TB)
                    if inside(t - 1):
                        turn_weights(t - 1, o, 2)
                        turn_weights(t - 1, o, 3)
                        context(t - 1, o, (t - 1) // TB)
                    if inside(t - 2):
                        turn_context(t - 2, r)
                    if inside(t - 3) and l == 0:
                        output(t - 3, o)

            @block.scalar
            def _(act):
                def queries(t, r):
                    act.wait_ge(sem(s + "_q"), t + 1)
                    for half in range(KD):
                        act.activation(qt[r][:, half, :], PS[:, QB, half * P:(half + 1) * P], ACT.Identity,
                                       bias=xq_b[l][:, half:half + 1]).then_inc(sem(s + "_qt"), 1)

                def copy_weights(t, r, c):
                    act.wait_ge(sem(s + "_wtp"), t * 4 + c + 1)
                    if late(t - 1):
                        act.wait_ge(sem(s + "_op"), t - 1)
                    act.copy(wT[r][0:C, c * 4:c * 4 + 4, :], PS[0:C, WB + c % 2, :].rearrange("p (j n) -> p j n", j=4)
                             ).then_inc(sem(s + "_wt"), 1)

                def body(act, t, r):
                    o = 1 - r
                    if top and inside(t - 1):
                        act.wait_ge(sem(s + "_d2"), t)
                        act.activation(left[o], left[o], ACT.Exp, scale=SCALE).then_inc(sem(s + "_e2"), 1)
                    if inside(t + 1):
                        queries(t + 1, o)
                    if inside(t - 1):
                        copy_weights(t - 1, o, 0)
                        copy_weights(t - 1, o, 1)
                    if top and inside(t + 1):
                        act.wait_ge(sem(s + "_s"), t + 2)
                        if late(t):
                            act.wait_ge(sem(s + "_d"), t)
                            act.wait_ge(sem(s + "_k0"), t * NH)
                        for c0, bank, nb, w in OUTS:
                            act.copy(sc[o].rearrange("p h c -> p (h c)")[:, c0:c0 + nb * w].rearrange("p (a n) -> p a n", a=nb),
                                     PS[:, bank:bank + nb, 0:w]).then_inc(sem(s + "_scout"), 1)
                    if inside(t - 1):
                        copy_weights(t - 1, o, 2)
                        copy_weights(t - 1, o, 3)
                    if inside(t):
                        act.wait_ge(sem(s + "_d"), t + 1)
                        act.activation(ex[r], ex[r], ACT.Exp, scale=SCALE if top else 1.0).then_inc(sem(s + "_e"), 1)
                    if inside(t - 1):
                        act.wait_ge(sem(s + "_op"), t)
                        if late(t - 2):
                            act.wait_ge(sem(s + "_otp"), t - 2)
                        act.copy(ot[o], PS[:, OB, :].rearrange("p (g n) -> p g n", g=NG)).then_inc(sem(s + "_ot"), 1)
                    if l == 0 and inside(t - 3):
                        act.wait_ge(sem(s + "_ctp"), t - 2)
                        if late(t - 4):
                            act.wait_ge(sem(s + "_y"), t - 4)
                        act.copy(ct[o], PS[:, QB, 0:D].rearrange("p (k n) -> p k n", k=KD)).then_inc(sem(s + "_ct"), 1)
                        act.wait_ge(sem(s + "_y"), t - 2)
                        act.copy(row_of(x, t - 3), PS[:, QB, D:2 * D]).then_inc(sem(s + "_xd"), 1)
                each(body)(act)

            @block.gpsimd
            def _(pool):
                def less_max(dst, src, r):
                    return pool.tensor_tensor(dst, src, m8[r][:, 0, :, 0:1].to_broadcast([P, NH, C]), ALU.subtract)

                def body(pool, t, r):
                    o = 1 - r
                    if top and inside(t - 1):
                        pool.wait_ge(sem(s + "_topped"), t * NH)
                        less_max(left[o], left[o], o).then_inc(sem(s + "_d2"), 1)
                        pool.wait_ge(sem(s + "_e2"), t)
                        pool.wait_ge(sem(s + "_e"), t)
                        pool.tensor_tensor(ex[o], ex[o], left[o], ALU.subtract).then_inc(sem(s + "_w"), 1)
                    if inside(t):
                        pool.wait_ge(sem(s + "_m"), (t + 1) * (NH if top else 1))
                        if late(t - 1):
                            pool.wait_ge(sem(s + "_wtp"), (t - 1) * 4)
                        less_max(ex[r], sc[r], r).then_inc(sem(s + "_d"), 1)
                        if l == 1:
                            pool.tensor_tensor(row_of(x, t), row_of(x, t), beta, ALU.add).then_inc(sem(s + "_xb"), 1)
                if l == 1:
                    pool.wait_ge(sem("w_in"), W_IN)
                    pool.wait_ge(sem(lns + "_h"), T)
                each(body)(pool)

            @block.vector
            def _(dve):
                if l == 1:
                    dve.wait_ge(sem(lns + "_h"), T)

                def largest(t, r):
                    hn = t * NH
                    dve.wait_ge(sem(s + "_scout"), t * 2 + 2)
                    dve.memset(cell[:, r, 8:9], 0.0)
                    if late(t - 1):
                        dve.wait_ge(sem(s + "_w"), t - 1)
                        dve.memset(cell[:, r, 9:10], 0.0)
                    for k in range(4):
                        if k:
                            dve.wait_ge(sem(f"{s}_k{k - 1}"), hn + NH)
                            dve.memset(cell[:, r, 2 * k:2 * k + 1], 0.0)
                        for hd in range(NH):
                            src = (sc if k == 0 else left)[r][:, hd, :]
                            dve.max(m8[r][:, k, hd, :], src).then_inc(sem(s + "_m" if k == 0 else f"{s}_m{k}"), 1)
                        dve.wait_ge(sem(s + "_m" if k == 0 else f"{s}_m{k}"), hn + NH)
                        dve.memset(cell[:, r, 2 * k + 1:2 * k + 2], 0.0)
                        for hd in range(NH):
                            src = (sc if k == 0 else left)[r][:, hd, :]
                            dve.match_replace(out=left[r][:, hd, :], in_to_replace=m8[r][:, k, hd, :], in_values=src,
                                              imm_value=LOWEST).then_inc(sem(f"{s}_k{k}" if k < 3 else s + "_topped"), 1)

                def maxima(t, r):
                    dve.wait_ge(sem(s + "_s"), t + 1)
                    if late(t - 1):
                        dve.wait_ge(sem(s + "_d"), t - 1)
                    for c0, bank, nb, w in OUTS:
                        dve.tensor_scalar(sc[r].rearrange("p h c -> p (h c)")[:, c0:c0 + nb * w].rearrange("p (a n) -> p a n", a=nb),
                                          PS[:, bank:bank + nb, 0:w], -3.4028234e38, None, ALU.max).then_inc(sem(s + "_scout"), 1)
                    dve.wait_ge(sem(s + "_scout"), t * 2 + 2)
                    dve.tensor_reduce(m8[r][:, 0, :, 0], sc[r], AX.X, ALU.max).then_inc(sem(s + "_m"), 1)

                def normalize(t, r):
                    o = PS[:, TB7, :].rearrange("p (h s) -> p h s", h=NH)
                    dve.wait_ge(sem(s + "_otp"), t + 1)
                    total = o[:, :, HD]
                    if not top:
                        dve.tensor_scalar(rs[r], total, 1e-30, None, ALU.max).then_inc(sem(s + "_sum"), 1)
                        dve.wait_ge(sem(s + "_sum"), t + 1)
                        total = rs[r]
                    dve.reciprocal(rs[r], total).then_inc(sem(s + "_rs"), 1)
                    dve.wait_ge(sem(s + "_rs"), t + 1)
                    if late(t - 1):
                        if l == 0:
                            dve.wait_ge(sem(s + "_ctp"), t - 1)
                        else:
                            dve.wait_ge(sem(f"{s}_zst{r}"), (t - r) * 8)
                    dve.tensor_tensor(cx[r].rearrange("p (h d) -> p h d", h=NH), o[:, :, 0:HD],
                                      rs[r].unsqueeze(2).to_broadcast([P, NH, HD]), ALU.mult).then_inc(sem(s + "_n"), 1)

                def body(dve, t, r):
                    o = 1 - r
                    if inside(t):
                        if top:
                            largest(t, r)
                        else:
                            maxima(t, r)
                    if inside(t - NLAG):
                        normalize(t - NLAG, r if NLAG == 2 else o)
                    if not top and inside(t):
                        dve.wait_ge(sem(s + "_e"), t + 1)
                        dve.tensor_scalar(ex[r], ex[r], 0.0, None, ALU.max).then_inc(sem(s + "_w"), 1)
                    if l == 1 and isinstance(t, int) and 14 <= t < 14 + TB // 2:
                        dve.wait_ge(sem(s + "_z0"), 16)
                        add_context(2 * (t - 14))
                        add_context(2 * (t - 14) + 1)

                def add_context(t):
                    dve.tensor_tensor(h[:, t, :], h[:, t, :], z[:, t, :], ALU.add).then_inc(sem(s + "_hz"), 1)
                    dve.wait_ge(sem(s + "_hz"), t + 1)
                    dve.bn_stats(stats[:, t, :], h[:, t, :]).then_inc(sem(s + "_st2"), 1)

                def norm_rows(b):
                    bt = slice(b * TB, (b + 1) * TB)
                    for t in range(b * TB, (b + 1) * TB):
                        dve.wait_ge(sem(s + "_st2"), t + 1)
                        dve.bn_aggr(mv[:, t, :], stats[:, t, :]).then_inc(sem(s + "_mv2"), 1)
                    dve.wait_ge(sem(s + "_mv2"), (b + 1) * TB)
                    dve.tensor_scalar(std[:, bt], mv[:, bt, 1], LN_EPS, None, ALU.add).then_inc(sem(s + "_var2"), 1)
                    dve.wait_ge(sem(s + "_std2"), b + 1)
                    dve.reciprocal(rstd[:, bt], std[:, bt]).then_inc(sem(s + "_rstd2"), 1)
                    dve.wait_ge(sem(s + "_rstd2"), b + 1)
                    for t in range(b * TB, (b + 1) * TB):
                        dve.tensor_scalar(h[:, t, :], h[:, t, :], mv[:, t, 0:1], rstd[:, t:t + 1], ALU.subtract,
                                          ALU.mult).then_inc(sem(s + "_n2"), 1)

                def add_rows(b):
                    dve.wait_ge(sem(s + "_xb"), T)
                    for t in range(b * TB, (b + 1) * TB):
                        dve.wait_ge(sem(s + "_g2"), t + 1)
                        dve.tensor_tensor(x[:, t, :], x[:, t, :], h[:, t, :], ALU.add).then_inc(sem(s + "_x2"), 1)
                        if t % TB:
                            row_stats(dve, "ln5", t - 1, s + "_x2")
                    row_stats(dve, "ln5", (b + 1) * TB - 1, s + "_x2")

                each(body)(dve)
                if l == 1:
                    norm_rows(0)
                    add_rows(0)
                    dve.wait_ge(sem(s + "_z1"), 16)
                    for t in range(TB, T):
                        add_context(t)
                    norm_rows(1)
                    add_rows(1)

            if l == 1:
                @block.sync
                def _(sp):
                    def store(t, r):
                        sp.wait_ge(sem(s + "_n"), t + 1)
                        sp.dma_start(z_dram[b].rearrange("h t p d -> t p h d")[t - b * TB],
                                     cx[r].rearrange("p (h d) -> p h d", h=NH)).then_inc(sem(f"{s}_zst{r}"), 16)

                    for b in range(B):
                        with sp.Fori(b * TB // 2, (b + 1) * TB // 2) as i:
                            store(i * 2, 0)
                            store(i * 2 + 1, 1)
                        for r in range(2):
                            sp.wait_ge(sem(f"{s}_zst{r}"), 16 * (b + 1) * TB // 2)
                        sp.dma_start(z[:, b * TB:(b + 1) * TB, :],
                                     z_dram[b].rearrange("h t p d -> (h t p d)").rearrange("(t p d) -> p t d", t=TB, p=P)
                                     ).then_inc(sem(f"{s}_z{b}"), 16)

                @block.scalar
                def _(act):
                    for b in range(B):
                        bt = slice(b * TB, (b + 1) * TB)
                        act.wait_ge(sem(s + "_var2"), b + 1)
                        act.activation(std[:, bt], std[:, bt], ACT.Sqrt).then_inc(sem(s + "_std2"), 1)

                @block.gpsimd
                def _(pool):
                    for t in range(T):
                        pool.wait_ge(sem(s + "_n2"), t + 1)
                        pool.tensor_tensor(h[:, t, :], h[:, t, :], gamma, ALU.mult).then_inc(sem(s + "_g2"), 1)

        def moe(block, l, free_sem, free_val):
            s, lns = f"e{l}", ("ln2", "ln5")[l]
            big = l == 1
            R.at = base_mark if big else work_mark
            lg = R.f32(T * E).rearrange("p (t e) -> p t e", t=T)
            oh = R.f32(T * E).rearrange("p (t e) -> p t e", t=T)
            ohb = R.bf16(T * E).rearrange("p (t e) -> p t e", t=T)
            ta = R.f32(T * E).rearrange("p (t e) -> p t e", t=T)
            tb = R.f32(T * E).rearrange("p (t e) -> p t e", t=T)
            tot = R.f32(T * E).rearrange("p (t e) -> p t e", t=T)
            c1, c2, c3 = R.f32(E), R.f32(E), R.f32(E)
            nt = R.f32(E)
            cmp1 = R.f32(24 * T).rearrange("p (e j) -> p e j", e=24)
            m1, gate, posf = R.f32(T), R.f32(T), R.f32(T)
            posi = R.f32(T).bitcast(I32)
            eidf = R.f32(24)
            eid = R.f32(24).bitcast(I32)
            NB1 = E * F if big else E * D
            bias_raw = R.f32(NB1 // P)
            bias_part = [R.bf16(NB1 // P) for _ in range(NPART)]
            bias2_raw = R.f32(E * D // P)
            bias2_part = [R.bf16(E * D // P) for _ in range(NPART)]
            b1 = hT.rearrange("p k n -> p (k n)").bitcast(BF16)[0:NPART, 0:NB1]
            b2 = R.bf16(E * D)[0:NPART]
            yb = [R.f32(D) for _ in range(NTB)]
            NY = 4
            yg = [R.f32(D) for _ in range(NY)]
            H = Region(h.rearrange("p t d -> p (t d)"), T * D)
            xs = [H.f32(D) for _ in range(NTB)]
            xsT = [H.f32(KD * P).rearrange("p (k n) -> p k n", k=KD) for _ in range(NTB)]
            if big:
                h1 = H.f32(F)
                h1T = H.f32(F).rearrange("p (k n) -> p k n", k=KF)
                W1 = R.f32(E * KD * F)
                W2 = R.f32(E * KF * D)
            else:
                raw = R.f32(E * KD * D).rearrange("p (e k n) -> p e k n", e=E, k=KD)
                WeT = R.f32(E * KD * D)
            bias_names = (("L1_ffn_b1", bias_raw, bias_part, b1, NB1), ("L1_ffn_b2", bias2_raw, bias2_part, b2, E * D)) \
                if big else (("L0_ffn_expert_b", bias_raw, bias_part, b1, NB1),)
            bias_rows = [scratch(f"bias{l}{i}", [NPART, n], BF16) for i, (_, _, _, _, n) in enumerate(bias_names)]

            EARLY = 5

            def load_expert(sp, e):
                sp.dma_start(W1[:, e * KD * F:(e + 1) * KD * F].rearrange("p (k f) -> p k f", k=KD),
                             a["L1_ffn_W1"][e].rearrange("(k p) f -> p k f", p=P)).then_inc(sem(f"{s}_w{e}"), 16)
                sp.dma_start(W2[:, e * KF * D:(e + 1) * KF * D].rearrange("p (k f) -> p k f", k=KF),
                             a["L1_ffn_W2"][e].rearrange("(k p) f -> p k f", p=P)).then_inc(sem(f"{s}_w{e}"), 16)

            @block.sync
            def _(sp):
                sp.wait_ge(sem(free_sem), free_val)

                def load(dst, src):
                    sp.dma_start(dst, src).then_inc(sem(s + "_win"), 16)
                for name, raw_b, _, _, n in bias_names:
                    load(raw_b, a[name].rearrange("(o e) f -> o (e f)", o=1).rearrange("o (p n) -> p (o n)", p=P))

                if big:
                    for e in range(EARLY):
                        load_expert(sp, e)
                else:
                    for e in range(E):
                        load(raw[:, e], a["L0_ffn_expert_w"][e].rearrange("(k p) n -> p k n", p=P))
                sp.wait_ge(sem(s + "_bparts"), len(bias_names) * NPART)
                for (_, _, parts, _, n), rows in zip(bias_names, bias_rows):
                    for i in range(NPART):
                        sp.dma_start(rows[i].rearrange("(p n) -> p n", p=P), parts[i]).then_inc(sem(s + "_bst"), 16)
                sp.wait_ge(sem(s + "_bst"), 16 * NPART * len(bias_names))
                sp.wait_ge(sem(lns + "_lt"), T // 4)
                for (_, _, _, dst, n), rows in zip(bias_names, bias_rows):
                    sp.dma_start(dst, rows).then_inc(sem(s + "_brow"), 16)
            WIN = 16 * (2 if big else 1 + E)

            @block.tensor
            def _(pe):
                pe.wait_ge(sem(s + "_win"), WIN)
                pe.wait_ge(sem(s + "_oh"), 1)
                oh2 = ohb.rearrange("p t e -> p (t e)")
                pe.matmul(PS[:, 6, 0:T * E], upper, oh2, start=True, stop=True)
                pe.matmul(PS[:, 7, 0:T * E], onesb, oh2, start=True, stop=True).then_inc(sem(s + "_rank"), 1)
                if not big:
                    for e in range(E):
                        if e >= 2:
                            pe.wait_ge(sem(s + "_weT"), e - 1)
                        for ko in range(KD):
                            for ki in range(KD):
                                mm = pe.transpose(PS[:, 4 + e % 2, (ki * KD + ko) * P:(ki * KD + ko + 1) * P],
                                                  raw[:, e, ko, ki * P:(ki + 1) * P], ident)
                        mm.then_inc(sem(s + "_wep"), 1)

            @block.scalar
            def _(act):
                act.wait_ge(sem(s + "_ld"), 1)
                act.activation(tb, ta, ACT.Exp).then_inc(sem(s + "_le"), 1)

            if not big:
                @block.scalar
                def _(act):
                    for e in range(E):
                        act.wait_ge(sem(s + "_wep"), e + 1)
                        act.copy(WeT[:, e * KD * D:(e + 1) * KD * D], PS[:, 4 + e % 2, :]).then_inc(sem(s + "_weT"), 1)

            @block.vector
            def _(dve):
                n = [0, 0]

                def link(ins):
                    n[0] += 1
                    ins.then_inc(sem(s + "_chain"), 1)
                    dve.wait_ge(sem(s + "_chain"), n[0])

                dve.wait_ge(sem(s + "_win"), WIN)
                for _, raw_b, parts, _, _ in bias_names:
                    for i in range(NPART):
                        ins = dve.tensor_copy(parts[i], raw_b)
                        ins.then_inc(sem(s + "_bparts"), 1)
                        n[1] += 1
                        if i < NPART - 1:
                            dve.wait_ge(sem(s + "_bparts"), n[1])
                            link(dve.tensor_tensor(raw_b, raw_b, parts[i], ALU.subtract))
                dve.wait_ge(sem(lns + "_lt"), T // 4)
                te = [P, T, E]
                link(dve.tensor_tensor(lg, PS[:, 3, 0:T * E].rearrange("p (t e) -> p t e", t=T),
                                       br[l].unsqueeze(1).to_broadcast(te), ALU.add))
                link(dve.tensor_reduce(m1, lg, AX.X, ALU.max))
                m1b = m1.unsqueeze(2).to_broadcast(te)
                dve.tensor_tensor(ta, lg, m1b, ALU.subtract).then_inc(sem(s + "_ld"), 1)
                link(dve.tensor_tensor(oh, lg, m1b, ALU.is_equal))
                link(dve.tensor_tensor(lg, oh, order.unsqueeze(1).to_broadcast(te), ALU.mult))
                link(dve.tensor_reduce(posf, lg, AX.X, ALU.max))
                link(dve.tensor_tensor(oh, lg, posf.unsqueeze(2).to_broadcast(te), ALU.is_equal))
                dve.tensor_copy(ohb, oh).then_inc(sem(s + "_oh"), 1)
                dve.wait_ge(sem(s + "_le"), 1)
                link(dve.tensor_reduce(m1, tb, AX.X, ALU.add))
                link(dve.reciprocal(gate, m1))
                dve.wait_ge(sem(s + "_rank"), 1)
                link(dve.tensor_copy(tot, PS[:, 7, 0:T * E].rearrange("p (t e) -> p t e", t=T)))
                cur, nxt = tot, ta
                d = 1
                while d < T:
                    dve.tensor_copy(nxt[:, 0:d, :], cur[:, 0:d, :]).then_inc(sem(s + "_chain"), 1)
                    n[0] += 1
                    link(dve.tensor_tensor(nxt[:, d:T, :], cur[:, d:T, :], cur[:, 0:T - d, :], ALU.add))
                    cur, nxt = nxt, (tb if nxt is ta else ta)
                    d *= 2
                total = cur[:, T - 1, :]
                link(dve.tensor_scalar(c1, total, 1.0 / P, None, ALU.mult))
                link(dve.tensor_tensor(cmp1[:, 0:E, :], c1.unsqueeze(2).to_broadcast([P, E, T]),
                                       count[:, 0:T].unsqueeze(1).to_broadcast([P, E, T]), ALU.is_gt))
                link(dve.tensor_reduce(nt, cmp1[:, 0:E, :], AX.X, ALU.add))
                a0, a1 = nt, c2
                d = 1
                while d < E:
                    dve.tensor_copy(a1[:, 0:d], a0[:, 0:d]).then_inc(sem(s + "_chain"), 1)
                    n[0] += 1
                    link(dve.tensor_tensor(a1[:, d:E], a0[:, d:E], a0[:, 0:E - d], ALU.add))
                    a0, a1 = a1, (c3 if a1 is c2 else c2)
                    d *= 2
                ends = a0
                link(dve.tensor_tensor(c1, ends, nt, ALU.subtract))
                link(dve.tensor_scalar(c1, c1, float(P), None, ALU.mult))
                link(dve.tensor_tensor(lg, cur, tot, ALU.subtract))
                link(dve.tensor_tensor(lg, lg, c1.unsqueeze(1).to_broadcast(te), ALU.add))
                link(dve.tensor_tensor(lg, lg, PS[:, 6, 0:T * E].rearrange("p (t e) -> p t e", t=T), ALU.add))
                link(dve.tensor_tensor(lg, lg, oh, ALU.mult))
                link(dve.tensor_reduce(posf, lg, AX.X, ALU.add))
                dve.tensor_copy(posi, posf).then_inc(sem(s + "_pos"), 1)
                ee = cmp1.rearrange("p e j -> p (e j)")[:, 0:24 * E].rearrange("p (s e) -> p s e", s=24)
                link(dve.tensor_tensor(ee, ends.unsqueeze(1).to_broadcast([P, 24, E]),
                                       count[:, 0:24].unsqueeze(2).to_broadcast([P, 24, E]), ALU.is_le))
                link(dve.tensor_reduce(eidf, ee, AX.X, ALU.add))
                link(dve.tensor_scalar(eidf, eidf, float(E - 1), None, ALU.min))
                dve.tensor_copy(eid, eidf).then_inc(sem(s + "_eid"), 1)

            @block.gpsimd
            def _(pool):
                pool.wait_ge(sem(s + "_pos"), 1)
                pool.wait_ge(sem("xs_clear"), XS_CLEAR)
                pool.wait_ge(sem(lns + "_h"), T)
                for t in range(T):
                    pool.indirect_dma_start(
                        out=xs_dram[l], out_offset=bass.IndirectOffsetOnAxis(ap=posi[:, t:t + 1], axis=0),
                        in_=h[:, t, :], in_offset=None).then_inc(sem(s + "_sc"), 16)
                if big:
                    for e in range(E):
                        pool.wait_ge(sem(f"{s}_w{e}"), 2 * 16)
                        pool.nop().then_inc(sem(s + "_experts"), 1)
                for r in range(NTB):
                    pool.wait_ge(sem(f"{s}_yst{r}"), 16 * len(range(r, NS, NTB)))
                for t in range(T):
                    if t >= NY:
                        pool.wait_ge(sem(s + "_x"), t - NY + 1)
                    pool.indirect_dma_start(
                        out=yg[t % NY], out_offset=None, in_=ys_dram[l],
                        in_offset=bass.IndirectOffsetOnAxis(ap=posi[:, t:t + 1], axis=0)).then_inc(sem(f"{s}_yg{t % NY}"), 16)

            TBANK = (0, 1, 0, 1) if big else (0, 1, 2, 3)
            YBANK = (6, 7, 6, 7) if big else (4, 5, 6, 7)
            BANKS = len(set(TBANK))

            def late(v):
                return not isinstance(v, int) or v > 0

            def inside(t):
                return not isinstance(t, int) or 0 <= t < NS

            def each(eng, body):
                for t in range(-2, NTB):
                    body(t, t % NTB)
                with eng.Fori(1, NS // NTB) as i:
                    for r in range(NTB):
                        body(i * NTB + r, r)
                for t in range(NS // NTB * NTB, NS):
                    body(t, t % NTB)

            def tile_rows(ap, t):
                return ap.rearrange("(s p) d -> s p d", p=P)[t]

            def expert(t):
                return eid[0:1, t:t + 1] if isinstance(t, int) else eid[0:1, bass.ds(t, 1)]

            @block.sync
            def _(sp):
                sp.wait_ge(sem(s + "_sc"), 16 * T)

                def load(t, r):
                    if late(t - NTB + 1):
                        sp.wait_ge(sem(s + "_tp"), t - NTB + 1)
                    sp.dma_start(xs[r], tile_rows(xs_dram[l], t)).then_inc(sem(f"{s}_xs{r}"), 16)

                def store(t, r):
                    if big:
                        sp.wait_ge(sem(s + "_yb"), t + 1)
                        sp.dma_start(tile_rows(ys_dram[l], t), yb[r]).then_inc(sem(f"{s}_yst{r}"), 16)

                AHEAD = NTB + 1
                for t in range(AHEAD):
                    load(t, t % NTB)
                    if big and t == NTB - 1:
                        for e in range(EARLY, E):
                            load_expert(sp, e)
                for t in range(NTB):
                    load(t + AHEAD, (t + AHEAD) % NTB)
                    store(t, t)
                with sp.Fori(1, (NS - AHEAD) // NTB) as i:
                    for r in range(NTB):
                        load(i * NTB + r + AHEAD, (r + AHEAD) % NTB)
                        store(i * NTB + r, r)
                for t in range((NS - AHEAD) // NTB * NTB, NS):
                    if t + AHEAD < NS:
                        load(t + AHEAD, (t + AHEAD) % NTB)
                    store(t, t % NTB)

            @block.tensor
            def _(pe):
                pe.wait_ge(sem(s + "_eid"), 1)
                pe.wait_ge(sem(s + "_brow"), 16 * len(bias_names))
                if not big:
                    pe.wait_ge(sem(s + "_weT"), E)

                def turn(t, r):
                    pe.wait_ge(sem(f"{s}_xs{r}"), (t - r) * (16 // NTB) + 16)
                    if late(t - BANKS + 1):
                        pe.wait_ge(sem(s + "_xT"), t - BANKS + 1)
                    for k in range(KD):
                        mm = pe.transpose(PS[:, TBANK[r], k * P:(k + 1) * P], xs[r][:, k * P:(k + 1) * P], ident)
                    mm.then_inc(sem(s + "_tp"), 1)

                def hidden(t, r):
                    e = pe.value_load(expert(t), min_val=0, max_val=E - 1)
                    pe.wait_ge(sem(s + "_experts"), e + 1)
                    pe.wait_ge(sem(s + "_xT"), t + 1)
                    if late(t):
                        pe.wait_ge(sem(s + "_h1"), t)
                    for k in range(KD):
                        for half in range(2):
                            pe.matmul(PS[:, 2 + half, :], xsT[r][:, k, :],
                                      W1[:, bass.ds(e * (KD * F) + k * F + half * BANK, BANK)], start=(k == 0), stop=False)
                    for half in range(2):
                        mm = pe.matmul(PS[:, 2 + half, :], onesb[0:NPART, :], b1[:, bass.ds(e * F + half * BANK, BANK)],
                                       start=False, stop=True)
                    mm.then_inc(sem(s + "_h1p"), 1)

                def turn_hidden(t):
                    pe.wait_ge(sem(s + "_h1"), t + 1)
                    if late(t):
                        pe.wait_ge(sem(s + "_h1T"), t)
                    for k in range(KF):
                        mm = pe.transpose(PS[:, 4 + k // 4, (k % 4) * P:(k % 4 + 1) * P], h1[:, k * P:(k + 1) * P], ident)
                    mm.then_inc(sem(s + "_h1tp"), 1)

                def output(t, r):
                    e = pe.value_load(expert(t), min_val=0, max_val=E - 1)
                    if big:
                        pe.wait_ge(sem(s + "_h1T"), t + 1)
                        lhs, W, nk, b = h1T, W2, KF, b2
                    else:
                        pe.wait_ge(sem(s + "_xT"), t + 1)
                        lhs, W, nk, b = xsT[r], WeT, KD, b1
                    if late(t - BANKS + 1):
                        pe.wait_ge(sem(s + "_yb"), t - BANKS + 1)
                    ps = PS[:, YBANK[r], 0:D]
                    for k in range(nk):
                        pe.matmul(ps, lhs[:, k, :], W[:, bass.ds(e * (nk * D) + k * D, D)], start=(k == 0), stop=False)
                    pe.matmul(ps, onesb[0:NPART, :], b[:, bass.ds(e * D, D)], start=False, stop=True).then_inc(sem(s + "_y"), 1)

                def step(t, r):
                    if big and inside(t):
                        turn_hidden(t)
                    if inside(t + 2):
                        turn(t + 2, (r + 2) % NTB)
                    if big and inside(t + 1):
                        hidden(t + 1, (r + 1) % NTB)
                    if inside(t):
                        output(t, r)
                each(pe, step)

            @block.scalar
            def _(act):
                def step(t, r):
                    if inside(t + 2):
                        o = (r + 2) % NTB
                        act.wait_ge(sem(s + "_tp"), t + 3)
                        if late(t + 3 - NTB):
                            act.wait_ge(sem(s + ("_h1p" if big else "_y")), t + 3 - NTB)
                        act.copy(xsT[o], PS[:, TBANK[o], 0:KD * P].rearrange("p (k n) -> p k n", k=KD)).then_inc(sem(s + "_xT"), 1)
                    if big and inside(t + 1):
                        act.wait_ge(sem(s + "_h1p"), t + 2)
                        if late(t + 1):
                            act.wait_ge(sem(s + "_h1tp"), t + 1)
                        act.activation(h1.rearrange("p (a n) -> p a n", a=2), PS[:, 2:4, :], ACT.Relu).then_inc(sem(s + "_h1"), 1)
                    if big and inside(t):
                        act.wait_ge(sem(s + "_y"), t + 1)
                        if late(t - NTB + 1):
                            act.wait_ge(sem(f"{s}_yst{r}"), (t - r) * (16 // NTB))
                        act.copy(yb[r], PS[:, YBANK[r], 0:D]).then_inc(sem(s + "_yb"), 1)
                    if not big and inside(t):
                        act.wait_ge(sem(s + "_yb"), t + 1)
                        act.dma_start(tile_rows(ys_dram[l], t), yb[r]).then_inc(sem(f"{s}_yst{r}"), 16)
                each(act, step)

            @block.vector
            def _(dve):
                def step(t, r):
                    if big and inside(t):
                        dve.wait_ge(sem(s + "_h1tp"), t + 1)
                        if late(t):
                            dve.wait_ge(sem(s + "_y"), t)
                        dve.tensor_copy(h1T.rearrange("p (a k) n -> p a (k n)", a=2), PS[:, 4:6, :]).then_inc(sem(s + "_h1T"), 1)
                    if not big and inside(t):
                        dve.wait_ge(sem(s + "_y"), t + 1)
                        if late(t - NTB + 1):
                            dve.wait_ge(sem(f"{s}_yst{r}"), (t - r) * (16 // NTB))
                        dve.tensor_copy(yb[r], PS[:, YBANK[r], 0:D]).then_inc(sem(s + "_yb"), 1)
                each(dve, step)
                for t in range(T):
                    dve.wait_ge(sem(f"{s}_yg{t % NY}"), 16 * (t // NY + 1))
                    dve.scalar_tensor_tensor(out=x[:, t, :], in0=yg[t % NY], scalar=gate[:, t:t + 1], in1=x[:, t, :],
                                             op0=ALU.mult, op1=ALU.add).then_inc(sem(s + "_x"), 1)
                    if l == 0 and t:
                        row_stats(dve, "ln3", t - 1, s + "_x")
                if l == 0:
                    row_stats(dve, "ln3", T - 1, s + "_x")

        with nc.Block() as block:
            prepare(block)
            ln(block, "ln0", "x_in", 16 * 4, banks=(6, 7))
            centre(block)
            add_bias(block, "ln0", b_out[0], "w_in", W_IN)
            turn_cross = prepare_cross(block)
            qkv0(block)
            turn_cross()
            attention(block, 0, causal=False)
            project(block, 0)
            ln(block, "ln1", "p0_x", T, stats_due=False)
            add_bias(block, "ln1", xb_out, "w_in", W_IN)
            cross(block, 0, top=True)
            ln(block, "ln2", "x0_xd", T, router=0)
            moe(block, 0, "x0_xd", T)

        nc.clear_and_free_semaphores([sems.pop(n) for n in list(sems) if n not in KEPT])
        nc.all_engine_barrier()

        with nc.Block() as block:
            ln(block, "ln3", "e0_x", T, stats_due=False)
            qkv1(block)
            add_bias(block, "ln3", b_out[1], "w_in", W_IN)
            attention(block, 1, causal=True)
            project(block, 1)
            ln(block, "ln4", "p1_x", T, stats_due=False)
            cross(block, 1, top=False)
            ln(block, "ln5", "x1_x2", T, stats_due=False, router=1)
            moe(block, 1, "x1_x2", T)

            @block.sync
            def _(sp):
                for t in range(T):
                    sp.wait_ge(sem("e1_x"), t + 1)
                    sp.dma_start(out[t // TB, (t % TB) * P:(t % TB + 1) * P, :], x[:, t, :]).then_inc(sem("out"), 16)
                sp.wait_ge(sem("out"), 16 * T)


def kernel(**inputs):
    import numpy as _np
    import concourse.bacc as _bacc
    from concourse import mybir as _mybir
    from concourse.bass_utils import run_bass_kernel_spmd as _run

    nc = _bacc.Bacc("TRN2", target_bir_lowering=False, num_devices=1)
    arrays, aps = {}, {}
    for name, value in inputs.items():
        v = _np.ascontiguousarray(value)
        arrays[f"in_{name}"] = v
        aps[name] = nc.dram_tensor(f"in_{name}", v.shape, _mybir.dt.from_np(v.dtype), kind="ExternalInput").ap()
    out = nc.dram_tensor("decoded", (B, S, D), F32, kind="ExternalOutput").ap()
    build(nc, aps, out)
    r = _run(nc, [arrays], core_ids=[0])
    return r.results[0]["decoded"]
```
